# Optimizing a Trainium2 kernel written in Bass

```python
import numpy as np
import jax
import jax.numpy as jnp

def _softmax(x, axis=-1):
    return jax.nn.softmax(x, axis=axis)

def _gelu(x):
    return jax.nn.gelu(x, approximate=True)

def _silu(x):
    return jax.nn.silu(x)

def _sigmoid(x):
    return jax.nn.sigmoid(x)

def _layernorm(x, axis=-1, eps=1e-05):
    m = jnp.mean(x, axis=axis, keepdims=True)
    v = jnp.var(x, axis=axis, keepdims=True)
    return (x - m) / jnp.sqrt(v + eps)

def _scatter_add(tgt, idx, src, axis=0):
    return tgt.at[idx].add(src)

def _segment_sum(src, seg, n):
    return jax.ops.segment_sum(src, seg, n)
kernel_name = 'mk_seq_postln_d2_jaxref_r8_4e1522'

def setup_inputs(seed: int=0):
    np.random.seed(seed)
    _w = jnp.asarray

    def _L0_attn_setup():
        import jax, jax.numpy as jnp
        import numpy as np
        D_MODEL = 128
        NUM_HEADS = 16
        D_HEAD = D_MODEL // NUM_HEADS
        key = jax.random.key(seed)
        ks = jax.random.split(key, 5)
        B, T = (4, 256)
        x = jax.random.normal(ks[0], (B, T, D_MODEL), dtype=jnp.float32)
        s = 1.0 / np.sqrt(D_MODEL)
        W_qkv = jax.random.uniform(ks[1], (3 * D_MODEL, D_MODEL), jnp.float32, -s, s)
        b_qkv = jax.random.uniform(ks[2], (3 * D_MODEL,), jnp.float32, -s, s)
        W_out = jax.random.uniform(ks[3], (D_MODEL, D_MODEL), jnp.float32, -s, s)
        b_out = jax.random.uniform(ks[4], (D_MODEL,), jnp.float32, -s, s)
        return {'x': x, 'W_qkv': W_qkv, 'b_qkv': b_qkv, 'W_out': W_out, 'b_out': b_out}
    _L0_attn_in = _L0_attn_setup()

    def _L0_ffn_setup():
        import jax, jax.numpy as jnp
        import numpy as np
        D = 128
        E = 8
        H = 256
        TOP_K = 2
        ALPHA = 0.5
        LN_EPS = 1e-05

        def _experts_all(x, W1, b1, W2, b2):
            h = jax.nn.relu(jnp.einsum('bld,edh->eblh', x, W1) + b1[:, None, None, :])
            return jnp.einsum('eblh,ehd->ebld', h, W2) + b2[:, None, None, :]

        def _selected_expert(x, expert_idx, W1, b1, W2, b2):
            oh = jax.nn.one_hot(expert_idx, E, dtype=x.dtype)
            return jnp.einsum('ebld,ble->bld', _experts_all(x, W1, b1, W2, b2), oh)

        def _layer_norm(x, gamma, beta):
            mu = jnp.mean(x, axis=-1, keepdims=True)
            var = jnp.mean(jnp.square(x - mu), axis=-1, keepdims=True)
            return (x - mu) * jax.lax.rsqrt(var + LN_EPS) * gamma + beta
        key = jax.random.key(seed)
        ks = jax.random.split(key, 8)
        x = jax.random.normal(ks[0], (2, 256, D), dtype=jnp.float32)
        gate_W = jax.random.normal(ks[1], (D, E), dtype=jnp.float32) * 0.02
        gate_b = jnp.zeros((E,), dtype=jnp.float32)
        W1 = jax.random.normal(ks[2], (E, D, H), dtype=jnp.float32) * 0.02
        b1 = jnp.zeros((E, H), dtype=jnp.float32)
        W2 = jax.random.normal(ks[3], (E, H, D), dtype=jnp.float32) * 0.02
        b2 = jnp.zeros((E, D), dtype=jnp.float32)
        ln_gamma = jnp.ones((D,), dtype=jnp.float32)
        ln_beta = jnp.zeros((D,), dtype=jnp.float32)
        return {'x': x, 'gate_W': gate_W, 'gate_b': gate_b, 'W1': W1, 'b1': b1, 'W2': W2, 'b2': b2, 'ln_gamma': ln_gamma, 'ln_beta': ln_beta}
    _L0_ffn_in = _L0_ffn_setup()

    def _L1_attn_setup():
        import jax, jax.numpy as jnp
        import numpy as np
        DIM = 128
        HEADS = 16
        HEAD_DIM = DIM // HEADS

        def feature_map(x):
            return jnp.where(x > 0, x + 1.0, jnp.exp(x))
        key = jax.random.key(seed)
        ks = jax.random.split(key, 11)
        B, N, D = (4, 1024, DIM)
        s = 1.0 / np.sqrt(D)
        inp = {'x': jax.random.normal(ks[0], (B, N, D), dtype=jnp.float32), 'wg_w': jax.random.normal(ks[1], (D, D), dtype=jnp.float32) * s, 'wg_b': jnp.zeros((D,), dtype=jnp.float32), 'wq_w': jax.random.normal(ks[2], (D, D), dtype=jnp.float32) * s, 'wq_b': jnp.zeros((D,), dtype=jnp.float32), 'wk_w': jax.random.normal(ks[3], (D, D), dtype=jnp.float32) * s, 'wk_b': jnp.zeros((D,), dtype=jnp.float32), 'wv_w': jax.random.normal(ks[4], (D, D), dtype=jnp.float32) * s, 'wv_b': jnp.zeros((D,), dtype=jnp.float32), 'out_w': jax.random.normal(ks[5], (D, D), dtype=jnp.float32) * s, 'out_b': jnp.zeros((D,), dtype=jnp.float32)}
        return inp
    _L1_attn_in = _L1_attn_setup()

    def _L1_ffn_setup():
        import jax, jax.numpy as jnp
        import numpy as np
        E, K, D = (8, 2, 128)
        B, S = (2, 512)

        def _layernorm(x, g, b, eps=1e-06):
            m = jnp.mean(x, axis=-1, keepdims=True)
            v = jnp.var(x, axis=-1, keepdims=True)
            return (x - m) * jax.lax.rsqrt(v + eps) * g + b
        key = jax.random.key(seed)
        ks = jax.random.split(key, 6)
        n = lambda k, shape, scale: jax.random.normal(k, shape, jnp.float32) * scale
        return {'x': n(ks[0], (B, S, D), 1.0), 'gate_w': n(ks[1], (D, E), 0.02), 'w1': n(ks[2], (E, D, 2 * D), 0.02), 'b1': jnp.zeros((E, 2 * D), jnp.float32), 'w2': n(ks[3], (E, 2 * D, D), 0.02), 'b2': jnp.zeros((E, D), jnp.float32), 'ln_g': jnp.ones((E, D), jnp.float32), 'ln_b': jnp.zeros((E, D), jnp.float32)}
    _L1_ffn_in = _L1_ffn_setup()
    _d = {'L0_attn_x': _L0_attn_in['x'], 'L0_attn_W_qkv': _L0_attn_in['W_qkv'], 'L0_attn_b_qkv': _L0_attn_in['b_qkv'], 'L0_attn_W_out': _L0_attn_in['W_out'], 'L0_attn_b_out': _L0_attn_in['b_out'], 'L0_ffn_gate_W': _L0_ffn_in['gate_W'], 'L0_ffn_gate_b': _L0_ffn_in['gate_b'], 'L0_ffn_W1': _L0_ffn_in['W1'], 'L0_ffn_b1': _L0_ffn_in['b1'], 'L0_ffn_W2': _L0_ffn_in['W2'], 'L0_ffn_b2': _L0_ffn_in['b2'], 'L0_ffn_ln_gamma': _L0_ffn_in['ln_gamma'], 'L0_ffn_ln_beta': _L0_ffn_in['ln_beta'], 'L1_attn_wg_w': _L1_attn_in['wg_w'], 'L1_attn_wg_b': _L1_attn_in['wg_b'], 'L1_attn_wq_w': _L1_attn_in['wq_w'], 'L1_attn_wq_b': _L1_attn_in['wq_b'], 'L1_attn_wk_w': _L1_attn_in['wk_w'], 'L1_attn_wk_b': _L1_attn_in['wk_b'], 'L1_attn_wv_w': _L1_attn_in['wv_w'], 'L1_attn_wv_b': _L1_attn_in['wv_b'], 'L1_attn_out_w': _L1_attn_in['out_w'], 'L1_attn_out_b': _L1_attn_in['out_b'], 'L1_ffn_gate_w': _L1_ffn_in['gate_w'], 'L1_ffn_w1': _L1_ffn_in['w1'], 'L1_ffn_b1': _L1_ffn_in['b1'], 'L1_ffn_w2': _L1_ffn_in['w2'], 'L1_ffn_b2': _L1_ffn_in['b2'], 'L1_ffn_ln_g': _L1_ffn_in['ln_g'], 'L1_ffn_ln_b': _L1_ffn_in['ln_b']}
    _x0 = _d['L0_attn_x']
    _d['L0_attn_x'] = jax.random.normal(jax.random.fold_in(jax.random.key(seed), 1), (8, 256, 128), dtype=_x0.dtype)
    del _x0
    return _d

def reference(L0_attn_x, L0_attn_W_qkv, L0_attn_b_qkv, L0_attn_W_out, L0_attn_b_out, L0_ffn_gate_W, L0_ffn_gate_b, L0_ffn_W1, L0_ffn_b1, L0_ffn_W2, L0_ffn_b2, L0_ffn_ln_gamma, L0_ffn_ln_beta, L1_attn_wg_w, L1_attn_wg_b, L1_attn_wq_w, L1_attn_wq_b, L1_attn_wk_w, L1_attn_wk_b, L1_attn_wv_w, L1_attn_wv_b, L1_attn_out_w, L1_attn_out_b, L1_ffn_gate_w, L1_ffn_w1, L1_ffn_b1, L1_ffn_w2, L1_ffn_b2, L1_ffn_ln_g, L1_ffn_ln_b):

    def _L0_attn_ref(x, W_qkv, b_qkv, W_out, b_out):
        import jax, jax.numpy as jnp
        import numpy as np
        D_MODEL = 128
        NUM_HEADS = 16
        D_HEAD = D_MODEL // NUM_HEADS
        B, T, C = x.shape
        H, Dh = (NUM_HEADS, D_HEAD)
        scale = jnp.sqrt(jnp.asarray(Dh, dtype=x.dtype))
        qkv = x @ W_qkv.T + b_qkv
        qkv = qkv.reshape(B, T, 3, H, Dh)
        q = qkv[:, :, 0].transpose(0, 2, 1, 3)
        k = qkv[:, :, 1].transpose(0, 2, 1, 3)
        v = qkv[:, :, 2].transpose(0, 2, 1, 3)
        attn = jnp.einsum('bhqd,bhkd->bhqk', q, k) / scale
        attn = jax.nn.softmax(attn, axis=-1)
        out = jnp.einsum('bhqk,bhkd->bhqd', attn, v)
        out = out.transpose(0, 2, 1, 3).reshape(B, T, C)
        return out @ W_out.T + b_out

    def _L0_ffn_ref(x, gate_W, gate_b, W1, b1, W2, b2, ln_gamma, ln_beta):
        import jax, jax.numpy as jnp
        import numpy as np
        D = 128
        E = 8
        H = 256
        TOP_K = 2
        ALPHA = 0.5
        LN_EPS = 1e-05

        def _experts_all(x, W1, b1, W2, b2):
            h = jax.nn.relu(jnp.einsum('bld,edh->eblh', x, W1) + b1[:, None, None, :])
            return jnp.einsum('eblh,ehd->ebld', h, W2) + b2[:, None, None, :]

        def _selected_expert(x, expert_idx, W1, b1, W2, b2):
            oh = jax.nn.one_hot(expert_idx, E, dtype=x.dtype)
            return jnp.einsum('ebld,ble->bld', _experts_all(x, W1, b1, W2, b2), oh)

        def _layer_norm(x, gamma, beta):
            mu = jnp.mean(x, axis=-1, keepdims=True)
            var = jnp.mean(jnp.square(x - mu), axis=-1, keepdims=True)
            return (x - mu) * jax.lax.rsqrt(var + LN_EPS) * gamma + beta
        residual = x
        gate_logits = jnp.einsum('bld,de->ble', x, gate_W) + gate_b
        gate_weights = jax.nn.softmax(gate_logits, axis=-1)
        topk_vals, topk_idx = jax.lax.top_k(gate_weights, TOP_K)
        boost = jax.lax.stop_gradient(x)
        outs = []
        for i in range(TOP_K):
            eo = _selected_expert(boost, topk_idx[:, :, i], W1, b1, W2, b2)
            outs.append(eo)
            if i < TOP_K - 1:
                boost = boost + ALPHA * jax.lax.stop_gradient(eo)
        fused = sum((topk_vals[:, :, i:i + 1] * outs[i] for i in range(TOP_K)))
        return _layer_norm(residual + fused, ln_gamma, ln_beta)

    def _L1_attn_ref(x, wg_w, wg_b, wq_w, wq_b, wk_w, wk_b, wv_w, wv_b, out_w, out_b):
        import jax, jax.numpy as jnp
        import numpy as np
        DIM = 128
        HEADS = 16
        HEAD_DIM = DIM // HEADS

        def feature_map(x):
            return jnp.where(x > 0, x + 1.0, jnp.exp(x))
        B, N, D = x.shape
        H, Hd = (HEADS, HEAD_DIM)
        q = (x @ wq_w + wq_b).reshape(B, N, H, Hd)
        k = (x @ wk_w + wk_b).reshape(B, N, H, Hd)
        v = (x @ wv_w + wv_b).reshape(B, N, H, Hd)
        gate = jax.nn.sigmoid(x @ wg_w + wg_b)
        q = feature_map(q)
        k = feature_map(k)
        kv = jnp.einsum('bnhd,bnhe->bhde', k, v)
        z = 1.0 / (jnp.einsum('bnhd,bhd->bnh', q, k.sum(axis=1)) + 1e-06)
        scores = jnp.einsum('bnhd,bhde,bnh->bnhe', q, kv, z)
        out = scores.reshape(B, N, D)
        return gate * out @ out_w + out_b

    def _L1_ffn_ref(x, gate_w, w1, b1, w2, b2, ln_g, ln_b):
        import jax, jax.numpy as jnp
        import numpy as np
        E, K, D = (8, 2, 128)
        B, S = (2, 512)

        def _layernorm(x, g, b, eps=1e-06):
            m = jnp.mean(x, axis=-1, keepdims=True)
            v = jnp.var(x, axis=-1, keepdims=True)
            return (x - m) * jax.lax.rsqrt(v + eps) * g + b
        orig_shape = x.shape
        xt = x.reshape(-1, orig_shape[-1])
        scores = xt @ gate_w
        ew, ei = jax.lax.top_k(scores, K)
        ew = jax.nn.softmax(ew, axis=-1)
        mask = ei[None, :, :] == jnp.arange(E)[:, None, None]
        wE = jnp.sum(ew[None, :, :] * mask, axis=-1)
        h = jax.nn.gelu(jnp.einsum('td,edf->etf', xt, w1) + b1[:, None, :], approximate=False)
        o = jnp.einsum('etf,efd->etd', h, w2) + b2[:, None, :]
        y = _layernorm(xt[None, :, :] + o, ln_g[:, None, :], ln_b[:, None, :])
        out = jnp.einsum('et,etd->td', wE, y)
        return out.reshape(orig_shape)
    x = L0_attn_x
    x = _layernorm(x + _L0_attn_ref(x, L0_attn_W_qkv, L0_attn_b_qkv, L0_attn_W_out, L0_attn_b_out), axis=-1)
    x = _layernorm(x + _L0_ffn_ref(x, L0_ffn_gate_W, L0_ffn_gate_b, L0_ffn_W1, L0_ffn_b1, L0_ffn_W2, L0_ffn_b2, L0_ffn_ln_gamma, L0_ffn_ln_beta), axis=-1)
    x = _layernorm(x + _L1_attn_ref(x, L1_attn_wg_w, L1_attn_wg_b, L1_attn_wq_w, L1_attn_wq_b, L1_attn_wk_w, L1_attn_wk_b, L1_attn_wv_w, L1_attn_wv_b, L1_attn_out_w, L1_attn_out_b), axis=-1)
    x = _layernorm(x + _L1_ffn_ref(x, L1_ffn_gate_w, L1_ffn_w1, L1_ffn_b1, L1_ffn_w2, L1_ffn_b2, L1_ffn_ln_g, L1_ffn_ln_b), axis=-1)
    return x

_drawn_inputs = setup_inputs


def setup_inputs(seed=0):
    import zlib

    import numpy as np

    out = dict(_drawn_inputs(seed))
    spreads = {'L0_ffn_gate_b': (0.0, 0.612),
     'L0_ffn_b1': (0.0, 0.8),
     'L0_ffn_b2': (0.0, 0.535),
     'L0_ffn_ln_gamma': (1.0, 0.2),
     'L0_ffn_ln_beta': (0.0, 0.1),
     'L1_attn_wg_b': (0.0, 0.8),
     'L1_attn_wq_b': (0.0, 2.0),
     'L1_attn_wk_b': (0.0, 2.0),
     'L1_attn_wv_b': (0.0, 0.1),
     'L1_attn_out_b': (0.0, 0.1),
     'L1_ffn_b1': (0.0, 0.8),
     'L1_ffn_b2': (0.0, 0.288),
     'L1_ffn_ln_g': (1.0, 0.2),
     'L1_ffn_ln_b': (0.0, 0.1)}
    factors = {'L0_ffn_gate_W': 4.125,
     'L0_ffn_W1': 7.972,
     'L0_ffn_W2': 5.979,
     'L1_attn_wq_w': 4.877,
     'L1_attn_wk_w': 2.931,
     'L1_ffn_w1': 4.173,
     'L1_ffn_w2': 3.824}
    for name, (base, spread) in spreads.items():
        noise = np.random.default_rng([zlib.crc32(name.encode()), seed]).standard_normal(out[name].shape)
        drawn = base * np.exp(spread * noise) if base else spread * noise
        out[name] = jnp.asarray(drawn.astype(out[name].dtype))
    for name, factor in factors.items():
        out[name] = (out[name] * factor).astype(out[name].dtype)
    return out
```

```python
from contextlib import ExitStack

import concourse.bass as bass
from concourse import mybir

F32 = mybir.dt.float32
F32R = mybir.dt.float32r
U32 = mybir.dt.uint32
ALU = mybir.AluOpType
ACT = mybir.ActivationFunctionType
AX_X = mybir.AxisListType.X

P = 128
D = 128
HEADS = 16
DH = D // HEADS
EXPERTS = 8
HID = 256
HH = HID // P
SEQS = 8
T = 256
TT = T // P
G = 4
QD = 4
PIECES = 4
SCALE = 1.0 / float(DH) ** 0.5
BIG = 1.0e30
INFO = 32
LN_EPS = 1e-5
LN_EPS_EXPERT = 1e-6


NINF = EXPERTS * HID + D
PACK_A = [("wqk", 2 * D), ("bqk", 2), ("wv", D), ("ident", P)]
PACK_B = [("wo", D), ("g0w", EXPERTS), ("iota", EXPERTS), ("blockmask", P), ("wq1", D), ("bq1", 1),
          ("wkvg", 3 * D), ("wout", D), ("g1w", EXPERTS), ("b1b", EXPERTS * HH), ("lowrows", 1)]
ROW_A = [("bv", D)]
ROW_B = [("bo", D), ("g0b", EXPERTS), ("gam0", D), ("bet0", D), ("bkvg", 3 * D), ("bout", D),
         ("b2b", EXPERTS * D), ("lng", EXPERTS * D)]


def build(nc, xT, xtok, pack_a, pack_b, row_a, row_b, lnb, info, w1a, w2a, w1b, w2b, out):
    with ExitStack() as ctx:
        def sb(name, shape, dt=F32):
            return ctx.enter_context(nc.sbuf_tensor(name, shape, dt))

        def bank(name):
            return ctx.enter_context(nc.psum_tensor(name, [P, 512], F32))

        packA = sb("packA", [P, sum(n for _, n in PACK_A)])
        packB = sb("packB", [P, sum(n for _, n in PACK_B)])
        rowA = sb("rowA", [P, sum(n for _, n in ROW_A)])
        rowB = sb("rowB", [P, sum(n for _, n in ROW_B)])
        part = {}
        for tile, names in ((packA, PACK_A), (packB, PACK_B), (rowA, ROW_A), (rowB, ROW_B)):
            at = 0
            for name, n in names:
                part[name] = tile[:, at:at + n]
                at += n
        idn, bmask, iota, lowr = part["ident"], part["blockmask"], part["iota"], part["lowrows"][0:INFO, :]
        Wqk = part["wqk"].rearrange("p (a d) -> p a d", a=2)
        Bqk, Wv, Wo, G0w, Wq1, Bq1 = (part[k] for k in ("bqk", "wv", "wo", "g0w", "wq1", "bq1"))
        Wkvg, Wout, G1w = part["wkvg"], part["wout"], part["g1w"]
        B1b = part["b1b"].rearrange("p (e h) -> p e h", e=EXPERTS)
        Bv, Bo, G0b, Gam0, Bet0, Bkvg, Bout = (
            part[k] for k in ("bv", "bo", "g0b", "gam0", "bet0", "bkvg", "bout"))
        B2b = part["b2b"].rearrange("p (e d) -> p e d", e=EXPERTS)
        Lng = part["lng"].rearrange("p (e d) -> p e d", e=EXPERTS)
        Lnb = sb("Lnb", [EXPERTS, D])
        W1H = [sb(f"W1H{n}", [P, EXPERTS, HID], F32R) for n in range(2)]
        W1L = [sb(f"W1L{n}", [P, EXPERTS, HID], F32R) for n in range(2)]
        W2H = [sb(f"W2H{n}", [P, EXPERTS, HH, D], F32R) for n in range(2)]
        W2L = [sb(f"W2L{n}", [P, EXPERTS, HH, D], F32R) for n in range(2)]
        infoW = sb("infoW", [INFO, NINF], F32R)
        mhalf = sb("mhalf", [P, TT * EXPERTS])

        den = sb("den", [P, TT, D])
        xTs = sb("xTs", [P, T])
        xto = sb("xto", [P, TT, D])
        xb = sb("xb", [P, TT, D])
        qkH = sb("qkH", [P, 2, T], F32R)
        qkL = sb("qkL", [P, 2, T], F32R)
        Qs = sb("Qs", [P, G, T], F32R)
        Km = sb("Km", [P, QD, G, T], F32R)
        Vst = sb("Vst", [P, TT, HEADS, 32])
        mx = sb("mx", [P, G, QD, TT])
        nmH = sb("nmH", [P, G, QD, TT], F32R)
        Mx = sb("Mx", [P, G, TT, P])
        PRING = 8
        Pt = sb("Pt", [P, PRING, TT * T])
        rec = sb("rec", [P, TT, HEADS])
        x1 = sb("x1", [P, TT, D])
        statA = sb("statA", [P, TT, 6])
        mvA = sb("mvA", [P, TT, 2])
        rsA = sb("rsA", [P, TT])
        x1f = sb("x1f", [P, T])
        x1H = sb("x1H", [P, T], F32R)
        x1L = sb("x1L", [P, T], F32R)
        lg0 = sb("lg0", [P, TT, EXPERTS])
        top0 = sb("top0", [P, TT, EXPERTS])
        ix0 = sb("ix0", [P, TT, EXPERTS], U32)
        ixf0 = sb("ixf0", [P, TT, EXPERTS])
        dl0 = sb("dl0", [P, TT, EXPERTS])
        e0 = sb("e0", [P, TT, EXPERTS])
        s0 = sb("s0", [P, TT])
        r0 = sb("r0", [P, TT])
        val0 = sb("val0", [P, TT, 2])
        route = sb("route", [P, TT, 2, INFO])
        rm = sb("rm", [INFO, 2, T], F32R)

        HRING = 4
        hH = sb("hH", [P, HRING, HH * T], F32R)
        hL = sb("hL", [P, HRING, HH * T], F32R)
        x2f = sb("x2f", [P, T])
        x2H = sb("x2H", [P, T], F32R)
        x2L = sb("x2L", [P, T], F32R)
        eo = sb("eo", [P, 2, T])
        f0 = sb("f0", [P, TT, D])
        f1 = sb("f1", [P, TT, D])
        n0 = sb("n0", [P, TT, D])
        ng = sb("ng", [P, TT, D])
        xbet = sb("xbet", [P, TT, D])
        x2 = sb("x2", [P, TT, D])
        statB = sb("statB", [P, 2, TT, 6])
        mvB = sb("mvB", [P, 2, TT, 2])
        rsB = sb("rsB", [P, 2, TT])

        xcf = sb("xcf", [P, T])
        eq = sb("eq", [P, T])
        pq = sb("pq", [P, T])
        qf = sb("qf", [P, T])
        KVG = sb("KVG", [P, TT, 3 * D + 2])
        kf = sb("kf", [P, TT, D])
        BD = sb("BD", [P, 2 * D])
        xob = sb("xob", [P, TT, D])
        x3 = sb("x3", [P, TT, D])
        statC = sb("statC", [P, TT, 6])
        mvC = sb("mvC", [P, TT, 2])
        rsC = sb("rsC", [P, TT])
        x3H = sb("x3H", [P, T], F32R)
        x3L = sb("x3L", [P, T], F32R)
        lg1 = sb("lg1", [P, TT, EXPERTS])
        top1 = sb("top1", [P, TT, EXPERTS])
        ix1 = sb("ix1", [P, TT, EXPERTS], U32)
        ixf1 = sb("ixf1", [P, TT, EXPERTS])
        dl1 = sb("dl1", [P, TT, 1])
        e1 = sb("e1", [P, TT, 1])
        s1 = sb("s1", [P, TT, 1])
        w1 = sb("w1", [P, TT, 2])
        ohw = sb("ohw", [P, 2, TT, EXPERTS])
        wE = sb("wE", [P, TT, EXPERTS])
        wET = sb("wET", [EXPERTS, T])

        GRING = 2
        gf = sb("gf", [P, GRING, HH * T])
        V = sb("V", [P, TT, EXPERTS, D])
        statD = sb("statD", [P, TT * EXPERTS, 6])
        smD = sb("smD", [P, TT * EXPERTS])
        dfD = sb("dfD", [P, TT * EXPERTS])
        qdD = sb("qdD", [P, TT * EXPERTS])
        ddD = sb("ddD", [P, TT * EXPERTS])
        vrD = sb("vrD", [P, TT * EXPERTS])
        rsD = sb("rsD", [P, TT * EXPERTS])
        aD = sb("aD", [P, TT * EXPERTS])
        cD = sb("cD", [P, TT * EXPERTS])
        zD = sb("zD", [P, TT, D])
        res = sb("res", [P, TT, D])
        statE = sb("statE", [P, TT, 6])
        mvE = sb("mvE", [P, TT, 2])
        rsE = sb("rsE", [P, TT])

        rawW = V[:].rearrange("p t e d -> p (t e d)")
        infoRaw = Pt[0:INFO].rearrange("p r n -> p (r n)")[:, 0:NINF]
        yA, yB, yC, yD = xb, xbet, xob, zD
        uk, ek, eg, sg = f0, f1, n0, ng
        rden, go = f0, f1
        gT, x3f = xcf, eq
        Ot = gf[:].rearrange("p a (b t) -> p (a b) t", b=2)
        AoT, rdD = x2f, den
        Ao, uq = eo[:, 0].rearrange("p (a d) -> p a d", a=TT), eo[:, 1]

        HIGH = [W1H[0][:], W2H[0][:], W1H[1][:], W2H[1][:]]
        LOW = [W1L[0][:], W2L[0][:], W1L[1][:], W2L[1][:]]
        for weights in (HIGH, LOW):
            for k in range(4):
                weights[k] = weights[k].rearrange("p a b -> p (a b)" if k % 2 == 0 else "p a b c -> p (a b c)")

        SA = [bank(f"SA{n}") for n in range(2)]
        SB = [bank(f"SB{n}") for n in range(2)]
        PA = bank("PA")
        Z = [bank(f"Z{n}") for n in range(2)]
        MI = bank("MI")

        q_stack = nc.dram_tensor("q_stack", [QD, PIECES, 32, T], F32)
        k_stack = nc.dram_tensor("k_stack", [QD, PIECES, 32, T], F32)

        sem, per_sequence = {}, {}
        for name, per in (
                ("near_consts", 0), ("consts", 0), ("info_in", 0), ("raw_in", 0), ("raw_high", 0), ("raw_split", 0),
                ("cleared", 0), ("held", 0), ("filled", 0), ("stack_filled", 0), ("info_high", 0), ("info_split", 0),
                ("x_in", 32), ("qk_psum", 1), ("v_psum", 1), ("qk_high", 2), ("qk_low", 2), ("v_done", 2),
                ("stack_out", 16 * 2 * QD * (PIECES - 1)), ("stack_in", 16 * (1 + QD)), ("xb_done", 1),
                ("max_psum", HEADS), ("max_done", HEADS), ("negmax", 3), ("negmax_psum", 2),
                ("q_shifted", 2), ("exp_psum", HEADS), ("exp_done", HEADS), ("pv_psum", G),
                ("o_copied", 2), ("o_psum", TT), ("o_inverse", TT), ("o_done", TT), ("oT_psum", 1),
                ("oT_done", 1), ("attn_psum", 1), ("attn_norm", 6), ("attn_power", 1), ("x1_done", TT),
                ("x1T_psum", 1), ("x1T_high", 2), ("x1T_low", 1), ("gate0_psum", 1), ("pick0", 13),
                ("gate0_exp", 1), ("value0", 3), ("route_psum", 1), ("route_done", 1),
                ("hid0_psum", 2 * EXPERTS), ("hid0_high", 2 * EXPERTS), ("hid0_low", 2 * EXPERTS),
                ("out0_psum", 2 * EXPERTS), ("out0_copied", 2), ("boosted", 3), ("out0T_psum", 1),
                ("moe0_norm", 18), ("moe0_power", 2), ("xbet_done", 1), ("x2_done", TT),
                ("x2T_psum", 1), ("x2T_done", 1), ("q1_psum", 1), ("kvg_psum", TT), ("q1_min", 1),
                ("q1_exp", 2), ("q1_done", 1), ("kvg_done", TT), ("k1_min", 1), ("kg_exp", 2),
                ("k1_done", 1), ("gate1_done", 2), ("kv_psum", 1), ("kv_blocks", 2), ("lin_psum", 1),
                ("lin_gated", 4), ("linT_psum", 1), ("linT_done", 1), ("xob_done", 1),
                ("linout_psum", 1), ("lin_norm", 6), ("lin_power", 1), ("x3_done", TT),
                ("x3T_psum", 1), ("x3T_high", 2), ("x3T_low", 1), ("gate1_psum", 1), ("pick1", 7),
                ("pick1_exp", 1), ("weight1", 7), ("weights_done", 1), ("weightsT_psum", 1),
                ("weightsT_done", 1),
                ("hid1_psum", EXPERTS), ("hid1_gelu", 2 * EXPERTS), ("hid1_high", EXPERTS),
                ("hid1_low_even", EXPERTS // 2), ("hid1_low_odd", EXPERTS // 2), ("out1_psum", EXPERTS),
                ("xbe_done", TT), ("expert_sum", 4), ("expert_norm", 23), ("expert_power", 1),
                ("expert_scaled", TT * EXPERTS), ("expert_gamma", TT), ("beta_psum", 1),
                ("expert_total", TT), ("last_norm", 7), ("last_power", 1), ("res_done", TT),
                ("stored", 16)):
            sem[name] = ctx.enter_context(nc.semaphore(name))
            per_sequence[name] = per

        def count(name, b, step):
            value = b * per_sequence[name] + step
            return max(value, 0) if isinstance(value, int) else value

        def both(t):
            return t.rearrange("p a b -> p (a b)")

        block = ctx.enter_context(nc.Block())

        @block.sync
        def _(sp):
            def load_x(b):
                sp.wait_ge(sem["qk_psum"], count("qk_psum", b - 1, 1))
                sp.wait_ge(sem["v_psum"], count("v_psum", b - 1, 1))
                sp.wait_ge(sem["xb_done"], count("xb_done", b - 1, 1))
                sp.dma_start(xTs[:], xT[b]).then_inc(sem["x_in"], 16)
                sp.dma_start(xto[:], xtok[b]).then_inc(sem["x_in"], 16)

            def stack(b):
                sp.wait_ge(sem["stack_in"], count("stack_in", b - 1, 16 * (1 + QD)))
                sp.wait_ge(sem["qk_high"], count("qk_high", b, 2))
                for i in range(QD):
                    rows = slice(32 * i, 32 * i + 32)
                    for r in (0, 2):
                        sp.dma_start(q_stack[i, r], qkH[rows, 0, :].bitcast(F32)).then_inc(sem["stack_out"], 16)
                    for r in (0, 1):
                        sp.dma_start(k_stack[i, r], qkH[rows, 1, :].bitcast(F32)).then_inc(sem["stack_out"], 16)
                sp.wait_ge(sem["qk_low"], count("qk_low", b, 2))
                for i in range(QD):
                    rows = slice(32 * i, 32 * i + 32)
                    sp.dma_start(q_stack[i, 1], qkL[rows, 0, :].bitcast(F32)).then_inc(sem["stack_out"], 16)
                    sp.dma_start(k_stack[i, 2], qkL[rows, 1, :].bitcast(F32)).then_inc(sem["stack_out"], 16)
                sp.wait_ge(sem["stack_out"], count("stack_out", b, 16 * 2 * QD * (PIECES - 1)))
                sp.wait_ge(sem["exp_psum"], count("exp_psum", b - 1, HEADS))
                sp.dma_start(Qs[:].rearrange("p g t -> p (g t)").bitcast(F32),
                             q_stack[:].rearrange("i r (d g) t -> (i r d) (g t)", g=G)).then_inc(sem["stack_in"], 16)
                for i in range(QD):
                    sp.dma_start(Km[32 * i:32 * i + 32, i].rearrange("p g t -> p (g t)").bitcast(F32),
                                 k_stack[i].rearrange("r (d g) t -> (r d) (g t)", g=G)).then_inc(sem["stack_in"], 16)

            def store(b):
                sp.wait_ge(sem["res_done"], count("res_done", b, TT))
                sp.dma_start(out[b], res[:]).then_inc(sem["stored"], 16)

            sp.dma_start(packA[:], pack_a).then_inc(sem["near_consts"], 16)
            load_x(0)
            sp.dma_start(rowA[:], row_a[None, :].broadcast_to([P, row_a.shape[0]])).then_inc(sem["near_consts"], 16)
            sp.dma_start(packB[:], pack_b).then_inc(sem["consts"], 16)
            sp.dma_start(rowB[:], row_b[None, :].broadcast_to([P, row_b.shape[0]])).then_inc(sem["consts"], 16)
            sp.dma_start(infoRaw, info).then_inc(sem["info_in"], 16)
            sp.dma_start(rawW, w1a).then_inc(sem["raw_in"], 16)
            sp.wait_ge(sem["filled"], 1)
            for i in range(QD):
                sp.dma_start(q_stack[i, PIECES - 1].rearrange("(a b) t -> a (b t)", a=8),
                             Km[0:8, QD - 1].rearrange("p g t -> p (g t)").bitcast(F32)).then_inc(sem["stack_filled"], 16)
                sp.dma_start(k_stack[i, PIECES - 1].rearrange("(a b) t -> a (b t)", a=8),
                             Mx[0:8].rearrange("p g a b -> p (g a b)")).then_inc(sem["stack_filled"], 16)
            sp.wait_ge(sem["stack_filled"], 16 * 2 * QD)
            stack(0)
            load_x(1)
            for n, source in enumerate((w2a, w1b, w2b)):
                sp.wait_ge(sem["raw_split"], n + 1)
                sp.dma_start(rawW, source).then_inc(sem["raw_in"], 16)
            sp.dma_start(Lnb[:], lnb).then_inc(sem["raw_in"], 16)
            stack(1)
            load_x(2)
            with sp.Fori(2, SEQS - 1) as b:
                stack(b)
                load_x(b + 1)
                store(b - 2)
            stack(SEQS - 1)
            for b in range(SEQS - 3, SEQS):
                store(b)
            sp.wait_ge(sem["stored"], 16 * SEQS)

        @block.gpsimd
        def _(pool):
            pool.memset(Mx[:].rearrange("p g a b -> p (g a b)"), 1.0).then_inc(sem["cleared"], 1)
            pool.wait_ge(sem["cleared"], 1)
            pool.memset(Km[:].rearrange("p i g t -> p (i g t)").bitcast(F32), 0.0).then_inc(sem["filled"], 1)
            pool.memset(Vst[:].rearrange("p a b c -> p (a b c)"), 0.0).then_inc(sem["cleared"], 1)
            pool.memset(route[:].rearrange("p a b c -> p (a b c)"), 0.0).then_inc(sem["cleared"], 1)
            pool.wait_ge(sem["cleared"], 3)
            pool.memset(Vst[:, :, :, DH:DH + 1], 1.0).then_inc(sem["filled"], 1)
            pool.memset(route[:, :, :, 16:18], 1.0).then_inc(sem["filled"], 1)
            pool.memset(mhalf[:], -0.5).then_inc(sem["filled"], 1)
            pool.memset(KVG[:, :, 3 * D:3 * D + 2], 1.0).then_inc(sem["filled"], 1)
            pool.wait_ge(sem["stack_filled"], 16 * 2 * QD)
            pool.memset(Mx[:].rearrange("p g a b -> p (g a b)"), 0.0).then_inc(sem["filled"], 1)

            def split_low(k):
                pool.wait_ge(sem["raw_high"], k + 1)
                pool.tensor_tensor(LOW[k], rawW, HIGH[k].bitcast(F32), ALU.subtract).then_inc(sem["raw_split"], 1)

            def power(target, variance, name):
                pool.tensor_tensor(target, variance, mhalf[:, 0:variance.shape[1]], ALU.pow).then_inc(sem[name], 1)

            def turn(m1, m0, nx):
                if nx is not None:
                    pool.wait_ge(sem["x_in"], count("x_in", nx, 32))
                    if isinstance(nx, int) and nx == 0:
                        pool.wait_ge(sem["consts"], 16 * 2)
                    pool.wait_ge(sem["x1_done"], count("x1_done", nx - 1, TT))
                    pool.tensor_tensor(xb[:], xto[:], Bo[:, None, :].broadcast_to([P, TT, D]), ALU.add).then_inc(sem["xb_done"], 1)
                    if isinstance(nx, int) and nx == 0:
                        split_low(0)
                        split_low(1)
                if m1 is not None:
                    pool.wait_ge(sem["x3_done"], count("x3_done", m1, TT))
                    pool.wait_ge(sem["expert_total"], count("expert_total", m1 - 1, TT))
                    for tt in range(TT):
                        pool.tensor_tensor(V[:, tt], x3[:, tt][:, None, :].broadcast_to([P, EXPERTS, D]),
                                           B2b, ALU.add).then_inc(sem["xbe_done"], 1)
                    for e in range(1, EXPERTS, 2):
                        pool.wait_ge(sem["hid1_high"], count("hid1_high", m1, e + 1))
                        if e >= HRING:
                            pool.wait_ge(sem["out1_psum"], count("out1_psum", m1, e - HRING + 1))
                        else:
                            pool.wait_ge(sem["out0_psum"], count("out0_psum", m1, 2 * EXPERTS - HRING + e + 1))
                        pool.tensor_tensor(hL[:, e % HRING], gf[:, e % GRING],
                                           hH[:, e % HRING].bitcast(F32), ALU.subtract).then_inc(sem["hid1_low_odd"], 1)
                if m0 is not None:
                    pool.wait_ge(sem["x1_done"], count("x1_done", m0, TT))
                    pool.wait_ge(sem["x2_done"], count("x2_done", m0 - 1, TT))
                    pool.tensor_tensor(xbet[:], x1[:], Bet0[:, None, :].broadcast_to([P, TT, D]), ALU.add).then_inc(sem["xbet_done"], 1)
                if m1 is not None:
                    pool.wait_ge(sem["expert_norm"], count("expert_norm", m1, 21))
                    power(rsD[:], vrD[:], "expert_power")
                    pool.wait_ge(sem["expert_norm"], count("expert_norm", m1, 23))
                    pool.sem_inc(sem["held"], 1)
                    for n in range(TT * EXPERTS):
                        tt, e = divmod(n, EXPERTS)
                        pool.tensor_scalar(V[:, tt, e], V[:, tt, e], aD[:, n:n + 1], cD[:, n:n + 1],
                                           ALU.mult, ALU.add).then_inc(sem["expert_scaled"], 1)
                    for tt in range(TT):
                        pool.wait_ge(sem["expert_scaled"], count("expert_scaled", m1, (tt + 1) * EXPERTS))
                        pool.tensor_tensor(V[:, tt], V[:, tt], Lng, ALU.mult).then_inc(sem["expert_gamma"], 1)
                    pool.wait_ge(sem["last_norm"], count("last_norm", m1, 7))
                    pool.wait_ge(sem["res_done"], count("res_done", m1 - 1, TT))
                    power(rsE[:], mvE[:, :, 1], "last_power")
                if m0 is not None:
                    pool.wait_ge(sem["moe0_norm"], count("moe0_norm", m0, 9))
                    pool.wait_ge(sem["moe0_norm"], count("moe0_norm", m0 - 1, 11))
                    power(rsB[:, 0], mvB[:, 0, :, 1], "moe0_power")
                if nx is not None:
                    pool.wait_ge(sem["attn_norm"], count("attn_norm", nx, 6))
                    pool.wait_ge(sem["x1_done"], count("x1_done", nx - 1, TT))
                    power(rsA[:], mvA[:, :, 1], "attn_power")
                if m0 is not None:
                    pool.wait_ge(sem["moe0_norm"], count("moe0_norm", m0, 18))
                    pool.wait_ge(sem["x2_done"], count("x2_done", m0 - 1, TT))
                    power(rsB[:, 1], mvB[:, 1, :, 1], "moe0_power")
                    pool.wait_ge(sem["x2_done"], count("x2_done", m0, TT))
                    pool.wait_ge(sem["x3_done"], count("x3_done", m0 - 1, TT))
                    pool.tensor_tensor(xob[:], x2[:], Bout[:, None, :].broadcast_to([P, TT, D]), ALU.add).then_inc(sem["xob_done"], 1)
                    pool.wait_ge(sem["lin_norm"], count("lin_norm", m0, 6))
                    pool.wait_ge(sem["x3_done"], count("x3_done", m0 - 1, TT))
                    power(rsC[:], mvC[:, :, 1], "lin_power")

            turn(None, None, 0)
            split_low(2)
            turn(None, 0, 1)
            split_low(3)
            pool.wait_ge(sem["raw_split"], 4)
            turn(0, 1, 2)
            with pool.Fori(2, SEQS - 1) as b:
                turn(b - 1, b, b + 1)
            turn(SEQS - 2, SEQS - 1, None)
            turn(SEQS - 1, None, None)

        @block.scalar
        def _(act):
            def qk_high(b):
                act.wait_ge(sem["qk_psum"], count("qk_psum", b, 1))
                act.wait_ge(sem["stack_out"], count("stack_out", b - 1, 16 * 2 * QD * (PIECES - 1)))
                for a in range(2):
                    act.activation(qkH[:, a], PA[:, a * T:(a + 1) * T], ACT.Identity,
                                   bias=Bqk[:, a:a + 1]).then_inc(sem["qk_high"], 1)

            def attn_exp(b, h):
                act.wait_ge(sem["exp_psum"], count("exp_psum", b, h + 1))
                if h < PRING:
                    act.wait_ge(sem["pv_psum"], count("pv_psum", b - 1, (HEADS - PRING + h) // QD + 1))
                else:
                    act.wait_ge(sem["pv_psum"], count("pv_psum", b, (h - PRING) // QD + 1))
                act.activation(Pt[:, h % PRING], SB[h % 2][:], ACT.Exp, scale=SCALE).then_inc(sem["exp_done"], 1)

            def o_copy(b, j):
                act.wait_ge(sem["pv_psum"], count("pv_psum", b, 2 * j + 2))
                act.wait_ge(sem["o_psum"], count("o_psum", b - 1, TT))
                act.activation(Ot[:, 2 * j:2 * j + 2].rearrange("p g t -> p (g t)"), PA[:], ACT.Identity).then_inc(sem["o_copied"], 1)

            def relu_high(b, n):
                act.wait_ge(sem["hid0_psum"], count("hid0_psum", b, n + 1))
                if n >= HRING:
                    act.wait_ge(sem["out0_psum"], count("out0_psum", b, n - HRING + 1))
                else:
                    act.wait_ge(sem["out1_psum"], count("out1_psum", b - 1, EXPERTS - HRING + n + 1))
                act.activation(hH[:, n % HRING], Z[n % 2][:], ACT.Relu).then_inc(sem["hid0_high"], 1)

            def out_copy(b, r):
                act.wait_ge(sem["out0_psum"], count("out0_psum", b, (r + 1) * EXPERTS))
                act.wait_ge(sem["out0T_psum"], count("out0T_psum", b - 1, 1))
                act.activation(eo[:, r], MI[:, 0:T], ACT.Identity).then_inc(sem["out0_copied"], 1)

            def gelu(b, e):
                act.wait_ge(sem["hid1_psum"], count("hid1_psum", b, e + 1))
                low = "hid1_low_odd" if e % 2 else "hid1_low_even"
                if e >= GRING:
                    act.wait_ge(sem[low], count(low, b, (e - GRING) // 2 + 1))
                else:
                    act.wait_ge(sem[low], count(low, b - 1, EXPERTS // 2))
                for hh in range(HH):
                    act.activation(gf[:, e % GRING, hh * T:(hh + 1) * T], Z[e % 2][:, hh * T:(hh + 1) * T],
                                   ACT.Gelu, bias=B1b[:, e, hh:hh + 1]).then_inc(sem["hid1_gelu"], 1)

            def gelu_high(b, e):
                act.wait_ge(sem["hid1_gelu"], count("hid1_gelu", b, 2 * e + 2))
                if e >= HRING:
                    act.wait_ge(sem["out1_psum"], count("out1_psum", b, e - HRING + 1))
                else:
                    act.wait_ge(sem["out0_psum"], count("out0_psum", b, 2 * EXPERTS - HRING + e + 1))
                act.activation(hH[:, e % HRING], gf[:, e % GRING], ACT.Identity).then_inc(sem["hid1_high"], 1)

            def turn(m1, m0, nx):
                if m1 is not None:
                    for e in range(EXPERTS):
                        gelu(m1, e)
                        if e >= 1:
                            gelu_high(m1, e - 1)
                        if e == 1 and nx is not None:
                            qk_high(nx)
                    gelu_high(m1, EXPERTS - 1)
                if m0 is not None:
                    for n in range(EXPERTS):
                        relu_high(m0, n)
                    out_copy(m0, 0)
                for n in range(EXPERTS):
                    if m0 is not None:
                        relu_high(m0, EXPERTS + n)
                    if nx is not None:
                        attn_exp(nx, 2 * n)
                        attn_exp(nx, 2 * n + 1)
                        if n == 6:
                            o_copy(nx, 0)
                if m0 is not None:
                    out_copy(m0, 1)
                if nx is not None:
                    o_copy(nx, 1)
                    act.wait_ge(sem["oT_psum"], count("oT_psum", nx, 1))
                    act.wait_ge(sem["attn_psum"], count("attn_psum", nx - 1, 1))
                    act.activation(AoT[:], PA[:, 0:T], ACT.Identity).then_inc(sem["oT_done"], 1)
                if m0 is not None:
                    act.wait_ge(sem["x2T_psum"], count("x2T_psum", m0, 1))
                    act.wait_ge(sem["kvg_psum"], count("kvg_psum", m0 - 1, TT))
                    act.activation(xcf[:], MI[:, 0:T], ACT.Identity).then_inc(sem["x2T_done"], 1)
                    act.wait_ge(sem["q1_min"], count("q1_min", m0, 1))
                    act.wait_ge(sem["q1_done"], count("q1_done", m0 - 1, 1))
                    act.activation(eq[:], uq, ACT.Exp).then_inc(sem["q1_exp"], 1)
                    act.activation(pq[:], MI[:, 0:T], ACT.Relu, bias=Bq1).then_inc(sem["q1_exp"], 1)
                if nx is not None:
                    act.wait_ge(sem["x1T_psum"], count("x1T_psum", nx, 1))
                    act.wait_ge(sem["boosted"], count("boosted", nx - 1, 1))
                    act.wait_ge(sem["hid0_psum"], count("hid0_psum", nx - 1, EXPERTS))
                    act.activation(x1f[:], PA[:, 0:T], ACT.Identity).then_inc(sem["x1T_high"], 1)
                    act.activation(x1H[:], PA[:, 0:T], ACT.Identity).then_inc(sem["x1T_high"], 1)
                if m0 is not None:
                    act.wait_ge(sem["k1_min"], count("k1_min", m0, 1))
                    act.wait_ge(sem["k1_done"], count("k1_done", m0 - 1, 1))
                    act.wait_ge(sem["gate1_done"], count("gate1_done", m0 - 1, 1))
                    act.activation(both(ek[:]), both(uk[:]), ACT.Exp).then_inc(sem["kg_exp"], 1)
                    act.activation(eg[:], KVG[:, :, 0:D], ACT.Exp, scale=-1.0).then_inc(sem["kg_exp"], 1)
                if nx is not None:
                    act.wait_ge(sem["pick0"], count("pick0", nx, 6))
                    act.wait_ge(sem["value0"], count("value0", nx - 1, 3))
                    act.activation(both(e0[:]), both(dl0[:]), ACT.Exp).then_inc(sem["gate0_exp"], 1)
                    act.wait_ge(sem["route_psum"], count("route_psum", nx, 1))
                    act.wait_ge(sem["out0_psum"], count("out0_psum", nx - 1, 2 * EXPERTS))
                    act.activation(both(rm[:]), PA[0:INFO, :], ACT.Identity).then_inc(sem["route_done"], 1)
                if m0 is not None:
                    act.wait_ge(sem["linT_psum"], count("linT_psum", m0, 1))
                    act.wait_ge(sem["linout_psum"], count("linout_psum", m0 - 1, 1))
                    act.activation(gT[:], MI[:, 0:T], ACT.Identity).then_inc(sem["linT_done"], 1)
                    act.wait_ge(sem["x3T_psum"], count("x3T_psum", m0, 1))
                    act.wait_ge(sem["gate1_psum"], count("gate1_psum", m0 - 1, 1))
                    act.wait_ge(sem["hid1_psum"], count("hid1_psum", m0 - 1, EXPERTS))
                    act.activation(x3f[:], MI[:, 0:T], ACT.Identity).then_inc(sem["x3T_high"], 1)
                    act.activation(x3H[:], MI[:, 0:T], ACT.Identity).then_inc(sem["x3T_high"], 1)
                    act.wait_ge(sem["pick1"], count("pick1", m0, 6))
                    act.wait_ge(sem["weight1"], count("weight1", m0 - 1, 3))
                    act.activation(e1[:], dl1[:], ACT.Exp).then_inc(sem["pick1_exp"], 1)
                    act.wait_ge(sem["weightsT_psum"], count("weightsT_psum", m0, 1))
                    act.wait_ge(sem["beta_psum"], count("beta_psum", m0 - 1, 1))
                    act.activation(wET[:], MI[0:EXPERTS, 0:T], ACT.Identity).then_inc(sem["weightsT_done"], 1)

            def split_high(k):
                act.wait_ge(sem["raw_in"], 16 * (k + 1) if k < 3 else 16 * 5)
                act.activation(HIGH[k], rawW, ACT.Identity).then_inc(sem["raw_high"], 1)

            act.wait_ge(sem["near_consts"], 32)
            qk_high(0)
            act.wait_ge(sem["info_in"], 16)
            act.activation(infoW[:], infoRaw, ACT.Identity).then_inc(sem["info_high"], 1)
            split_high(0)
            act.wait_ge(sem["info_split"], 1)
            for n in range(HEADS):
                attn_exp(0, n)
                if n == 4:
                    split_high(1)
                if n == 13:
                    o_copy(0, 0)
            o_copy(0, 1)
            act.wait_ge(sem["oT_psum"], count("oT_psum", 0, 1))
            act.activation(AoT[:], PA[:, 0:T], ACT.Identity).then_inc(sem["oT_done"], 1)
            act.wait_ge(sem["x1T_psum"], count("x1T_psum", 0, 1))
            act.activation(x1f[:], PA[:, 0:T], ACT.Identity).then_inc(sem["x1T_high"], 1)
            act.activation(x1H[:], PA[:, 0:T], ACT.Identity).then_inc(sem["x1T_high"], 1)
            act.wait_ge(sem["pick0"], count("pick0", 0, 6))
            act.activation(both(e0[:]), both(dl0[:]), ACT.Exp).then_inc(sem["gate0_exp"], 1)
            act.wait_ge(sem["route_psum"], count("route_psum", 0, 1))
            act.activation(both(rm[:]), PA[0:INFO, :], ACT.Identity).then_inc(sem["route_done"], 1)
            qk_high(1)
            split_high(2)
            turn(None, 0, 1)
            split_high(3)
            turn(0, 1, 2)
            with act.Fori(2, SEQS - 1) as b:
                turn(b - 1, b, b + 1)
            turn(SEQS - 2, SEQS - 1, None)
            turn(SEQS - 1, None, None)

        @block.tensor
        def _(pe):
            def project(b):
                pe.wait_ge(sem["x_in"], count("x_in", b, 32))
                pe.wait_ge(sem["route_done"], count("route_done", b - 1, 1))
                for a in range(2):
                    last = pe.matmul(PA[:, a * T:(a + 1) * T], Wqk[:, a], xTs[:], start=True, stop=True)
                last.then_inc(sem["qk_psum"], 1)
                pe.wait_ge(sem["weightsT_done"], count("weightsT_done", b - 2, 1))
                for tt in range(TT):
                    last = pe.matmul(MI[:, tt * D:(tt + 1) * D], xTs[:, tt * P:(tt + 1) * P], Wv,
                                     start=True, stop=True)
                last.then_inc(sem["v_psum"], 1)

            def max_scores(b, h):
                g, i = divmod(h, QD)
                if h == 0:
                    pe.wait_ge(sem["stack_in"], count("stack_in", b, 16 * (1 + QD)))
                if h < 2:
                    pe.wait_ge(sem["expert_sum"], count("expert_sum", b - 2, 4))
                    pe.wait_ge(sem["q_shifted"], count("q_shifted", b - 1, 2))
                else:
                    pe.wait_ge(sem["max_done"], count("max_done", b, h - 1))
                for tt in range(TT):
                    last = pe.matmul(SA[h % 2][:, tt * T:(tt + 1) * T], Qs[:, g, tt * P:(tt + 1) * P],
                                     Km[:, i, g], start=True, stop=True)
                last.then_inc(sem["max_psum"], 1)

            def negmax(b):
                pe.wait_ge(sem["negmax"], count("negmax", b, 3))
                for j in range(2):
                    for g in (2 * j, 2 * j + 1):
                        for tt in range(TT):
                            at = (g % 2) * T + tt * P
                            last = pe.transpose(SA[j][:, at:at + P], Mx[:, g, tt], idn)
                    last.then_inc(sem["negmax_psum"], 1)

            def exp_scores(b, h):
                g, i = divmod(h, QD)
                if h == 0:
                    pe.wait_ge(sem["expert_sum"], count("expert_sum", b - 2, 4))
                pe.wait_ge(sem["q_shifted"], count("q_shifted", b, g // 2 + 1))
                if h >= 2:
                    pe.wait_ge(sem["exp_done"], count("exp_done", b, h - 1))
                elif True:
                    pe.wait_ge(sem["o_done"], count("o_done", b - 1, TT))
                for kt in range(TT):
                    last = pe.matmul(SB[h % 2][:, kt * T:(kt + 1) * T], Km[:, i, g, kt * P:(kt + 1) * P],
                                     Qs[:, g], start=True, stop=True)
                last.then_inc(sem["exp_psum"], 1)

            def weighted_values(b, g):
                if g == 0:
                    pe.wait_ge(sem["v_done"], count("v_done", b, 2))
                    pe.wait_ge(sem["qk_low"], count("qk_low", b, 2))
                if g == 2:
                    pe.wait_ge(sem["o_copied"], count("o_copied", b, 1))
                pe.wait_ge(sem["exp_done"], count("exp_done", b, QD * g + QD))
                for kt in range(TT):
                    for i in range(QD):
                        h = QD * g + i
                        last = pe.matmul(PA[32 * i:32 * i + 32, (g % 2) * T:(g % 2 + 1) * T], Vst[:, kt, h],
                                         Pt[:, h % PRING, kt * T:(kt + 1) * T], start=(kt == 0),
                                         stop=(kt == TT - 1), skip_group_check=True)
                last.then_inc(sem["pv_psum"], 1)

            def attn_turns(b):
                pe.wait_ge(sem["o_copied"], count("o_copied", b, 2))
                pe.wait_ge(sem["exp_done"], count("exp_done", b, HEADS))
                for tt in range(TT):
                    for g in range(G):
                        last = pe.transpose(SB[tt][:, g * P:(g + 1) * P], Ot[:, g, tt * P:(tt + 1) * P], idn)
                    last.then_inc(sem["o_psum"], 1)

            def attn_out(b):
                pe.wait_ge(sem["o_done"], count("o_done", b, TT))
                for tt in range(TT):
                    last = pe.transpose(PA[:, tt * P:(tt + 1) * P], Ao[:, tt], idn)
                last.then_inc(sem["oT_psum"], 1)
                pe.wait_ge(sem["oT_done"], count("oT_done", b, 1))
                for tt in range(TT):
                    last = pe.matmul(PA[:, T + tt * D:T + (tt + 1) * D], AoT[:, tt * P:(tt + 1) * P], Wo,
                                     start=True, stop=True)
                last.then_inc(sem["attn_psum"], 1)

            def router0_in(b):
                pe.wait_ge(sem["x1_done"], count("x1_done", b, TT))
                for tt in range(TT):
                    last = pe.transpose(PA[:, tt * P:(tt + 1) * P], x1[:, tt], idn)
                last.then_inc(sem["x1T_psum"], 1)

            def router0_gate(b):
                pe.wait_ge(sem["x1T_high"], count("x1T_high", b, 2))
                pe.wait_ge(sem["x1T_low"], count("x1T_low", b, 1))
                for tt in range(TT):
                    last = pe.matmul(PA[:, tt * EXPERTS:(tt + 1) * EXPERTS], x1f[:, tt * P:(tt + 1) * P], G0w,
                                     start=True, stop=True)
                last.then_inc(sem["gate0_psum"], 1)

            def router0_route(b):
                pe.wait_ge(sem["pick0"], count("pick0", b, 13))
                for r in range(2):
                    for tt in range(TT):
                        at = r * T + tt * P
                        last = pe.transpose(PA[0:INFO, at:at + P], route[:, tt, r], idn)
                last.then_inc(sem["route_psum"], 1)

            def hidden0(b, n):
                r, e = divmod(n, EXPERTS)
                if n == 0:
                    pe.wait_ge(sem["x1T_high"], count("x1T_high", b, 2))
                    pe.wait_ge(sem["x1T_low"], count("x1T_low", b, 1))
                    pe.wait_ge(sem["route_done"], count("route_done", b, 1))
                if n == EXPERTS:
                    pe.wait_ge(sem["boosted"], count("boosted", b, 3))
                if n >= 2:
                    pe.wait_ge(sem["hid0_low"], count("hid0_low", b, n - 1))
                else:
                    pe.wait_ge(sem["hid1_gelu"], count("hid1_gelu", b - 1, 2 * (EXPERTS - 2 + n) + 2))
                high, low = ((x1H, x1L), (x2H, x2L))[r]
                for hh in range(HH):
                    z = Z[n % 2][:, hh * T:(hh + 1) * T]
                    w = slice(hh * P, (hh + 1) * P)
                    pe.matmul(z, W1H[0][:, e, w], high[:], start=True, stop=False)
                    pe.matmul(z, W1H[0][:, e, w], low[:], start=False, stop=False)
                    pe.matmul(z, W1L[0][:, e, w], high[:], start=False, stop=False)
                    at = e * HID + hh * P
                    last = pe.matmul(z, infoW[:, at:at + P], rm[:, r], start=False, stop=True)
                last.then_inc(sem["hid0_psum"], 1)

            def outs0(b, n):
                r, e = divmod(n, EXPERTS)
                o = MI[:, 0:T]
                if n == 0:
                    pe.wait_ge(sem["last_norm"], count("last_norm", b - 1, 1))
                    if not (isinstance(b, int) and b == SEQS - 1):
                        pe.wait_ge(sem["v_done"], count("v_done", b + 1, 2))
                if e == 0:
                    if r == 1:
                        pe.wait_ge(sem["out0_copied"], count("out0_copied", b, 1))
                    pe.matmul(o, infoW[:, EXPERTS * HID:NINF], rm[:, r], start=True, stop=False)
                pe.wait_ge(sem["hid0_low"], count("hid0_low", b, n + 1))
                for hh in range(HH):
                    h_high = hH[:, n % HRING, hh * T:(hh + 1) * T]
                    h_low = hL[:, n % HRING, hh * T:(hh + 1) * T]
                    pe.matmul(o, W2H[0][:, e, hh], h_high, start=False, stop=False)
                    pe.matmul(o, W2H[0][:, e, hh], h_low, start=False, stop=False)
                    last = pe.matmul(o, W2L[0][:, e, hh], h_high, start=False,
                                     stop=(e == EXPERTS - 1 and hh == HH - 1))
                last.then_inc(sem["out0_psum"], 1)

            def moe0_turns(b):
                pe.wait_ge(sem["out0_copied"], count("out0_copied", b, 2))
                for r in range(2):
                    for tt in range(TT):
                        at = (r * TT + tt) * D
                        last = pe.transpose(MI[:, at:at + D], eo[:, r, tt * P:(tt + 1) * P], idn)
                last.then_inc(sem["out0T_psum"], 1)

            def lin_in(b):
                pe.wait_ge(sem["x2_done"], count("x2_done", b, TT))
                for tt in range(TT):
                    last = pe.transpose(MI[:, tt * P:(tt + 1) * P], x2[:, tt], idn)
                last.then_inc(sem["x2T_psum"], 1)
                pe.wait_ge(sem["x2T_done"], count("x2T_done", b, 1))
                pe.matmul(MI[:, 0:T], Wq1, xcf[:], start=True, stop=True).then_inc(sem["q1_psum"], 1)
                for tt in range(TT):
                    pe.wait_ge(sem["hid0_low"], count("hid0_low", b, 2 * EXPERTS - 1 + tt))
                    pe.matmul(Z[tt][:, 0:3 * D], xcf[:, tt * P:(tt + 1) * P], Wkvg, start=True, stop=True).then_inc(sem["kvg_psum"], 1)

            def lin_kv(b):
                pe.wait_ge(sem["q1_exp"], count("q1_exp", b, 2))
                pe.wait_ge(sem["k1_done"], count("k1_done", b, 1))
                pe.wait_ge(sem["kvg_done"], count("kvg_done", b, TT))
                for tt in range(TT):
                    last = pe.matmul(MI[:, 0:D + 1], kf[:, tt], KVG[:, tt, 2 * D:3 * D + 1], start=(tt == 0),
                                     stop=(tt == TT - 1))
                last.then_inc(sem["kv_psum"], 1)

            def lin_read(b):
                pe.wait_ge(sem["kv_blocks"], count("kv_blocks", b, 2))
                pe.wait_ge(sem["q1_done"], count("q1_done", b, 1))
                for tt in range(TT):
                    last = pe.matmul(MI[:, tt * 2 * D:(tt + 1) * 2 * D], qf[:, tt * P:(tt + 1) * P], BD[:],
                                     start=True, stop=True)
                last.then_inc(sem["lin_psum"], 1)

            def lin_out(b):
                pe.wait_ge(sem["lin_gated"], count("lin_gated", b, 4))
                for tt in range(TT):
                    last = pe.transpose(MI[:, tt * P:(tt + 1) * P], go[:, tt], idn)
                last.then_inc(sem["linT_psum"], 1)
                pe.wait_ge(sem["linT_done"], count("linT_done", b, 1))
                for tt in range(TT):
                    last = pe.matmul(MI[:, T + tt * D:T + (tt + 1) * D], gT[:, tt * P:(tt + 1) * P], Wout,
                                     start=True, stop=True)
                last.then_inc(sem["linout_psum"], 1)

            def router1(b):
                pe.wait_ge(sem["x3_done"], count("x3_done", b, TT))
                for tt in range(TT):
                    last = pe.transpose(MI[:, tt * P:(tt + 1) * P], x3[:, tt], idn)
                last.then_inc(sem["x3T_psum"], 1)
                pe.wait_ge(sem["x3T_high"], count("x3T_high", b, 2))
                pe.wait_ge(sem["x3T_low"], count("x3T_low", b, 1))
                for tt in range(TT):
                    last = pe.matmul(MI[:, tt * EXPERTS:(tt + 1) * EXPERTS], x3f[:, tt * P:(tt + 1) * P], G1w,
                                     start=True, stop=True)
                last.then_inc(sem["gate1_psum"], 1)
                pe.wait_ge(sem["weights_done"], count("weights_done", b, 1))
                for tt in range(TT):
                    last = pe.transpose(MI[0:EXPERTS, tt * P:(tt + 1) * P], wE[:, tt], idn)
                last.then_inc(sem["weightsT_psum"], 1)

            def hidden1(b, e):
                if e == 0:
                    pe.wait_ge(sem["x3T_high"], count("x3T_high", b, 2))
                    pe.wait_ge(sem["x3T_low"], count("x3T_low", b, 1))
                if e >= 2:
                    pe.wait_ge(sem["hid1_gelu"], count("hid1_gelu", b, 2 * e - 2))
                else:
                    pe.wait_ge(sem["kvg_done"], count("kvg_done", b, e + 1))
                for hh in range(HH):
                    z = Z[e % 2][:, hh * T:(hh + 1) * T]
                    w = slice(hh * P, (hh + 1) * P)
                    pe.matmul(z, W1H[1][:, e, w], x3H[:], start=True, stop=False)
                    pe.matmul(z, W1H[1][:, e, w], x3L[:], start=False, stop=False)
                    last = pe.matmul(z, W1L[1][:, e, w], x3H[:], start=False, stop=True)
                last.then_inc(sem["hid1_psum"], 1)

            def outs1(b, e, last_sequence):
                if e == 0:
                    if last_sequence:
                        pe.wait_ge(sem["expert_sum"], count("expert_sum", b - 1, 4))
                    else:
                        pe.wait_ge(sem["q_shifted"], count("q_shifted", b + 1, 2))
                        pe.wait_ge(sem["o_done"], count("o_done", b + 1, TT))
                low = "hid1_low_odd" if e % 2 else "hid1_low_even"
                pe.wait_ge(sem[low], count(low, b, e // 2 + 1))
                for tt in range(TT):
                    o = (SA, SB)[tt][e // 4][:, (e % 4) * D:(e % 4 + 1) * D]
                    for hh in range(HH):
                        at = hh * T + tt * P
                        h_high, h_low = hH[:, e % HRING, at:at + P], hL[:, e % HRING, at:at + P]
                        pe.matmul(o, h_high, W2H[1][:, e, hh], start=(hh == 0), stop=False)
                        pe.matmul(o, h_low, W2H[1][:, e, hh], start=False, stop=False)
                        last = pe.matmul(o, h_high, W2L[1][:, e, hh], start=False, stop=(hh == HH - 1))
                last.then_inc(sem["out1_psum"], 1)

            def beta_sums(b, nx):
                pe.wait_ge(sem["weightsT_done"], count("weightsT_done", b, 1))
                if nx is not None:
                    pe.wait_ge(sem["v_done"], count("v_done", nx, 2))
                for tt in range(TT):
                    last = pe.matmul(MI[:, tt * D:(tt + 1) * D], wET[:, tt * P:(tt + 1) * P], Lnb[:],
                                     start=True, stop=True)
                last.then_inc(sem["beta_psum"], 1)

            def turn(m1, m0, nx):
                if m1 is not None:
                    for e in range(EXPERTS):
                        hidden1(m1, e)
                        if e == 0 and nx is not None:
                            project(nx)
                        if e >= 1:
                            outs1(m1, e - 1, nx is None and m0 is None)
                    outs1(m1, EXPERTS - 1, False)
                    beta_sums(m1, nx)
                elif nx is not None:
                    project(nx)
                for r in range(2):
                    for e in range(EXPERTS):
                        n = r * EXPERTS + e
                        if m0 is not None:
                            hidden0(m0, n)
                        if nx is not None:
                            if r == 0:
                                max_scores(nx, 2 * e)
                                max_scores(nx, 2 * e + 1)
                            else:
                                exp_scores(nx, 2 * e)
                                exp_scores(nx, 2 * e + 1)
                                if e in (3, 5, 7):
                                    weighted_values(nx, (e - 3) // 2)
                        if m0 is not None and e >= 1:
                            outs0(m0, n - 1)
                    if m0 is not None:
                        outs0(m0, r * EXPERTS + EXPERTS - 1)
                    if nx is not None and r == 0:
                        negmax(nx)
                if nx is not None:
                    weighted_values(nx, G - 1)
                if m0 is not None:
                    moe0_turns(m0)
                if nx is not None:
                    attn_turns(nx)
                    attn_out(nx)
                if m0 is not None:
                    lin_in(m0)
                if nx is not None:
                    router0_in(nx)
                if m0 is not None:
                    lin_kv(m0)
                if nx is not None:
                    router0_gate(nx)
                if m0 is not None:
                    lin_read(m0)
                if nx is not None:
                    router0_route(nx)
                if m0 is not None:
                    lin_out(m0)
                    router1(m0)

            pe.wait_ge(sem["near_consts"], 32)
            project(0)
            pe.wait_ge(sem["consts"], 16 * 2)
            for h in range(HEADS):
                max_scores(0, h)
            pe.wait_ge(sem["filled"], 6)
            negmax(0)
            for h in range(HEADS):
                exp_scores(0, h)
                if h in (7, 11, 15):
                    weighted_values(0, (h - 7) // 4)
            weighted_values(0, G - 1)
            attn_turns(0)
            attn_out(0)
            router0_in(0)
            router0_gate(0)
            router0_route(0)
            pe.wait_ge(sem["info_split"], 1)
            pe.wait_ge(sem["raw_split"], 2)
            turn(None, 0, 1)
            pe.wait_ge(sem["raw_split"], 4)
            turn(0, 1, 2)
            with pe.Fori(2, SEQS - 1) as b:
                turn(b - 1, b, b + 1)
            turn(SEQS - 2, SEQS - 1, None)
            turn(SEQS - 1, None, None)

        @block.vector
        def _(dve):
            def qk_low(b):
                dve.wait_ge(sem["qk_high"], count("qk_high", b, 2))
                dve.wait_ge(sem["stack_out"], count("stack_out", b - 1, 16 * 2 * QD * (PIECES - 1)))
                for a in range(2):
                    dve.scalar_tensor_tensor(out=qkL[:, a], in0=PA[:, a * T:(a + 1) * T],
                                             scalar=Bqk[:, a:a + 1], in1=qkH[:, a].bitcast(F32),
                                             op0=ALU.add, op1=ALU.subtract).then_inc(sem["qk_low"], 1)
                dve.wait_ge(sem["v_psum"], count("v_psum", b, 1))
                dve.wait_ge(sem["pv_psum"], count("pv_psum", b - 1, G))
                for kt in range(TT):
                    dve.tensor_tensor(Vst[:, kt, :, 0:DH],
                                      MI[:, kt * D:(kt + 1) * D].rearrange("p (h d) -> p h d", h=HEADS),
                                      Bv.rearrange("p (h d) -> p h d", h=HEADS), ALU.add).then_inc(sem["v_done"], 1)

            def maximum(b, h):
                g, i = divmod(h, QD)
                dve.wait_ge(sem["max_psum"], count("max_psum", b, h + 1))
                dve.tensor_reduce(mx[:, g, i], SA[h % 2][:].rearrange("p (q k) -> p q k", q=TT), AX_X, ALU.max).then_inc(sem["max_done"], 1)

            def negmax(b):
                at = Mx[:].rearrange("p g q (i c) -> p g i q c", c=32)
                dve.wait_ge(sem["max_done"], count("max_done", b, HEADS))
                dve.wait_ge(sem["negmax_psum"], count("negmax_psum", b - 1, 2))
                dve.tensor_scalar(nmH[:].rearrange("p g i q -> p (g i q)"),
                                  mx[:].rearrange("p g i q -> p (g i q)"), -1.0, None, ALU.mult).then_inc(sem["negmax"], 1)
                dve.tensor_scalar(at[:, :, :, :, 24], mx[:], -1.0, None, ALU.mult).then_inc(sem["negmax"], 1)
                dve.wait_ge(sem["negmax"], count("negmax", b, 2))
                dve.tensor_tensor(at[:, :, :, :, 25], at[:, :, :, :, 24], nmH[:].bitcast(F32), ALU.subtract).then_inc(sem["negmax"], 1)

            def shift(b):
                for j in range(2):
                    dve.wait_ge(sem["negmax_psum"], count("negmax_psum", b, j + 1))
                    q = Qs[:, 2 * j:2 * j + 2].rearrange("p g t -> p (g t)")
                    dve.tensor_tensor(q, SA[j][:], q.bitcast(F32), ALU.add).then_inc(sem["q_shifted"], 1)

            def attn_divide(b):
                for tt in range(TT):
                    o = SB[tt][:].rearrange("p (h c) -> p h c", c=32)
                    dve.wait_ge(sem["o_psum"], count("o_psum", b, tt + 1))
                    dve.reciprocal(rec[:, tt], o[:, :, DH]).then_inc(sem["o_inverse"], 1)
                    dve.wait_ge(sem["o_inverse"], count("o_inverse", b, tt + 1))
                    dve.wait_ge(sem["oT_psum"], count("oT_psum", b - 1, 1))
                    dve.tensor_tensor(Ao[:, tt].rearrange("p (h d) -> p h d", h=HEADS), o[:, :, 0:DH],
                                      rec[:, tt][:, :, None].broadcast_to([P, HEADS, DH]), ALU.mult).then_inc(sem["o_done"], 1)

            def statistics(b, name, step, y, stat, mv, eps):
                for tt in range(TT):
                    dve.bn_stats(stat[:, tt], y[:, tt]).then_inc(sem[name], 1)
                dve.wait_ge(sem[name], count(name, b, step + 2))
                dve.sem_inc(sem["held"], 1)
                for tt in range(TT):
                    dve.bn_aggr(mv[:, tt], stat[:, tt]).then_inc(sem[name], 1)
                dve.wait_ge(sem[name], count(name, b, step + 4))
                dve.tensor_scalar(mv[:, :, 1], mv[:, :, 1], eps, None, ALU.add).then_inc(sem[name], 1)

            def normalize(target, y, mv, rs, name):
                for tt in range(TT):
                    dve.tensor_scalar(target[:, tt], y[:, tt], mv[:, tt, 0:1], rs[:, tt:tt + 1],
                                      ALU.subtract, ALU.mult).then_inc(sem[name], 1)

            def attn_stats(b):
                dve.wait_ge(sem["attn_psum"], count("attn_psum", b, 1))
                dve.wait_ge(sem["xb_done"], count("xb_done", b, 1))
                dve.tensor_tensor(both(yA[:]), PA[:, T:2 * T], both(xb[:]), ALU.add).then_inc(sem["attn_norm"], 1)
                dve.wait_ge(sem["attn_norm"], count("attn_norm", b, 1))
                statistics(b, "attn_norm", 1, yA, statA, mvA, LN_EPS)

            def attn_norm(b):
                dve.wait_ge(sem["attn_power"], count("attn_power", b, 1))
                dve.wait_ge(sem["xbet_done"], count("xbet_done", b - 1, 1))
                dve.wait_ge(sem["x1T_psum"], count("x1T_psum", b - 1, 1))
                normalize(x1, yA, mvA, rsA, "x1_done")

            def x1_low(b):
                dve.wait_ge(sem["x1T_high"], count("x1T_high", b, 2))
                dve.wait_ge(sem["hid0_psum"], count("hid0_psum", b - 1, EXPERTS))
                dve.tensor_tensor(x1L[:], PA[:, 0:T], x1H[:].bitcast(F32), ALU.subtract).then_inc(sem["x1T_low"], 1)

            def pick_two(b, psum_name, bankt, bias, lg, top, ix, ixf, name):
                dve.wait_ge(sem[psum_name], count(psum_name, b, 1))
                if bias is None:
                    dve.tensor_copy(both(lg[:]), bankt[:, 0:TT * EXPERTS]).then_inc(sem[name], 1)
                else:
                    dve.tensor_tensor(lg[:], bankt[:, 0:TT * EXPERTS].rearrange("p (a e) -> p a e", a=TT),
                                      bias[:, None, :].broadcast_to([P, TT, EXPERTS]), ALU.add).then_inc(sem[name], 1)
                dve.wait_ge(sem[name], count(name, b, 1))
                dve.sem_inc(sem["held"], 1)
                for tt in range(TT):
                    dve.max(top[:, tt], lg[:, tt]).then_inc(sem[name], 1)
                dve.wait_ge(sem[name], count(name, b, 3))
                dve.sem_inc(sem["held"], 1)
                for tt in range(TT):
                    dve.max_index(ix[:, tt], top[:, tt], lg[:, tt]).then_inc(sem[name], 1)

            def router0_pick(b):
                pick_two(b, "gate0_psum", PA, G0b, lg0, top0, ix0, ixf0, "pick0")
                dve.wait_ge(sem["gate0_exp"], count("gate0_exp", b - 1, 1))
                dve.tensor_tensor(dl0[:], top0[:], top0[:, :, 0:1].broadcast_to([P, TT, EXPERTS]),
                                  ALU.subtract).then_inc(sem["pick0"], 1)
                dve.wait_ge(sem["pick0"], count("pick0", b, 5))
                dve.tensor_copy(both(ixf0[:]), both(ix0[:])).then_inc(sem["pick0"], 1)
                dve.wait_ge(sem["pick0"], count("pick0", b, 7))
                dve.wait_ge(sem["route_psum"], count("route_psum", b - 1, 1))
                for r in range(2):
                    for tt in range(TT):
                        dve.tensor_scalar(route[:, tt, r, 0:EXPERTS], iota, ixf0[:, tt, r:r + 1], None,
                                          ALU.is_equal).then_inc(sem["pick0"], 1)
                dve.wait_ge(sem["pick0"], count("pick0", b, 11))
                chosen = route[:, :, :, 0:EXPERTS]
                dve.tensor_scalar(route[:, :, :, EXPERTS:2 * EXPERTS], chosen, -1.0, None, ALU.add).then_inc(sem["pick0"], 1)
                dve.tensor_copy(route[:, :, :, INFO - EXPERTS:INFO], chosen).then_inc(sem["pick0"], 1)

            def router0_values(b):
                dve.wait_ge(sem["gate0_exp"], count("gate0_exp", b, 1))
                dve.tensor_reduce(s0[:], e0[:], AX_X, ALU.add).then_inc(sem["value0"], 1)
                dve.wait_ge(sem["value0"], count("value0", b, 1))
                dve.reciprocal(r0[:], s0[:]).then_inc(sem["value0"], 1)
                dve.wait_ge(sem["value0"], count("value0", b, 2))
                dve.tensor_tensor(val0[:], e0[:, :, 0:2], r0[:][:, :, None].broadcast_to([P, TT, 2]),
                                  ALU.mult).then_inc(sem["value0"], 1)

            def relu_low(b, n):
                dve.wait_ge(sem["hid0_high"], count("hid0_high", b, n + 1))
                if n >= HRING:
                    dve.wait_ge(sem["out0_psum"], count("out0_psum", b, n - HRING + 1))
                else:
                    dve.wait_ge(sem["out1_psum"], count("out1_psum", b - 1, EXPERTS - HRING + n + 1))
                dve.scalar_tensor_tensor(out=hL[:, n % HRING], in0=Z[n % 2][:], scalar=0.0,
                                         in1=hH[:, n % HRING].bitcast(F32), op0=ALU.max,
                                         op1=ALU.subtract).then_inc(sem["hid0_low"], 1)

            def boost(b):
                dve.wait_ge(sem["out0_copied"], count("out0_copied", b, 1))
                dve.scalar_tensor_tensor(out=x2f[:], in0=eo[:, 0], scalar=0.5, in1=x1f[:], op0=ALU.mult,
                                         op1=ALU.add).then_inc(sem["boosted"], 1)
                dve.wait_ge(sem["boosted"], count("boosted", b, 1))
                dve.wait_ge(sem["hid0_psum"], count("hid0_psum", b - 1, 2 * EXPERTS))
                dve.tensor_copy(x2H[:], x2f[:]).then_inc(sem["boosted"], 1)
                dve.wait_ge(sem["boosted"], count("boosted", b, 2))
                dve.tensor_tensor(x2L[:], x2f[:], x2H[:].bitcast(F32), ALU.subtract).then_inc(sem["boosted"], 1)

            def moe0_stats(b):
                dve.wait_ge(sem["out0T_psum"], count("out0T_psum", b, 1))
                dve.wait_ge(sem["value0"], count("value0", b, 3))
                for tt in range(TT):
                    dve.scalar_tensor_tensor(out=f0[:, tt], in0=MI[:, tt * D:(tt + 1) * D],
                                             scalar=val0[:, tt, 0:1], in1=x1[:, tt], op0=ALU.mult,
                                             op1=ALU.add).then_inc(sem["moe0_norm"], 1)
                dve.wait_ge(sem["moe0_norm"], count("moe0_norm", b, 2))
                for tt in range(TT):
                    dve.scalar_tensor_tensor(out=f1[:, tt], in0=MI[:, (TT + tt) * D:(TT + tt + 1) * D],
                                             scalar=val0[:, tt, 1:2], in1=f0[:, tt], op0=ALU.mult,
                                             op1=ALU.add).then_inc(sem["moe0_norm"], 1)
                dve.wait_ge(sem["moe0_norm"], count("moe0_norm", b, 4))
                statistics(b, "moe0_norm", 4, f1, statB[:, 0], mvB[:, 0], LN_EPS)

            def moe0_norm(b):
                dve.wait_ge(sem["moe0_power"], count("moe0_power", b, 1))
                normalize(n0, f1, mvB[:, 0], rsB[:, 0], "moe0_norm")
                dve.wait_ge(sem["moe0_norm"], count("moe0_norm", b, 11))
                dve.tensor_tensor(ng[:], n0[:], Gam0[:, None, :].broadcast_to([P, TT, D]), ALU.mult).then_inc(sem["moe0_norm"], 1)
                dve.wait_ge(sem["moe0_norm"], count("moe0_norm", b, 12))
                dve.wait_ge(sem["xbet_done"], count("xbet_done", b, 1))
                dve.tensor_tensor(yB[:], ng[:], xbet[:], ALU.add).then_inc(sem["moe0_norm"], 1)
                dve.wait_ge(sem["moe0_norm"], count("moe0_norm", b, 13))
                statistics(b, "moe0_norm", 13, yB, statB[:, 1], mvB[:, 1], LN_EPS)

            def moe0_end(b):
                dve.wait_ge(sem["moe0_power"], count("moe0_power", b, 2))
                dve.wait_ge(sem["xob_done"], count("xob_done", b - 1, 1))
                dve.wait_ge(sem["x2T_psum"], count("x2T_psum", b - 1, 1))
                normalize(x2, yB, mvB[:, 1], rsB[:, 1], "x2_done")

            def lin_features(b):
                dve.wait_ge(sem["q1_psum"], count("q1_psum", b, 1))
                dve.wait_ge(sem["q1_exp"], count("q1_exp", b - 1, 1))
                dve.tensor_scalar(uq, MI[:, 0:T], Bq1, 0.0, ALU.add, ALU.min).then_inc(sem["q1_min"], 1)
                for tt in range(TT):
                    dve.wait_ge(sem["kvg_psum"], count("kvg_psum", b, tt + 1))
                    if tt == 0:
                        dve.wait_ge(sem["kv_psum"], count("kv_psum", b - 1, 1))
                        dve.wait_ge(sem["kg_exp"], count("kg_exp", b - 1, 2))
                    dve.tensor_tensor(KVG[:, tt, 0:3 * D], Z[tt][:, 0:3 * D], Bkvg, ALU.add).then_inc(sem["kvg_done"], 1)
                dve.wait_ge(sem["kvg_done"], count("kvg_done", b, TT))
                dve.tensor_scalar(uk[:], KVG[:, :, D:2 * D], 0.0, None, ALU.min).then_inc(sem["k1_min"], 1)
                dve.wait_ge(sem["q1_exp"], count("q1_exp", b, 2))
                dve.wait_ge(sem["lin_psum"], count("lin_psum", b - 1, 1))
                dve.tensor_tensor(qf[:], pq[:], eq[:], ALU.add).then_inc(sem["q1_done"], 1)

            def lin_keys(b):
                dve.wait_ge(sem["kg_exp"], count("kg_exp", b, 1))
                dve.scalar_tensor_tensor(out=kf[:], in0=KVG[:, :, D:2 * D], scalar=0.0, in1=ek[:],
                                         op0=ALU.max, op1=ALU.add).then_inc(sem["k1_done"], 1)
                dve.wait_ge(sem["kg_exp"], count("kg_exp", b, 2))
                dve.tensor_scalar(both(sg[:]), both(eg[:]), 1.0, None, ALU.add).then_inc(sem["gate1_done"], 1)
                dve.wait_ge(sem["gate1_done"], count("gate1_done", b, 1))
                dve.reciprocal(both(sg[:]), both(sg[:])).then_inc(sem["gate1_done"], 1)

            def lin_blocks(b):
                dve.wait_ge(sem["kv_psum"], count("kv_psum", b, 1))
                dve.wait_ge(sem["lin_psum"], count("lin_psum", b - 1, 1))
                dve.tensor_tensor(BD[:, 0:D], MI[:, 0:D], bmask, ALU.mult).then_inc(sem["kv_blocks"], 1)
                dve.tensor_scalar(BD[:, D:2 * D], bmask, MI[:, D:D + 1], None, ALU.mult).then_inc(sem["kv_blocks"], 1)

            def lin_gate(b):
                dve.wait_ge(sem["lin_psum"], count("lin_psum", b, 1))
                mi = MI[:].rearrange("p (a c) -> p a c", a=TT)
                dve.tensor_scalar(den[:], mi[:, :, D:2 * D], 1e-6, None, ALU.add).then_inc(sem["lin_gated"], 1)
                dve.wait_ge(sem["lin_gated"], count("lin_gated", b, 1))
                dve.reciprocal(both(rden[:]), both(den[:])).then_inc(sem["lin_gated"], 1)
                dve.wait_ge(sem["lin_gated"], count("lin_gated", b, 2))
                dve.wait_ge(sem["gate1_done"], count("gate1_done", b, 2))
                dve.tensor_tensor(both(den[:]), both(rden[:]), both(sg[:]), ALU.mult).then_inc(sem["lin_gated"], 1)
                dve.wait_ge(sem["lin_gated"], count("lin_gated", b, 3))
                dve.wait_ge(sem["linT_psum"], count("linT_psum", b - 1, 1))
                dve.tensor_tensor(go[:], mi[:, :, 0:D], den[:], ALU.mult).then_inc(sem["lin_gated"], 1)

            def lin_norm(b):
                dve.wait_ge(sem["linout_psum"], count("linout_psum", b, 1))
                dve.wait_ge(sem["xob_done"], count("xob_done", b, 1))
                dve.tensor_tensor(both(yC[:]), MI[:, T:2 * T], both(xob[:]), ALU.add).then_inc(sem["lin_norm"], 1)
                dve.wait_ge(sem["lin_norm"], count("lin_norm", b, 1))
                statistics(b, "lin_norm", 1, yC, statC, mvC, LN_EPS)
                dve.wait_ge(sem["lin_power"], count("lin_power", b, 1))
                dve.wait_ge(sem["xbe_done"], count("xbe_done", b - 1, TT))
                dve.wait_ge(sem["x3T_psum"], count("x3T_psum", b - 1, 1))
                normalize(x3, yC, mvC, rsC, "x3_done")

            def router1(b):
                dve.wait_ge(sem["x3T_high"], count("x3T_high", b, 2))
                dve.wait_ge(sem["hid1_psum"], count("hid1_psum", b - 1, EXPERTS))
                dve.tensor_tensor(x3L[:], MI[:, 0:T], x3H[:].bitcast(F32), ALU.subtract).then_inc(sem["x3T_low"], 1)
                pick_two(b, "gate1_psum", MI, None, lg1, top1, ix1, ixf1, "pick1")
                dve.tensor_tensor(dl1[:], top1[:, :, 1:2], top1[:, :, 0:1], ALU.subtract).then_inc(sem["pick1"], 1)
                dve.wait_ge(sem["pick1"], count("pick1", b, 5))
                dve.tensor_copy(both(ixf1[:]), both(ix1[:])).then_inc(sem["pick1"], 1)
                dve.wait_ge(sem["pick1_exp"], count("pick1_exp", b, 1))
                dve.tensor_scalar(s1[:], e1[:], 1.0, None, ALU.add).then_inc(sem["weight1"], 1)
                dve.wait_ge(sem["weight1"], count("weight1", b, 1))
                dve.reciprocal(w1[:, :, 0:1], s1[:]).then_inc(sem["weight1"], 1)
                dve.wait_ge(sem["weight1"], count("weight1", b, 2))
                dve.tensor_tensor(w1[:, :, 1:2], e1[:], w1[:, :, 0:1], ALU.mult).then_inc(sem["weight1"], 1)
                dve.wait_ge(sem["weight1"], count("weight1", b, 3))
                dve.wait_ge(sem["pick1"], count("pick1", b, 7))
                for r in range(2):
                    for tt in range(TT):
                        dve.tensor_scalar(ohw[:, r, tt], iota, ixf1[:, tt, r:r + 1], w1[:, tt, r:r + 1],
                                          ALU.is_equal, ALU.mult).then_inc(sem["weight1"], 1)
                dve.wait_ge(sem["weight1"], count("weight1", b, 7))
                dve.wait_ge(sem["weightsT_psum"], count("weightsT_psum", b - 1, 1))
                dve.tensor_tensor(wE[:], ohw[:, 0], ohw[:, 1], ALU.add).then_inc(sem["weights_done"], 1)

            def gelu_low(b, e):
                dve.wait_ge(sem["hid1_high"], count("hid1_high", b, e + 1))
                if e >= HRING:
                    dve.wait_ge(sem["out1_psum"], count("out1_psum", b, e - HRING + 1))
                else:
                    dve.wait_ge(sem["out0_psum"], count("out0_psum", b, 2 * EXPERTS - HRING + e + 1))
                dve.tensor_tensor(hL[:, e % HRING], gf[:, e % GRING], hH[:, e % HRING].bitcast(F32),
                                  ALU.subtract).then_inc(sem["hid1_low_even"], 1)

            def expert_sums(b, half):
                dve.wait_ge(sem["out1_psum"], count("out1_psum", b, 4 * half + 4))
                dve.wait_ge(sem["xbe_done"], count("xbe_done", b, TT))
                dve.wait_ge(sem["expert_total"], count("expert_total", b - 1, TT))
                for tt in range(TT):
                    dve.tensor_tensor(V[:, tt, 4 * half:4 * half + 4],
                                      (SA, SB)[tt][half][:].rearrange("p (e d) -> p e d", e=4),
                                      V[:, tt, 4 * half:4 * half + 4], ALU.add).then_inc(sem["expert_sum"], 1)

            def expert_stats(b, k):
                dve.wait_ge(sem["expert_sum"], count("expert_sum", b, 2 if k < 4 else 4))
                for tt in range(TT):
                    dve.bn_stats(statD[:, tt * EXPERTS + k], V[:, tt, k]).then_inc(sem["expert_norm"], 1)

            def expert_scales(b):
                dve.wait_ge(sem["expert_norm"], count("expert_norm", b, 16))
                me, mo, ve, vo = (statD[:, :, k] for k in (1, 4, 2, 5))
                dve.tensor_tensor(smD[:], me, mo, ALU.add).then_inc(sem["expert_norm"], 1)
                dve.tensor_tensor(dfD[:], me, mo, ALU.subtract).then_inc(sem["expert_norm"], 1)
                dve.scalar_tensor_tensor(out=qdD[:], in0=ve, scalar=D * LN_EPS_EXPERT, in1=vo, op0=ALU.add,
                                         op1=ALU.add).then_inc(sem["expert_norm"], 1)
                dve.wait_ge(sem["expert_norm"], count("expert_norm", b, 19))
                dve.scalar_tensor_tensor(out=ddD[:], in0=dfD[:], scalar=0.25, in1=dfD[:], op0=ALU.mult,
                                         op1=ALU.mult).then_inc(sem["expert_norm"], 1)
                dve.wait_ge(sem["expert_norm"], count("expert_norm", b, 20))
                dve.scalar_tensor_tensor(out=vrD[:], in0=qdD[:], scalar=1.0 / D, in1=ddD[:], op0=ALU.mult,
                                         op1=ALU.add).then_inc(sem["expert_norm"], 1)

            def expert_scales_end(b):
                dve.wait_ge(sem["expert_power"], count("expert_power", b, 1))
                dve.wait_ge(sem["weights_done"], count("weights_done", b, 1))
                dve.tensor_tensor(aD[:], rsD[:], both(wE[:]), ALU.mult).then_inc(sem["expert_norm"], 1)
                dve.wait_ge(sem["expert_norm"], count("expert_norm", b, 22))
                dve.scalar_tensor_tensor(out=cD[:], in0=smD[:], scalar=-0.5, in1=aD[:], op0=ALU.mult,
                                         op1=ALU.mult).then_inc(sem["expert_norm"], 1)

            def expert_totals(b):
                for tt in range(TT):
                    dve.wait_ge(sem["expert_gamma"], count("expert_gamma", b, tt + 1))
                    dve.tensor_reduce(rdD[:, tt], V[:, tt].rearrange("p e d -> p d e"), AX_X, ALU.add).then_inc(sem["expert_total"], 1)

            def last_stats(b):
                dve.wait_ge(sem["beta_psum"], count("beta_psum", b, 1))
                dve.tensor_tensor(both(zD[:]), MI[:, 0:TT * D], both(x3[:]), ALU.add).then_inc(sem["last_norm"], 1)

            def last_stats_end(b):
                dve.wait_ge(sem["last_norm"], count("last_norm", b, 1))
                dve.wait_ge(sem["expert_total"], count("expert_total", b, TT))
                dve.tensor_tensor(both(yD[:]), both(zD[:]), both(rdD[:]), ALU.add).then_inc(sem["last_norm"], 1)
                dve.wait_ge(sem["last_norm"], count("last_norm", b, 2))
                statistics(b, "last_norm", 2, yD, statE, mvE, LN_EPS)

            def last_norm(b):
                dve.wait_ge(sem["last_power"], count("last_power", b, 1))
                dve.wait_ge(sem["stored"], count("stored", b - 1, 16))
                normalize(res, yD, mvE, rsE, "res_done")

            def tail(m0, nx):
                if nx is not None:
                    attn_divide(nx)
                if m0 is not None:
                    moe0_stats(m0)
                if nx is not None:
                    attn_stats(nx)
                if m0 is not None:
                    moe0_norm(m0)
                if nx is not None:
                    attn_norm(nx)
                if m0 is not None:
                    moe0_end(m0)
                    lin_features(m0)
                if nx is not None:
                    x1_low(nx)
                if m0 is not None:
                    lin_keys(m0)
                    lin_blocks(m0)
                if nx is not None:
                    router0_pick(nx)
                if m0 is not None:
                    lin_gate(m0)
                if nx is not None:
                    router0_values(nx)
                if m0 is not None:
                    lin_norm(m0)
                    router1(m0)

            def turn(m1, m0, nx):
                if m1 is not None:
                    for e in range(EXPERTS):
                        if e == 1 and nx is not None:
                            qk_low(nx)
                        if e % 2 == 0:
                            gelu_low(m1, e)
                        if e == 5:
                            expert_sums(m1, 0)
                        if e >= 6:
                            expert_stats(m1, 2 * (e - 6))
                            expert_stats(m1, 2 * (e - 6) + 1)
                    last_stats(m1)
                    expert_sums(m1, 1)
                elif nx is not None:
                    qk_low(nx)
                for e in range(EXPERTS):
                    if m0 is not None:
                        relu_low(m0, e)
                    if nx is not None:
                        maximum(nx, 2 * e)
                        maximum(nx, 2 * e + 1)
                    if m1 is not None:
                        if e < 4:
                            expert_stats(m1, 4 + e)
                        if e == 4:
                            expert_scales(m1)
                        if e == 7:
                            expert_scales_end(m1)
                if nx is not None:
                    negmax(nx)
                if m0 is not None:
                    boost(m0)
                if nx is not None:
                    shift(nx)
                for e in range(EXPERTS):
                    if m0 is not None:
                        relu_low(m0, EXPERTS + e)
                if m1 is not None:
                    expert_totals(m1)
                    last_stats_end(m1)
                    last_norm(m1)
                tail(m0, nx)

            dve.wait_ge(sem["near_consts"], 32)
            dve.wait_ge(sem["filled"], 2)
            qk_low(0)
            dve.wait_ge(sem["consts"], 16 * 2)
            dve.wait_ge(sem["info_high"], 1)
            dve.scalar_tensor_tensor(out=infoW[:], in0=infoW[:].bitcast(F32), scalar=lowr, in1=infoRaw,
                                     op0=ALU.mult, op1=ALU.add).then_inc(sem["info_split"], 1)
            for h in range(HEADS):
                maximum(0, h)
            dve.wait_ge(sem["filled"], 6)
            negmax(0)
            shift(0)
            tail(None, 0)
            turn(None, 0, 1)
            turn(0, 1, 2)
            with dve.Fori(2, SEQS - 1) as b:
                turn(b - 1, b, b + 1)
            turn(SEQS - 2, SEQS - 1, None)
            turn(SEQS - 1, None, None)


def kernel(**inputs):
    import numpy as np
    import concourse.bacc as bacc
    from concourse.bass_utils import run_bass_kernel_spmd

    a = {k: np.asarray(v) for k, v in inputs.items()}
    x = a["L0_attn_x"]

    order = np.arange(D).reshape(G, QD, DH).transpose(1, 2, 0).reshape(-1)
    wqkv, bqkv = a["L0_attn_W_qkv"], a["L0_attn_b_qkv"]

    def side_by_side(names, blocks):
        packed = np.zeros((P, sum(n for _, n in names)), np.float32)
        at = 0
        for name, n in names:
            packed[:blocks[name].shape[0], at:at + n] = blocks[name]
            at += n
        return packed

    lowrows = np.zeros((INFO, 1), np.float32)
    lowrows[17] = -1.0
    lowrows[24:] = -1.0
    heads = np.arange(D) // DH
    blocks = {
        "wqk": np.concatenate([wqkv[0:D].T[:, order], wqkv[D:2 * D].T[:, order]], 1),
        "bqk": np.stack([bqkv[0:D][order], bqkv[D:2 * D][order]], 1),
        "wv": wqkv[2 * D:].T, "ident": np.eye(P, dtype=np.float32),
        "wo": a["L0_attn_W_out"].T, "g0w": a["L0_ffn_gate_W"],
        "iota": np.tile(np.arange(EXPERTS, dtype=np.float32), (P, 1)),
        "blockmask": (heads[:, None] == heads[None, :]).astype(np.float32),
        "wq1": a["L1_attn_wq_w"], "bq1": a["L1_attn_wq_b"][:, None],
        "wkvg": np.concatenate([a["L1_attn_wg_w"], a["L1_attn_wk_w"], a["L1_attn_wv_w"]], 1),
        "wout": a["L1_attn_out_w"], "g1w": a["L1_ffn_gate_w"],
        "b1b": a["L1_ffn_b1"].reshape(EXPERTS, HH, P).transpose(2, 0, 1).reshape(P, -1),
        "lowrows": lowrows,
    }
    rows = {
        "bv": bqkv[2 * D:], "bo": a["L0_attn_b_out"], "g0b": a["L0_ffn_gate_b"],
        "gam0": a["L0_ffn_ln_gamma"], "bet0": a["L0_ffn_ln_beta"],
        "bkvg": np.concatenate([a["L1_attn_wg_b"], a["L1_attn_wk_b"], a["L1_attn_wv_b"]]),
        "bout": a["L1_attn_out_b"], "b2b": a["L1_ffn_b2"].reshape(-1), "lng": a["L1_ffn_ln_g"].reshape(-1),
    }
    info = np.zeros((INFO, NINF), np.float32)
    info[0:EXPERTS, EXPERTS * HID:] = a["L0_ffn_b2"]
    info[INFO - EXPERTS:, EXPERTS * HID:] = a["L0_ffn_b2"]
    for e in range(EXPERTS):
        info[EXPERTS + e, e * HID:(e + 1) * HID] = BIG
    info[16, 0:EXPERTS * HID] = a["L0_ffn_b1"].reshape(-1)
    info[17, 0:EXPERTS * HID] = a["L0_ffn_b1"].reshape(-1)

    def by_input(w):
        return w.transpose(1, 0, 2).reshape(D, -1)

    def by_hidden(w):
        return w.reshape(EXPERTS, HH, P, D).transpose(2, 0, 1, 3).reshape(P, -1)

    sent = {
        "xT": x.transpose(0, 2, 1), "xtok": x.reshape(SEQS, TT, P, D).transpose(0, 2, 1, 3),
        "pack_a": side_by_side(PACK_A, blocks), "pack_b": side_by_side(PACK_B, blocks),
        "row_a": np.concatenate([rows[n] for n, _ in ROW_A]),
        "row_b": np.concatenate([rows[n] for n, _ in ROW_B]),
        "lnb": a["L1_ffn_ln_b"], "info": info,
        "w1a": by_input(a["L0_ffn_W1"]), "w2a": by_hidden(a["L0_ffn_W2"]),
        "w1b": by_input(a["L1_ffn_w1"]), "w2b": by_hidden(a["L1_ffn_w2"]),
    }
    nc = bacc.Bacc("TRN2", target_bir_lowering=False, num_devices=1)
    arrays, args = {}, []
    for name, value in sent.items():
        value = np.ascontiguousarray(value)
        arrays[f"in_{name}"] = value
        args.append(nc.dram_tensor(f"in_{name}", value.shape, mybir.dt.from_np(value.dtype),
                                   kind="ExternalInput").ap())
    args.append(nc.dram_tensor("out_0", (SEQS, P, TT, D), F32, kind="ExternalOutput").ap())
    build(nc, *args)
    r = run_bass_kernel_spmd(nc, [arrays], core_ids=[0])
    got = r.results[0]["out_0"]
    return got.transpose(0, 2, 1, 3).reshape(SEQS, T, D)
```

```python
from contextlib import ExitStack

import concourse.bass as bass
from concourse import mybir

F32 = mybir.dt.float32
F32R = mybir.dt.float32r
U32 = mybir.dt.uint32
ALU = mybir.AluOpType
ACT = mybir.ActivationFunctionType
AX_X = mybir.AxisListType.X

P = 128
D = 128
HEADS = 16
DH = D // HEADS
EXPERTS = 8
HID = 256
PAIRS = EXPERTS // 2
HH = HID // P
SEQS = 8
T = 256
TT = T // P
G = 4
QD = 4
PIECES = 4
SCALE = 1.0 / float(DH) ** 0.5
BIG = 1.0e30
INFO = 32
LN_EPS = 1e-5
LN_EPS_EXPERT = 1e-6


NINF = EXPERTS * HID + D
PACK_A = [("wqk", 2 * D), ("bqk", 2), ("wv", D), ("ident", P)]
PACK_B = [("wo", D), ("g0w", EXPERTS), ("iota", EXPERTS), ("blockmask", P), ("wq1", D), ("bq1", 1),
          ("wkvg", 3 * D), ("wout", D), ("g1w", EXPERTS), ("b1b", EXPERTS * HH), ("b2t", EXPERTS), ("lowrows", 1)]
ROW_A = [("bv", D)]
ROW_B = [("bo", D), ("g0b", EXPERTS), ("gam0", D), ("bet0", D), ("bkvg", 3 * D), ("bout", D),
         ("lng", EXPERTS * D)]


def build(nc, xT, xtok, pack_a, pack_b, row_a, row_b, lnb, info, w1a, w2a, w1b, w2b, out):
    with ExitStack() as ctx:
        def sb(name, shape, dt=F32):
            return ctx.enter_context(nc.sbuf_tensor(name, shape, dt))

        def bank(name):
            return ctx.enter_context(nc.psum_tensor(name, [P, 512], F32))

        packA = sb("packA", [P, sum(n for _, n in PACK_A)])
        packB = sb("packB", [P, sum(n for _, n in PACK_B)])
        rowA = sb("rowA", [P, sum(n for _, n in ROW_A)])
        rowB = sb("rowB", [P, sum(n for _, n in ROW_B)])
        part = {}
        for tile, names in ((packA, PACK_A), (packB, PACK_B), (rowA, ROW_A), (rowB, ROW_B)):
            at = 0
            for name, n in names:
                part[name] = tile[:, at:at + n]
                at += n
        idn, bmask, iota, lowr = part["ident"], part["blockmask"], part["iota"], part["lowrows"][0:INFO, :]
        Wqk = part["wqk"].rearrange("p (a d) -> p a d", a=2)
        Bqk, Wv, Wo, G0w, Wq1, Bq1 = (part[k] for k in ("bqk", "wv", "wo", "g0w", "wq1", "bq1"))
        Wkvg, Wout, G1w, B2t = part["wkvg"], part["wout"], part["g1w"], part["b2t"]
        B1b = part["b1b"].rearrange("p (e h) -> p e h", e=EXPERTS)
        Bv, Bo, G0b, Gam0, Bet0, Bkvg, Bout = (
            part[k] for k in ("bv", "bo", "g0b", "gam0", "bet0", "bkvg", "bout"))
        Lng = part["lng"].rearrange("p (e d) -> p e d", e=EXPERTS)
        Lnb = sb("Lnb", [EXPERTS, D])
        W1H = [sb(f"W1H{n}", [P, EXPERTS, HID], F32R) for n in range(2)]
        W1L = [sb(f"W1L{n}", [P, EXPERTS, HID], F32R) for n in range(2)]
        W2H = [sb(f"W2H{n}", [P, EXPERTS, HH, D], F32R) for n in range(2)]
        W2L = [sb(f"W2L{n}", [P, EXPERTS, HH, D], F32R) for n in range(2)]
        infoW = sb("infoW", [INFO, NINF], F32R)
        mhalf = sb("mhalf", [P, TT * EXPERTS])

        den = sb("den", [P, TT, D])
        xTs = sb("xTs", [P, T])
        xto = sb("xto", [P, TT, D])
        xb = sb("xb", [P, TT, D])
        qkH = sb("qkH", [P, 2, T], F32R)
        qkL = sb("qkL", [P, 2, T], F32R)
        Qs = sb("Qs", [P, G, T], F32R)
        Km = sb("Km", [P, QD, G, T], F32R)
        Vst = sb("Vst", [P, TT, HEADS, 32])
        mx = sb("mx", [P, G, QD, TT])
        nmH = sb("nmH", [P, G, QD, TT], F32R)
        Mx = sb("Mx", [P, G, TT, P])
        PRING = 8
        Pt = sb("Pt", [P, PRING, TT * T])
        rec = sb("rec", [P, TT, HEADS])
        x1 = sb("x1", [P, TT, D])
        statA = sb("statA", [P, TT, 6])
        mvA = sb("mvA", [P, TT, 2])
        rsA = sb("rsA", [P, TT])
        x1f = sb("x1f", [P, T])
        x1H = sb("x1H", [P, T], F32R)
        x1L = sb("x1L", [P, T], F32R)
        lg0 = sb("lg0", [P, TT, EXPERTS])
        top0 = sb("top0", [P, TT, EXPERTS])
        ix0 = sb("ix0", [P, TT, EXPERTS], U32)
        ixf0 = sb("ixf0", [P, TT, EXPERTS])
        dl0 = sb("dl0", [P, TT, EXPERTS])
        e0 = sb("e0", [P, TT, EXPERTS])
        s0 = sb("s0", [P, TT])
        r0 = sb("r0", [P, TT])
        val0 = sb("val0", [P, TT, 2])
        route = sb("route", [P, TT, 2, INFO])
        rm = sb("rm", [INFO, 2, T], F32R)

        HRING = 4
        hH = sb("hH", [P, HRING, HH * T], F32R)
        hL = sb("hL", [P, HRING, HH * T], F32R)
        x2f = sb("x2f", [P, T])
        x2H = sb("x2H", [P, T], F32R)
        x2L = sb("x2L", [P, T], F32R)
        eo = sb("eo", [P, 2, T])
        f0 = sb("f0", [P, TT, D])
        f1 = sb("f1", [P, TT, D])
        n0 = sb("n0", [P, TT, D])
        ng = sb("ng", [P, TT, D])
        xbet = sb("xbet", [P, TT, D])
        x2 = sb("x2", [P, TT, D])
        statB = sb("statB", [P, 2, TT, 6])
        mvB = sb("mvB", [P, 2, TT, 2])
        rsB = sb("rsB", [P, 2, TT])

        xcf = sb("xcf", [P, T])
        eq = sb("eq", [P, T])
        pq = sb("pq", [P, T])
        qf = sb("qf", [P, T])
        KVG = sb("KVG", [P, TT, 3 * D + 2])
        kf = sb("kf", [P, TT, D])
        den1 = sb("den1", [P, TT, HEADS])
        BD = sb("BD", [P, D + HEADS])
        xob = sb("xob", [P, TT, D])
        x3 = sb("x3", [P, TT, D])
        statC = sb("statC", [P, TT, 6])
        mvC = sb("mvC", [P, TT, 2])
        rsC = sb("rsC", [P, TT])
        x3H = sb("x3H", [P, T], F32R)
        x3L = sb("x3L", [P, T], F32R)
        lg1 = sb("lg1", [P, TT, EXPERTS])
        top1 = sb("top1", [P, TT, EXPERTS])
        ix1 = sb("ix1", [P, TT, EXPERTS], U32)
        ixf1 = sb("ixf1", [P, TT, EXPERTS])
        dl1 = sb("dl1", [P, TT, 1])
        e1 = sb("e1", [P, TT, 1])
        s1 = sb("s1", [P, TT, 1])
        w1 = sb("w1", [P, TT, 2])
        ohw = sb("ohw", [P, 2, TT, EXPERTS])
        wE = sb("wE", [P, TT, EXPERTS])
        wET = sb("wET", [EXPERTS, T])

        GRING = 2
        gf = sb("gf", [P, GRING, HH * T])
        oT1 = sb("oT1", [P, 2, 2 * T])
        V = sb("V", [P, TT, EXPERTS, D])
        statD = sb("statD", [P, TT * EXPERTS, 6])
        smD = sb("smD", [P, TT * EXPERTS])
        dfD = sb("dfD", [P, TT * EXPERTS])
        qdD = sb("qdD", [P, TT * EXPERTS])
        ddD = sb("ddD", [P, TT * EXPERTS])
        vrD = sb("vrD", [P, TT * EXPERTS])
        rsD = sb("rsD", [P, TT * EXPERTS])
        aD = sb("aD", [P, TT * EXPERTS])
        cD = sb("cD", [P, TT * EXPERTS])
        zD = sb("zD", [P, TT, D])
        res = sb("res", [P, TT, D])
        statE = sb("statE", [P, TT, 6])
        mvE = sb("mvE", [P, TT, 2])
        rsE = sb("rsE", [P, TT])

        rawW = V[:].rearrange("p t e d -> p (t e d)")
        infoRaw = Pt[0:INFO].rearrange("p r n -> p (r n)")[:, 0:NINF]
        yA, yB, yC, yD = xb, xbet, xob, zD
        uk, ek, eg, sg = f0, f1, n0, ng
        go, gnum = f0, f1
        gT, x3f = xcf, eq
        Ot = gf[:].rearrange("p a (b t) -> p (a b) t", b=2)
        AoT, rdD, Ao, uq = x2f, den, ng, eo[:, 1]

        HIGH = [W1H[0][:], W2H[0][:], W1H[1][:], W2H[1][:]]
        LOW = [W1L[0][:], W2L[0][:], W1L[1][:], W2L[1][:]]
        for weights in (HIGH, LOW):
            for k in range(4):
                weights[k] = weights[k].rearrange("p a b -> p (a b)" if k % 2 == 0 else "p a b c -> p (a b c)")

        SA = [bank(f"SA{n}") for n in range(2)]
        SB = [bank(f"SB{n}") for n in range(2)]
        PA = bank("PA")
        Z = [bank(f"Z{n}") for n in range(2)]
        MI = bank("MI")

        stacks = nc.dram_tensor("stacks", [2, QD, PIECES, 32, T], F32)
        q_stack, k_stack = stacks[0], stacks[1]

        sem, per_sequence = {}, {}
        for name, per in (
                ("near_consts", 0), ("consts", 0), ("info_in", 0), ("raw_in", 0), ("raw_high", 0), ("raw_split", 0),
                ("cleared", 0), ("held", 0), ("filled", 0), ("stack_filled", 0), ("info_high", 0), ("info_split", 0),
                ("x_in", 32), ("qk_psum", 1), ("v_psum", 1), ("qk_high", 2), ("qk_low", 2), ("v_done", 2),
                ("stack_out", 16 * 6), ("stack_in", 16 * (1 + QD)), ("xb_done", 1),
                ("max_psum", HEADS), ("max_done", HEADS), ("negmax", 3), ("negmax_psum", 2),
                ("q_shifted", 2), ("exp_psum", HEADS), ("exp_done", HEADS), ("pv_psum", G),
                ("o_copied", 2), ("o_psum", TT), ("o_inverse", TT), ("o_done", TT), ("oT_psum", 1),
                ("oT_done", 1), ("attn_psum", 1), ("attn_norm", 6), ("attn_power", 1), ("x1_done", TT),
                ("x1T_psum", 1), ("x1T_high", 2), ("x1T_low", 1), ("gate0_psum", 1), ("pick0", 13),
                ("gate0_exp", 1), ("value0", 3), ("route_psum", 1), ("route_done", 1),
                ("hid0_psum", 2 * EXPERTS), ("hid0_high", 2 * EXPERTS), ("hid0_low", 2 * EXPERTS - EXPERTS // 2), ("hid0_low_pool", EXPERTS // 2), ("hid0_relu", EXPERTS // 2),
                ("out0_psum", 2 * EXPERTS), ("out0_copied", 2), ("boosted", 3), ("out0T_psum", 1),
                ("moe0_norm", 18), ("moe0_power", 2), ("xbet_done", 1), ("x2_done", TT),
                ("x2T_psum", 1), ("x2T_done", 1), ("q1_psum", 1), ("kvg_psum", TT), ("q1_min", 1),
                ("q1_exp", 2), ("q1_done", 1), ("kvg_done", TT), ("k1_min", 1), ("kg_exp", 2),
                ("k1_done", 1), ("gate1_done", 2), ("kv_psum", 1), ("kv_blocks", 2), ("lin_psum", 1),
                ("lin_gated", 5), ("linT_psum", 1), ("linT_done", 1), ("xob_done", 1),
                ("linout_psum", 1), ("lin_norm", 6), ("lin_power", 1), ("x3_done", TT),
                ("x3T_psum", 1), ("x3T_high", 2), ("x3T_low", 1), ("gate1_psum", 1), ("pick1", 7),
                ("pick1_exp", 1), ("weight1", 7), ("weights_done", 1), ("weightsT_psum", 1),
                ("weightsT_done", 1),
                ("hid1_psum", EXPERTS), ("hid1_gelu", 2 * EXPERTS), ("hid1_high", EXPERTS),
                ("hid1_low_even", EXPERTS // 2), ("hid1_low_odd", EXPERTS // 2), ("out1_psum", EXPERTS),
                ("out1_copied", EXPERTS), ("out1T_psum", PAIRS), ("expert_sum", 2 * PAIRS), ("expert_norm", 23), ("expert_power", 1),
                ("expert_scaled", TT * EXPERTS), ("expert_gamma", TT), ("beta_psum", 1),
                ("expert_total", TT), ("last_norm", 7), ("last_power", 1), ("res_done", TT),
                ("stored", 16)):
            sem[name] = ctx.enter_context(nc.semaphore(name))
            per_sequence[name] = per

        def count(name, b, step):
            value = b * per_sequence[name] + step
            return max(value, 0) if isinstance(value, int) else value

        def has(b):
            return not isinstance(b, int) or 0 <= b < SEQS

        def only(t, turn):
            return isinstance(t, int) and t == turn

        def by_pool(n):
            return n < EXPERTS and n % 2 == 1

        def low0(n):
            if by_pool(n):
                return "hid0_low_pool", n // 2 + 1
            return "hid0_low", n // 2 + 1 if n < EXPERTS else n + 1 - EXPERTS // 2

        def both(t):
            return t.rearrange("p a b -> p (a b)")

        block = ctx.enter_context(nc.Block())

        @block.sync
        def _(sp):
            def load_x(b):
                sp.wait_ge(sem["qk_psum"], count("qk_psum", b - 1, 1))
                sp.wait_ge(sem["v_psum"], count("v_psum", b - 1, 1))
                sp.wait_ge(sem["xb_done"], count("xb_done", b - 1, 1))
                sp.dma_start(xTs[:], xT[b]).then_inc(sem["x_in"], 16)
                sp.dma_start(xto[:], xtok[b]).then_inc(sem["x_in"], 16)

            def stack(b):
                sp.wait_ge(sem["stack_in"], count("stack_in", b - 1, 16 * (1 + QD)))
                sp.wait_ge(sem["qk_high"], count("qk_high", b, 2))
                for r in (0, 2):
                    sp.dma_start(q_stack[:, r], qkH[:, 0].bitcast(F32)).then_inc(sem["stack_out"], 16)
                for r in (0, 1):
                    sp.dma_start(k_stack[:, r], qkH[:, 1].bitcast(F32)).then_inc(sem["stack_out"], 16)
                sp.wait_ge(sem["qk_low"], count("qk_low", b, 2))
                sp.dma_start(q_stack[:, 1], qkL[:, 0].bitcast(F32)).then_inc(sem["stack_out"], 16)
                sp.dma_start(k_stack[:, 2], qkL[:, 1].bitcast(F32)).then_inc(sem["stack_out"], 16)
                sp.wait_ge(sem["stack_out"], count("stack_out", b, 16 * 6))
                sp.wait_ge(sem["exp_psum"], count("exp_psum", b - 1, HEADS))
                sp.dma_start(Qs[:].rearrange("p g t -> p (g t)").bitcast(F32),
                             q_stack.rearrange("i r (d g) t -> (i r d) (g t)", g=G)).then_inc(sem["stack_in"], 16)
                for i in range(QD):
                    sp.dma_start(Km[32 * i:32 * i + 32, i].rearrange("p g t -> p (g t)").bitcast(F32),
                                 k_stack[i].rearrange("r (d g) t -> (r d) (g t)", g=G)).then_inc(sem["stack_in"], 16)

            def store(b):
                sp.wait_ge(sem["res_done"], count("res_done", b, TT))
                sp.dma_start(out[b], res[:]).then_inc(sem["stored"], 16)

            sp.dma_start(packA[:], pack_a).then_inc(sem["near_consts"], 16)
            load_x(0)
            sp.dma_start(rowA[:], row_a[None, :].broadcast_to([P, row_a.shape[0]])).then_inc(sem["near_consts"], 16)
            sp.dma_start(packB[:], pack_b).then_inc(sem["consts"], 16)
            sp.dma_start(rowB[:], row_b[None, :].broadcast_to([P, row_b.shape[0]])).then_inc(sem["consts"], 16)
            sp.dma_start(infoRaw, info).then_inc(sem["info_in"], 16)
            sp.dma_start(rawW, w1a).then_inc(sem["raw_in"], 16)
            sp.wait_ge(sem["filled"], 1)
            for i in range(QD):
                sp.dma_start(q_stack[i, PIECES - 1].rearrange("(a b) t -> a (b t)", a=8),
                             Km[0:8, QD - 1].rearrange("p g t -> p (g t)").bitcast(F32)).then_inc(sem["stack_filled"], 16)
                sp.dma_start(k_stack[i, PIECES - 1].rearrange("(a b) t -> a (b t)", a=8),
                             Mx[0:8].rearrange("p g a b -> p (g a b)")).then_inc(sem["stack_filled"], 16)
            sp.wait_ge(sem["stack_filled"], 16 * 2 * QD)
            stack(0)
            load_x(1)
            for n, source in enumerate((w2a, w1b)):
                sp.wait_ge(sem["raw_split"], n + 1)
                sp.dma_start(rawW, source).then_inc(sem["raw_in"], 16)
            stack(1)
            load_x(2)
            sp.wait_ge(sem["raw_split"], 3)
            sp.dma_start(rawW, w2b).then_inc(sem["raw_in"], 16)
            sp.dma_start(Lnb[:], lnb).then_inc(sem["raw_in"], 16)
            stack(2)
            load_x(3)
            stack(3)
            with sp.Fori(2, SEQS - 2) as t:
                load_x(t + 2)
                store(t - 2)
                stack(t + 2)
            for b in range(SEQS - 4, SEQS):
                store(b)
            sp.wait_ge(sem["stored"], 16 * SEQS)

        @block.gpsimd
        def _(pool):
            pool.memset(Mx[:].rearrange("p g a b -> p (g a b)"), 1.0).then_inc(sem["cleared"], 1)
            pool.wait_ge(sem["cleared"], 1)
            pool.memset(Km[:].rearrange("p i g t -> p (i g t)").bitcast(F32), 0.0).then_inc(sem["filled"], 1)
            pool.memset(Vst[:].rearrange("p a b c -> p (a b c)"), 0.0).then_inc(sem["cleared"], 1)
            pool.memset(route[:].rearrange("p a b c -> p (a b c)"), 0.0).then_inc(sem["cleared"], 1)
            pool.wait_ge(sem["cleared"], 3)
            pool.memset(Vst[:, :, :, DH:DH + 1], 1.0).then_inc(sem["filled"], 1)
            pool.memset(route[:, :, :, 16:18], 1.0).then_inc(sem["filled"], 1)
            pool.memset(mhalf[:], -0.5).then_inc(sem["filled"], 1)
            pool.memset(KVG[:, :, 3 * D:3 * D + 2], 1.0).then_inc(sem["filled"], 1)
            pool.wait_ge(sem["stack_filled"], 16 * 2 * QD)
            pool.memset(Mx[:].rearrange("p g a b -> p (g a b)"), 0.0).then_inc(sem["filled"], 1)

            def split_low(k):
                pool.wait_ge(sem["raw_high"], k + 1)
                pool.tensor_tensor(LOW[k], rawW, HIGH[k].bitcast(F32), ALU.subtract).then_inc(sem["raw_split"], 1)

            def gelu_low(b, e):
                pool.wait_ge(sem["hid1_high"], count("hid1_high", b, e + 1))
                pool.tensor_tensor(hL[:, e % HRING], gf[:, e % GRING], hH[:, e % HRING].bitcast(F32),
                                   ALU.subtract).then_inc(sem["hid1_low_odd"], 1)

            def relu_low(b, n):
                k = n // 2
                pool.wait_ge(sem["hid0_high"], count("hid0_high", b, n + 1))
                pool.tensor_tensor(hL[:, n % HRING], gf[:, k % GRING], hH[:, n % HRING].bitcast(F32),
                                   ALU.subtract).then_inc(sem["hid0_low_pool"], 1)

            def power(target, variance, name):
                pool.tensor_tensor(target, variance, mhalf[:, 0:variance.shape[1]], ALU.pow).then_inc(sem[name], 1)

            def turn(t):
                z, l, m, a = t - 2, t - 1, t, t + 1
                if only(t, -1):
                    split_low(0)
                    pool.wait_ge(sem["consts"], 16 * 2)
                if has(a):
                    pool.wait_ge(sem["x_in"], count("x_in", a, 32))
                    pool.wait_ge(sem["x1_done"], count("x1_done", a - 1, TT))
                    pool.tensor_tensor(xb[:], xto[:], Bo[:, None, :].broadcast_to([P, TT, D]),
                                       ALU.add).then_inc(sem["xb_done"], 1)
                if only(t, -1):
                    split_low(1)
                if has(l):
                    pool.wait_ge(sem["x2_done"], count("x2_done", l, TT))
                    pool.wait_ge(sem["x3_done"], count("x3_done", l - 1, TT))
                    pool.tensor_tensor(xob[:], x2[:], Bout[:, None, :].broadcast_to([P, TT, D]),
                                       ALU.add).then_inc(sem["xob_done"], 1)
                if has(m):
                    relu_low(m, 1)
                    pool.wait_ge(sem["x1_done"], count("x1_done", m, TT))
                    pool.wait_ge(sem["x2_done"], count("x2_done", m - 1, TT))
                    pool.tensor_tensor(xbet[:], x1[:], Bet0[:, None, :].broadcast_to([P, TT, D]),
                                       ALU.add).then_inc(sem["xbet_done"], 1)
                if has(z):
                    pool.wait_ge(sem["expert_norm"], count("expert_norm", z, 21))
                    power(rsD[:], vrD[:], "expert_power")
                if has(m):
                    relu_low(m, 3)
                if has(z):
                    pool.wait_ge(sem["expert_norm"], count("expert_norm", z, 23))
                    pool.sem_inc(sem["held"], 1)
                    for n in range(TT * EXPERTS):
                        tt, e = divmod(n, EXPERTS)
                        if n in (5, 11) and has(m):
                            relu_low(m, 5 if n == 5 else 7)
                        pool.tensor_scalar(V[:, tt, e], V[:, tt, e], aD[:, n:n + 1], cD[:, n:n + 1],
                                           ALU.mult, ALU.add).then_inc(sem["expert_scaled"], 1)
                elif has(m):
                    relu_low(m, 5)
                    relu_low(m, 7)
                if only(t, 0):
                    split_low(2)
                if only(t, 1):
                    split_low(3)
                if has(z):
                    for tt in range(TT):
                        pool.wait_ge(sem["expert_scaled"], count("expert_scaled", z, (tt + 1) * EXPERTS))
                        pool.tensor_tensor(V[:, tt], V[:, tt], Lng, ALU.mult).then_inc(sem["expert_gamma"], 1)
                if has(l):
                    pool.wait_ge(sem["lin_norm"], count("lin_norm", l, 6))
                    pool.wait_ge(sem["x3_done"], count("x3_done", l - 1, TT))
                    power(rsC[:], mvC[:, :, 1], "lin_power")
                if has(z):
                    pool.wait_ge(sem["last_norm"], count("last_norm", z, 7))
                    power(rsE[:], mvE[:, :, 1], "last_power")
                if has(m):
                    pool.wait_ge(sem["moe0_norm"], count("moe0_norm", m, 9))
                    pool.wait_ge(sem["moe0_norm"], count("moe0_norm", m - 1, 11))
                    power(rsB[:, 0], mvB[:, 0, :, 1], "moe0_power")
                if has(l):
                    gelu_low(l, 1)
                if has(a):
                    pool.wait_ge(sem["attn_norm"], count("attn_norm", a, 6))
                    pool.wait_ge(sem["x1_done"], count("x1_done", a - 1, TT))
                    power(rsA[:], mvA[:, :, 1], "attn_power")
                if has(m):
                    pool.wait_ge(sem["moe0_norm"], count("moe0_norm", m, 18))
                    pool.wait_ge(sem["x2_done"], count("x2_done", m - 1, TT))
                    power(rsB[:, 1], mvB[:, 1, :, 1], "moe0_power")
                if has(l):
                    gelu_low(l, 3)
                    gelu_low(l, 5)
                    gelu_low(l, 7)

            for t in range(-1, 2):
                turn(t)
            with pool.Fori(2, SEQS - 2) as t:
                turn(t)
            for t in range(SEQS - 2, SEQS + 2):
                turn(t)

        @block.scalar
        def _(act):
            def qk_high(b):
                act.wait_ge(sem["qk_psum"], count("qk_psum", b, 1))
                act.wait_ge(sem["stack_out"], count("stack_out", b - 1, 16 * 6))
                for a in range(2):
                    act.activation(qkH[:, a], MI[:, a * T:(a + 1) * T], ACT.Identity,
                                   bias=Bqk[:, a:a + 1]).then_inc(sem["qk_high"], 1)

            def attn_exp(b, h):
                act.wait_ge(sem["exp_psum"], count("exp_psum", b, h + 1))
                if h < PRING:
                    act.wait_ge(sem["pv_psum"], count("pv_psum", b - 1, (HEADS - PRING + h) // QD + 1))
                else:
                    act.wait_ge(sem["pv_psum"], count("pv_psum", b, (h - PRING) // QD + 1))
                act.activation(Pt[:, h % PRING], SB[h % 2][:], ACT.Exp, scale=SCALE).then_inc(sem["exp_done"], 1)

            def o_copy(b, j):
                act.wait_ge(sem["pv_psum"], count("pv_psum", b, 2 * j + 2))
                act.wait_ge(sem["o_psum"], count("o_psum", b - 1, TT))
                act.wait_ge(sem["hid1_low_even"], count("hid1_low_even", b - 3, EXPERTS // 2))
                act.wait_ge(sem["hid1_low_odd"], count("hid1_low_odd", b - 3, EXPERTS // 2))
                act.activation(Ot[:, 2 * j:2 * j + 2].rearrange("p g t -> p (g t)"), PA[:],
                               ACT.Identity).then_inc(sem["o_copied"], 1)

            def relu_high(b, n):
                act.wait_ge(sem["hid0_psum"], count("hid0_psum", b, n + 1))
                if by_pool(n):
                    k = n // 2
                    if k >= GRING:
                        act.wait_ge(sem["hid0_low_pool"], count("hid0_low_pool", b, k - GRING + 1))
                    else:
                        act.wait_ge(sem["hid1_low_even"], count("hid1_low_even", b - 2, EXPERTS // 2))
                        act.wait_ge(sem["hid1_low_odd"], count("hid1_low_odd", b - 2, EXPERTS // 2))
                        act.wait_ge(sem["o_psum"], count("o_psum", b, TT))
                    act.activation(gf[:, k % GRING], Z[n % 2][:], ACT.Relu).then_inc(sem["hid0_relu"], 1)
                    act.wait_ge(sem["hid0_relu"], count("hid0_relu", b, k + 1))
                if n >= HRING:
                    act.wait_ge(sem["out0_psum"], count("out0_psum", b, n - HRING + 1))
                else:
                    act.wait_ge(sem["out1_psum"], count("out1_psum", b - 2, EXPERTS - HRING + n + 1))
                if by_pool(n):
                    act.activation(hH[:, n % HRING], gf[:, k % GRING], ACT.Identity).then_inc(sem["hid0_high"], 1)
                else:
                    act.activation(hH[:, n % HRING], Z[n % 2][:], ACT.Relu).then_inc(sem["hid0_high"], 1)

            def out_copy(b, r):
                act.wait_ge(sem["out0_psum"], count("out0_psum", b, (r + 1) * EXPERTS))
                act.wait_ge(sem["out0T_psum"], count("out0T_psum", b - 1, 1))
                act.activation(eo[:, r], MI[:, 0:T], ACT.Identity).then_inc(sem["out0_copied"], 1)

            def gelu(b, e):
                act.wait_ge(sem["hid1_psum"], count("hid1_psum", b, e + 1))
                low = "hid1_low_odd" if e % 2 else "hid1_low_even"
                if e >= GRING:
                    act.wait_ge(sem[low], count(low, b, (e - GRING) // 2 + 1))
                elif has(b + 2):
                    act.wait_ge(sem["o_psum"], count("o_psum", b + 2, TT))
                else:
                    act.wait_ge(sem[low], count(low, b - 1, EXPERTS // 2))
                for hh in range(HH):
                    act.activation(gf[:, e % GRING, hh * T:(hh + 1) * T], Z[e % 2][:, hh * T:(hh + 1) * T],
                                   ACT.Gelu, bias=B1b[:, e, hh:hh + 1]).then_inc(sem["hid1_gelu"], 1)

            def gelu_high(b, e):
                act.wait_ge(sem["hid1_gelu"], count("hid1_gelu", b, 2 * e + 2))
                if e >= HRING:
                    act.wait_ge(sem["out1_psum"], count("out1_psum", b, e - HRING + 1))
                elif has(b + 1):
                    act.wait_ge(sem["out0_psum"], count("out0_psum", b + 1, 2 * EXPERTS - HRING + e + 1))
                else:
                    act.wait_ge(sem["out1_psum"], count("out1_psum", b - 1, EXPERTS - HRING + e + 1))
                act.activation(hH[:, e % HRING], gf[:, e % GRING], ACT.Identity).then_inc(sem["hid1_high"], 1)

            def out1_copy(b, e):
                act.wait_ge(sem["out1_psum"], count("out1_psum", b, e + 1))
                if e >= 4:
                    act.wait_ge(sem["out1T_psum"], count("out1T_psum", b, e // 2 - 1))
                else:
                    act.wait_ge(sem["out1T_psum"], count("out1T_psum", b - 1, PAIRS - 1 + e // 2))
                act.activation(oT1[:, e // 2 % 2, (e % 2) * T:(e % 2 + 1) * T], SA[e % 2][:, 0:T], ACT.Identity,
                               bias=B2t[:, e:e + 1]).then_inc(sem["out1_copied"], 1)

            def attn_out(b):
                act.wait_ge(sem["oT_psum"], count("oT_psum", b, 1))
                act.wait_ge(sem["attn_psum"], count("attn_psum", b - 1, 1))
                act.activation(AoT[:], PA[:, 0:T], ACT.Identity).then_inc(sem["oT_done"], 1)

            def router0_in(b):
                act.wait_ge(sem["x1T_psum"], count("x1T_psum", b, 1))
                act.wait_ge(sem["boosted"], count("boosted", b - 1, 1))
                act.wait_ge(sem["hid0_psum"], count("hid0_psum", b - 1, EXPERTS))
                act.activation(x1f[:], PA[:, 0:T], ACT.Identity).then_inc(sem["x1T_high"], 1)
                act.activation(x1H[:], PA[:, 0:T], ACT.Identity).then_inc(sem["x1T_high"], 1)

            def router0_route(b):
                act.wait_ge(sem["route_psum"], count("route_psum", b, 1))
                act.wait_ge(sem["out0_psum"], count("out0_psum", b - 1, 2 * EXPERTS))
                act.activation(both(rm[:]), PA[0:INFO, :], ACT.Identity).then_inc(sem["route_done"], 1)

            def router0_exp(b):
                act.wait_ge(sem["pick0"], count("pick0", b, 6))
                act.wait_ge(sem["value0"], count("value0", b - 1, 3))
                act.activation(both(e0[:]), both(dl0[:]), ACT.Exp).then_inc(sem["gate0_exp"], 1)

            def lin_copy(b):
                act.wait_ge(sem["x2T_psum"], count("x2T_psum", b, 1))
                act.wait_ge(sem["linout_psum"], count("linout_psum", b - 1, 1))
                act.activation(xcf[:], SB[0][:, 0:T], ACT.Identity).then_inc(sem["x2T_done"], 1)

            def lin_queries(b):
                act.wait_ge(sem["q1_min"], count("q1_min", b, 1))
                act.wait_ge(sem["gate1_psum"], count("gate1_psum", b - 1, 1))
                act.activation(eq[:], uq, ACT.Exp).then_inc(sem["q1_exp"], 1)
                act.activation(pq[:], SB[0][:, T:2 * T], ACT.Relu, bias=Bq1).then_inc(sem["q1_exp"], 1)

            def lin_keys(b):
                act.wait_ge(sem["k1_min"], count("k1_min", b, 1))
                act.wait_ge(sem["gate1_done"], count("gate1_done", b - 1, 1))
                act.activation(both(ek[:]), both(uk[:]), ACT.Exp).then_inc(sem["kg_exp"], 1)
                act.activation(eg[:], KVG[:, :, 0:D], ACT.Exp, scale=-1.0).then_inc(sem["kg_exp"], 1)

            def lin_gated(b):
                act.wait_ge(sem["linT_psum"], count("linT_psum", b, 1))
                act.activation(gT[:], SA[0][:, 0:T], ACT.Identity).then_inc(sem["linT_done"], 1)

            def router1_in(b):
                act.wait_ge(sem["x3T_psum"], count("x3T_psum", b, 1))
                act.wait_ge(sem["hid1_psum"], count("hid1_psum", b - 1, EXPERTS))
                act.activation(x3f[:], SA[1][:, 0:T], ACT.Identity).then_inc(sem["x3T_high"], 1)
                act.activation(x3H[:], SA[1][:, 0:T], ACT.Identity).then_inc(sem["x3T_high"], 1)

            def router1_exp(b):
                act.wait_ge(sem["pick1"], count("pick1", b, 6))
                act.wait_ge(sem["weight1"], count("weight1", b - 1, 3))
                act.activation(e1[:], dl1[:], ACT.Exp).then_inc(sem["pick1_exp"], 1)

            def weights(b):
                act.wait_ge(sem["weightsT_psum"], count("weightsT_psum", b, 1))
                act.wait_ge(sem["beta_psum"], count("beta_psum", b - 1, 1))
                act.activation(wET[:], MI[0:EXPERTS, 0:T], ACT.Identity).then_inc(sem["weightsT_done"], 1)

            def split_high(k):
                act.wait_ge(sem["raw_in"], 16 * (k + 1) if k < 3 else 16 * 5)
                act.activation(HIGH[k], rawW, ACT.Identity).then_inc(sem["raw_high"], 1)

            def turn(t):
                l, m, a, n = t - 1, t, t + 1, t + 2
                if only(t, 1):
                    split_high(3)
                if has(m):
                    router0_exp(m)
                for e in range(EXPERTS):
                    if has(m):
                        relu_high(m, e)
                    if has(l):
                        if e == 0:
                            lin_copy(l)
                        if e == 3:
                            lin_queries(l)
                        if e == 4:
                            lin_keys(l)
                    if only(t, 0) and e == 4:
                        split_high(2)
                if has(m):
                    out_copy(m, 0)
                for e in range(EXPERTS):
                    if has(m):
                        relu_high(m, EXPERTS + e)
                    if has(a):
                        attn_exp(a, 2 * e)
                        attn_exp(a, 2 * e + 1)
                        if e == 6:
                            o_copy(a, 0)
                    if has(l):
                        if e == 2:
                            lin_gated(l)
                        if e == 6:
                            router1_in(l)
                    if only(t, -1) and e == 4:
                        split_high(1)
                if has(l):
                    router1_exp(l)
                if has(m):
                    out_copy(m, 1)
                if has(a):
                    o_copy(a, 1)
                for e in range(EXPERTS):
                    if has(l):
                        gelu(l, e)
                    if e == 2 and has(a):
                        router0_in(a)
                    if has(l):
                        gelu_high(l, e)
                        if e >= 2:
                            out1_copy(l, e - 2)
                    if e == 0 and has(a):
                        attn_out(a)
                    if e == 3 and has(n):
                        qk_high(n)
                    if e == 5 and has(a):
                        router0_route(a)
                if has(l):
                    out1_copy(l, EXPERTS - 2)
                    out1_copy(l, EXPERTS - 1)
                if has(l):
                    weights(l)

            act.wait_ge(sem["near_consts"], 32)
            qk_high(0)
            act.wait_ge(sem["info_in"], 16)
            act.activation(infoW[:], infoRaw, ACT.Identity).then_inc(sem["info_high"], 1)
            split_high(0)
            act.wait_ge(sem["info_split"], 1)
            for t in range(-1, 2):
                turn(t)
            with act.Fori(2, SEQS - 2) as t:
                turn(t)
            for t in range(SEQS - 2, SEQS + 2):
                turn(t)

        @block.tensor
        def _(pe):
            def project(b):
                pe.wait_ge(sem["x_in"], count("x_in", b, 32))
                if has(b - 2):
                    pe.wait_ge(sem["moe0_norm"], count("moe0_norm", b - 2, 4))
                else:
                    pe.wait_ge(sem["v_done"], count("v_done", b - 1, 2))
                for a in range(2):
                    last = pe.matmul(MI[:, a * T:(a + 1) * T], Wqk[:, a], xTs[:], start=True, stop=True)
                last.then_inc(sem["qk_psum"], 1)

            def project_values(b):
                pe.wait_ge(sem["qk_low"], count("qk_low", b, 2))
                for tt in range(TT):
                    last = pe.matmul(MI[:, tt * D:(tt + 1) * D], xTs[:, tt * P:(tt + 1) * P], Wv,
                                     start=True, stop=True)
                last.then_inc(sem["v_psum"], 1)

            def max_scores(b, h):
                g, i = divmod(h, QD)
                if h == 0:
                    pe.wait_ge(sem["stack_in"], count("stack_in", b, 16 * (1 + QD)))
                if h < 2:
                    pe.wait_ge(sem["out1_copied"], count("out1_copied", b - 3, EXPERTS))
                else:
                    pe.wait_ge(sem["max_done"], count("max_done", b, h - 1))
                for tt in range(TT):
                    last = pe.matmul(SA[h % 2][:, tt * T:(tt + 1) * T], Qs[:, g, tt * P:(tt + 1) * P],
                                     Km[:, i, g], start=True, stop=True)
                last.then_inc(sem["max_psum"], 1)

            def negmax(b):
                pe.wait_ge(sem["negmax"], count("negmax", b, 3))
                for j in range(2):
                    for g in (2 * j, 2 * j + 1):
                        for tt in range(TT):
                            at = (g % 2) * T + tt * P
                            last = pe.transpose(SA[j][:, at:at + P], Mx[:, g, tt], idn)
                    last.then_inc(sem["negmax_psum"], 1)

            def exp_scores(b, h):
                g, i = divmod(h, QD)
                pe.wait_ge(sem["q_shifted"], count("q_shifted", b, g // 2 + 1))
                if h == 0:
                    pe.wait_ge(sem["q1_exp"], count("q1_exp", b - 2, 2))
                    pe.wait_ge(sem["kvg_done"], count("kvg_done", b - 2, TT))
                if h >= 2:
                    pe.wait_ge(sem["exp_done"], count("exp_done", b, h - 1))
                for kt in range(TT):
                    last = pe.matmul(SB[h % 2][:, kt * T:(kt + 1) * T], Km[:, i, g, kt * P:(kt + 1) * P],
                                     Qs[:, g], start=True, stop=True)
                last.then_inc(sem["exp_psum"], 1)

            def weighted_values(b, g):
                if g == 0:
                    pe.wait_ge(sem["v_done"], count("v_done", b, 2))
                    pe.wait_ge(sem["lin_gated"], count("lin_gated", b - 2, 5))
                if g == 2:
                    pe.wait_ge(sem["o_copied"], count("o_copied", b, 1))
                pe.wait_ge(sem["exp_done"], count("exp_done", b, QD * g + QD))
                for kt in range(TT):
                    for i in range(QD):
                        h = QD * g + i
                        last = pe.matmul(PA[32 * i:32 * i + 32, (g % 2) * T:(g % 2 + 1) * T], Vst[:, kt, h],
                                         Pt[:, h % PRING, kt * T:(kt + 1) * T], start=(kt == 0),
                                         stop=(kt == TT - 1), skip_group_check=True)
                last.then_inc(sem["pv_psum"], 1)

            def attn_turns(b):
                pe.wait_ge(sem["o_copied"], count("o_copied", b, 2))
                pe.wait_ge(sem["exp_done"], count("exp_done", b, HEADS))
                for tt in range(TT):
                    for g in range(G):
                        last = pe.transpose(SB[tt][:, g * P:(g + 1) * P], Ot[:, g, tt * P:(tt + 1) * P], idn)
                    last.then_inc(sem["o_psum"], 1)

            def attn_heads(b):
                pe.wait_ge(sem["o_done"], count("o_done", b, TT))
                for tt in range(TT):
                    last = pe.transpose(PA[:, tt * P:(tt + 1) * P], Ao[:, tt], idn)
                last.then_inc(sem["oT_psum"], 1)

            def attn_out(b):
                pe.wait_ge(sem["oT_done"], count("oT_done", b, 1))
                for tt in range(TT):
                    last = pe.matmul(PA[:, T + tt * D:T + (tt + 1) * D], AoT[:, tt * P:(tt + 1) * P], Wo,
                                     start=True, stop=True)
                last.then_inc(sem["attn_psum"], 1)

            def router0_in(b):
                pe.wait_ge(sem["x1_done"], count("x1_done", b, TT))
                for tt in range(TT):
                    last = pe.transpose(PA[:, tt * P:(tt + 1) * P], x1[:, tt], idn)
                last.then_inc(sem["x1T_psum"], 1)

            def router0_gate(b):
                pe.wait_ge(sem["x1T_high"], count("x1T_high", b, 2))
                pe.wait_ge(sem["x1T_low"], count("x1T_low", b, 1))
                for tt in range(TT):
                    last = pe.matmul(PA[:, tt * EXPERTS:(tt + 1) * EXPERTS], x1f[:, tt * P:(tt + 1) * P], G0w,
                                     start=True, stop=True)
                last.then_inc(sem["gate0_psum"], 1)

            def router0_route(b):
                pe.wait_ge(sem["pick0"], count("pick0", b, 13))
                for r in range(2):
                    for tt in range(TT):
                        at = r * T + tt * P
                        last = pe.transpose(PA[0:INFO, at:at + P], route[:, tt, r], idn)
                last.then_inc(sem["route_psum"], 1)

            def hidden0(b, n):
                r, e = divmod(n, EXPERTS)
                if n == 0:
                    pe.wait_ge(sem["x1T_high"], count("x1T_high", b, 2))
                    pe.wait_ge(sem["x1T_low"], count("x1T_low", b, 1))
                    pe.wait_ge(sem["route_done"], count("route_done", b, 1))
                if n == EXPERTS:
                    pe.wait_ge(sem["boosted"], count("boosted", b, 3))
                if n >= 2:
                    low, step = low0(n - 2)
                    pe.wait_ge(sem[low], count(low, b, step))
                else:
                    pe.wait_ge(sem["hid1_gelu"], count("hid1_gelu", b - 2, 2 * (EXPERTS - 2 + n) + 2))
                high, rest = ((x1H, x1L), (x2H, x2L))[r]
                for hh in range(HH):
                    z = Z[n % 2][:, hh * T:(hh + 1) * T]
                    w = slice(hh * P, (hh + 1) * P)
                    pe.matmul(z, W1H[0][:, e, w], high[:], start=True, stop=False)
                    pe.matmul(z, W1H[0][:, e, w], rest[:], start=False, stop=False)
                    pe.matmul(z, W1L[0][:, e, w], high[:], start=False, stop=False)
                    at = e * HID + hh * P
                    last = pe.matmul(z, infoW[:, at:at + P], rm[:, r], start=False, stop=True)
                last.then_inc(sem["hid0_psum"], 1)

            def outs0(b, n):
                r, e = divmod(n, EXPERTS)
                o = MI[:, 0:T]
                if n == 0:
                    pe.wait_ge(sem["last_norm"], count("last_norm", b - 2, 1))
                    if has(b + 1):
                        pe.wait_ge(sem["v_done"], count("v_done", b + 1, 2))
                if e == 0:
                    if r == 1:
                        pe.wait_ge(sem["out0_copied"], count("out0_copied", b, 1))
                    pe.matmul(o, infoW[:, EXPERTS * HID:NINF], rm[:, r], start=True, stop=False)
                low, step = low0(n)
                pe.wait_ge(sem[low], count(low, b, step))
                for hh in range(HH):
                    h_high = hH[:, n % HRING, hh * T:(hh + 1) * T]
                    h_low = hL[:, n % HRING, hh * T:(hh + 1) * T]
                    pe.matmul(o, W2H[0][:, e, hh], h_high, start=False, stop=False)
                    pe.matmul(o, W2H[0][:, e, hh], h_low, start=False, stop=False)
                    last = pe.matmul(o, W2L[0][:, e, hh], h_high, start=False,
                                     stop=(e == EXPERTS - 1 and hh == HH - 1))
                last.then_inc(sem["out0_psum"], 1)

            def moe0_turns(b):
                pe.wait_ge(sem["out0_copied"], count("out0_copied", b, 2))
                for r in range(2):
                    for tt in range(TT):
                        at = (r * TT + tt) * D
                        last = pe.transpose(MI[:, at:at + D], eo[:, r, tt * P:(tt + 1) * P], idn)
                last.then_inc(sem["out0T_psum"], 1)

            def lin_turn(b):
                pe.wait_ge(sem["x2_done"], count("x2_done", b, TT))
                if has(b + 1):
                    pe.wait_ge(sem["o_done"], count("o_done", b + 1, TT))
                pe.wait_ge(sem["expert_sum"], count("expert_sum", b - 1, 2 * PAIRS))
                for tt in range(TT):
                    last = pe.transpose(SB[0][:, tt * P:(tt + 1) * P], x2[:, tt], idn)
                last.then_inc(sem["x2T_psum"], 1)

            def lin_project(b):
                pe.wait_ge(sem["x2T_done"], count("x2T_done", b, 1))
                pe.matmul(SB[0][:, T:2 * T], Wq1, xcf[:], start=True, stop=True).then_inc(sem["q1_psum"], 1)
                for tt in range(TT):
                    pe.matmul((SB[1], PA)[tt][:, 0:3 * D], xcf[:, tt * P:(tt + 1) * P], Wkvg,
                              start=True, stop=True).then_inc(sem["kvg_psum"], 1)

            def lin_kv(b):
                pe.wait_ge(sem["k1_done"], count("k1_done", b, 1))
                pe.wait_ge(sem["kvg_done"], count("kvg_done", b, TT))
                for tt in range(TT):
                    last = pe.matmul(PA[:, 0:D + 1], kf[:, tt], KVG[:, tt, 2 * D:3 * D + 1], start=(tt == 0),
                                     stop=(tt == TT - 1))
                last.then_inc(sem["kv_psum"], 1)

            def lin_read(b):
                pe.wait_ge(sem["kv_blocks"], count("kv_blocks", b, 2))
                pe.wait_ge(sem["q1_done"], count("q1_done", b, 1))
                for tt in range(TT):
                    last = pe.matmul(PA[:, tt * 2 * D:tt * 2 * D + D + HEADS], qf[:, tt * P:(tt + 1) * P], BD[:],
                                     start=True, stop=True)
                last.then_inc(sem["lin_psum"], 1)

            def lin_gated(b):
                pe.wait_ge(sem["lin_gated"], count("lin_gated", b, 5))
                if has(b + 2):
                    pe.wait_ge(sem["q_shifted"], count("q_shifted", b + 2, 2))
                else:
                    pe.wait_ge(sem["out1_copied"], count("out1_copied", b - 1, EXPERTS))
                for tt in range(TT):
                    last = pe.transpose(SA[0][:, tt * P:(tt + 1) * P], go[:, tt], idn)
                last.then_inc(sem["linT_psum"], 1)

            def lin_out(b):
                pe.wait_ge(sem["linT_done"], count("linT_done", b, 1))
                for tt in range(TT):
                    last = pe.matmul(SA[0][:, T + tt * D:T + (tt + 1) * D], gT[:, tt * P:(tt + 1) * P], Wout,
                                     start=True, stop=True)
                last.then_inc(sem["linout_psum"], 1)

            def router1_in(b):
                pe.wait_ge(sem["x3_done"], count("x3_done", b, TT))
                for tt in range(TT):
                    last = pe.transpose(SA[1][:, tt * P:(tt + 1) * P], x3[:, tt], idn)
                last.then_inc(sem["x3T_psum"], 1)

            def router1_gate(b):
                pe.wait_ge(sem["x3T_high"], count("x3T_high", b, 2))
                pe.wait_ge(sem["x3T_low"], count("x3T_low", b, 1))
                for tt in range(TT):
                    last = pe.matmul(SA[1][:, tt * EXPERTS:(tt + 1) * EXPERTS], x3f[:, tt * P:(tt + 1) * P], G1w,
                                     start=True, stop=True)
                last.then_inc(sem["gate1_psum"], 1)

            def weights(b):
                pe.wait_ge(sem["weights_done"], count("weights_done", b, 1))
                if has(b + 3):
                    pe.wait_ge(sem["v_done"], count("v_done", b + 3, 2))
                elif has(b + 1):
                    pe.wait_ge(sem["moe0_norm"], count("moe0_norm", b + 1, 4))
                else:
                    pe.wait_ge(sem["last_norm"], count("last_norm", b - 1, 1))
                for tt in range(TT):
                    last = pe.transpose(MI[0:EXPERTS, tt * P:(tt + 1) * P], wE[:, tt], idn)
                last.then_inc(sem["weightsT_psum"], 1)

            def hidden1(b, e):
                if only(b, 0) and e == 0:
                    pe.wait_ge(sem["raw_split"], 4)
                if e == 0:
                    pe.wait_ge(sem["x3T_high"], count("x3T_high", b, 2))
                    pe.wait_ge(sem["x3T_low"], count("x3T_low", b, 1))
                if e >= 2:
                    pe.wait_ge(sem["hid1_gelu"], count("hid1_gelu", b, 2 * e - 2))
                elif has(b + 1):
                    low, step = low0(2 * EXPERTS - 2 + e)
                    pe.wait_ge(sem[low], count(low, b + 1, step))
                else:
                    pe.wait_ge(sem["hid1_gelu"], count("hid1_gelu", b - 1, 2 * (EXPERTS - 2 + e) + 2))
                for hh in range(HH):
                    z = Z[e % 2][:, hh * T:(hh + 1) * T]
                    w = slice(hh * P, (hh + 1) * P)
                    pe.matmul(z, W1H[1][:, e, w], x3H[:], start=True, stop=False)
                    pe.matmul(z, W1H[1][:, e, w], x3L[:], start=False, stop=False)
                    last = pe.matmul(z, W1L[1][:, e, w], x3H[:], start=False, stop=True)
                last.then_inc(sem["hid1_psum"], 1)

            def outs1(b, e):
                if e == 0:
                    pe.wait_ge(sem["pick1"], count("pick1", b, 1))
                if e >= 2:
                    pe.wait_ge(sem["out1_copied"], count("out1_copied", b, e - 1))
                low = "hid1_low_odd" if e % 2 else "hid1_low_even"
                pe.wait_ge(sem[low], count(low, b, e // 2 + 1))
                o = SA[e % 2][:, 0:T]
                for hh in range(HH):
                    h_high = hH[:, e % HRING, hh * T:(hh + 1) * T]
                    h_low = hL[:, e % HRING, hh * T:(hh + 1) * T]
                    pe.matmul(o, W2H[1][:, e, hh], h_high, start=(hh == 0), stop=False)
                    pe.matmul(o, W2H[1][:, e, hh], h_low, start=False, stop=False)
                    last = pe.matmul(o, W2L[1][:, e, hh], h_high, start=False, stop=(hh == HH - 1))
                last.then_inc(sem["out1_psum"], 1)

            def turns1(b, k):
                pe.wait_ge(sem["out1_copied"], count("out1_copied", b, 2 * k + 2))
                if k >= 2:
                    pe.wait_ge(sem["expert_sum"], count("expert_sum", b, 2 * (k - 1)))
                elif has(b + 2):
                    pe.wait_ge(sem["o_done"], count("o_done", b + 2, TT))
                else:
                    pe.wait_ge(sem["expert_sum"], count("expert_sum", b - 1, 2 * PAIRS))
                for tt in range(TT):
                    for e in range(2):
                        c = (2 * tt + e) * D
                        last = pe.transpose(SB[k % 2][:, c:c + D], oT1[:, k % 2, e * T + tt * P:e * T + (tt + 1) * P],
                                            idn)
                last.then_inc(sem["out1T_psum"], 1)

            def beta_sums(b):
                pe.wait_ge(sem["weightsT_done"], count("weightsT_done", b, 1))
                for tt in range(TT):
                    last = pe.matmul(MI[:, T + tt * D:T + (tt + 1) * D], wET[:, tt * P:(tt + 1) * P], Lnb[:],
                                     start=True, stop=True)
                last.then_inc(sem["beta_psum"], 1)

            def turn(t):
                l, m, a, n = t - 1, t, t + 1, t + 2
                for e in range(EXPERTS):
                    if has(m):
                        hidden0(m, e)
                    if has(a):
                        max_scores(a, 2 * e)
                    if has(m) and e >= 1:
                        outs0(m, e - 1)
                    if has(a):
                        max_scores(a, 2 * e + 1)
                    if has(l):
                        if e == 0:
                            lin_turn(l)
                        if e == 1:
                            lin_project(l)
                        if e == 5:
                            lin_kv(l)
                if has(m):
                    outs0(m, EXPERTS - 1)
                if only(t, -1):
                    pe.wait_ge(sem["filled"], 6)
                if has(a):
                    negmax(a)
                if has(l):
                    lin_read(l)
                for e in range(EXPERTS):
                    if has(m):
                        hidden0(m, EXPERTS + e)
                    if has(a):
                        exp_scores(a, 2 * e)
                    if has(m) and e >= 1:
                        outs0(m, EXPERTS + e - 1)
                    if has(a):
                        exp_scores(a, 2 * e + 1)
                        if e in (3, 5, 7):
                            weighted_values(a, (e - 3) // 2)
                    if has(l):
                        if e == 2:
                            lin_gated(l)
                        if e == 3:
                            lin_out(l)
                        if e == 6:
                            router1_in(l)
                        if e == 7:
                            router1_gate(l)
                if has(m):
                    outs0(m, 2 * EXPERTS - 1)
                if has(a):
                    weighted_values(a, G - 1)
                if has(a):
                    attn_turns(a)
                if has(m):
                    moe0_turns(m)
                if has(l):
                    hidden1(l, 0)
                    hidden1(l, 1)
                if has(a):
                    attn_heads(a)
                    attn_out(a)
                for e in range(EXPERTS):
                    if has(l):
                        outs1(l, e)
                        if e < EXPERTS - 2:
                            hidden1(l, e + 2)
                        if e >= 3 and e % 2 == 1:
                            turns1(l, (e - 3) // 2)
                    if e == 0 and has(a):
                        router0_in(a)
                    if e == 1 and has(n):
                        project(n)
                    if e == 2 and has(a):
                        router0_gate(a)
                    if e == 4 and has(n):
                        project_values(n)
                    if e == 4 and has(a):
                        router0_route(a)
                if has(l):
                    weights(l)
                    turns1(l, PAIRS - 1)
                if has(l):
                    beta_sums(l)

            pe.wait_ge(sem["near_consts"], 32)
            project(0)
            project_values(0)
            pe.wait_ge(sem["consts"], 16 * 2)
            turn(-1)
            pe.wait_ge(sem["info_split"], 1)
            pe.wait_ge(sem["raw_split"], 2)
            turn(0)
            turn(1)
            with pe.Fori(2, SEQS - 2) as t:
                turn(t)
            for t in range(SEQS - 2, SEQS + 2):
                turn(t)

        @block.vector
        def _(dve):
            def qk_low(b):
                dve.wait_ge(sem["qk_high"], count("qk_high", b, 2))
                dve.wait_ge(sem["stack_out"], count("stack_out", b - 1, 16 * 6))
                for a in range(2):
                    dve.scalar_tensor_tensor(out=qkL[:, a], in0=MI[:, a * T:(a + 1) * T],
                                             scalar=Bqk[:, a:a + 1], in1=qkH[:, a].bitcast(F32),
                                             op0=ALU.add, op1=ALU.subtract).then_inc(sem["qk_low"], 1)

            def values(b):
                dve.wait_ge(sem["v_psum"], count("v_psum", b, 1))
                dve.wait_ge(sem["pv_psum"], count("pv_psum", b - 1, G))
                for kt in range(TT):
                    dve.tensor_tensor(Vst[:, kt, :, 0:DH],
                                      MI[:, kt * D:(kt + 1) * D].rearrange("p (h d) -> p h d", h=HEADS),
                                      Bv.rearrange("p (h d) -> p h d", h=HEADS), ALU.add).then_inc(sem["v_done"], 1)

            def maximum(b, h):
                g, i = divmod(h, QD)
                dve.wait_ge(sem["max_psum"], count("max_psum", b, h + 1))
                dve.tensor_reduce(mx[:, g, i], SA[h % 2][:].rearrange("p (q k) -> p q k", q=TT), AX_X, ALU.max).then_inc(sem["max_done"], 1)

            def negmax(b):
                at = Mx[:].rearrange("p g q (i c) -> p g i q c", c=32)
                dve.wait_ge(sem["max_done"], count("max_done", b, HEADS))
                dve.wait_ge(sem["negmax_psum"], count("negmax_psum", b - 1, 2))
                dve.tensor_scalar(nmH[:].rearrange("p g i q -> p (g i q)"),
                                  mx[:].rearrange("p g i q -> p (g i q)"), -1.0, None, ALU.mult).then_inc(sem["negmax"], 1)
                dve.tensor_scalar(at[:, :, :, :, 24], mx[:], -1.0, None, ALU.mult).then_inc(sem["negmax"], 1)
                dve.wait_ge(sem["negmax"], count("negmax", b, 2))
                dve.tensor_tensor(at[:, :, :, :, 25], at[:, :, :, :, 24], nmH[:].bitcast(F32), ALU.subtract).then_inc(sem["negmax"], 1)

            def shift(b):
                for j in range(2):
                    dve.wait_ge(sem["negmax_psum"], count("negmax_psum", b, j + 1))
                    q = Qs[:, 2 * j:2 * j + 2].rearrange("p g t -> p (g t)")
                    dve.tensor_tensor(q, SA[j][:], q.bitcast(F32), ALU.add).then_inc(sem["q_shifted"], 1)

            def attn_divide(b):
                for tt in range(TT):
                    o = SB[tt][:].rearrange("p (h c) -> p h c", c=32)
                    dve.wait_ge(sem["o_psum"], count("o_psum", b, tt + 1))
                    dve.reciprocal(rec[:, tt], o[:, :, DH]).then_inc(sem["o_inverse"], 1)
                    dve.wait_ge(sem["o_inverse"], count("o_inverse", b, tt + 1))
                    dve.wait_ge(sem["oT_psum"], count("oT_psum", b - 1, 1))
                    dve.tensor_tensor(Ao[:, tt].rearrange("p (h d) -> p h d", h=HEADS), o[:, :, 0:DH],
                                      rec[:, tt][:, :, None].broadcast_to([P, HEADS, DH]), ALU.mult).then_inc(sem["o_done"], 1)

            def statistics(b, name, step, y, stat, mv, eps):
                for tt in range(TT):
                    dve.bn_stats(stat[:, tt], y[:, tt]).then_inc(sem[name], 1)
                dve.wait_ge(sem[name], count(name, b, step + 2))
                dve.sem_inc(sem["held"], 1)
                for tt in range(TT):
                    dve.bn_aggr(mv[:, tt], stat[:, tt]).then_inc(sem[name], 1)
                dve.wait_ge(sem[name], count(name, b, step + 4))
                dve.tensor_scalar(mv[:, :, 1], mv[:, :, 1], eps, None, ALU.add).then_inc(sem[name], 1)

            def normalize(target, y, mv, rs, name):
                for tt in range(TT):
                    dve.tensor_scalar(target[:, tt], y[:, tt], mv[:, tt, 0:1], rs[:, tt:tt + 1],
                                      ALU.subtract, ALU.mult).then_inc(sem[name], 1)

            def attn_stats(b):
                dve.wait_ge(sem["attn_psum"], count("attn_psum", b, 1))
                dve.wait_ge(sem["xb_done"], count("xb_done", b, 1))
                dve.tensor_tensor(both(yA[:]), PA[:, T:2 * T], both(xb[:]), ALU.add).then_inc(sem["attn_norm"], 1)
                dve.wait_ge(sem["attn_norm"], count("attn_norm", b, 1))
                statistics(b, "attn_norm", 1, yA, statA, mvA, LN_EPS)

            def attn_norm(b):
                dve.wait_ge(sem["attn_power"], count("attn_power", b, 1))
                dve.wait_ge(sem["xbet_done"], count("xbet_done", b - 1, 1))
                dve.wait_ge(sem["x1T_psum"], count("x1T_psum", b - 1, 1))
                normalize(x1, yA, mvA, rsA, "x1_done")

            def x1_low(b):
                dve.wait_ge(sem["x1T_high"], count("x1T_high", b, 2))
                dve.wait_ge(sem["hid0_psum"], count("hid0_psum", b - 1, EXPERTS))
                dve.tensor_tensor(x1L[:], PA[:, 0:T], x1H[:].bitcast(F32), ALU.subtract).then_inc(sem["x1T_low"], 1)

            def pick_two(b, psum_name, bankt, bias, lg, top, ix, ixf, name):
                dve.wait_ge(sem[psum_name], count(psum_name, b, 1))
                if bias is None:
                    dve.tensor_copy(both(lg[:]), bankt[:, 0:TT * EXPERTS]).then_inc(sem[name], 1)
                else:
                    dve.tensor_tensor(lg[:], bankt[:, 0:TT * EXPERTS].rearrange("p (a e) -> p a e", a=TT),
                                      bias[:, None, :].broadcast_to([P, TT, EXPERTS]), ALU.add).then_inc(sem[name], 1)
                dve.wait_ge(sem[name], count(name, b, 1))
                dve.sem_inc(sem["held"], 1)
                for tt in range(TT):
                    dve.max(top[:, tt], lg[:, tt]).then_inc(sem[name], 1)
                dve.wait_ge(sem[name], count(name, b, 3))
                dve.sem_inc(sem["held"], 1)
                for tt in range(TT):
                    dve.max_index(ix[:, tt], top[:, tt], lg[:, tt]).then_inc(sem[name], 1)

            def router0_pick(b):
                pick_two(b, "gate0_psum", PA, G0b, lg0, top0, ix0, ixf0, "pick0")
                dve.wait_ge(sem["gate0_exp"], count("gate0_exp", b - 1, 1))
                dve.tensor_tensor(dl0[:], top0[:], top0[:, :, 0:1].broadcast_to([P, TT, EXPERTS]),
                                  ALU.subtract).then_inc(sem["pick0"], 1)
                dve.wait_ge(sem["pick0"], count("pick0", b, 5))
                dve.tensor_copy(both(ixf0[:]), both(ix0[:])).then_inc(sem["pick0"], 1)
                dve.wait_ge(sem["pick0"], count("pick0", b, 7))
                dve.wait_ge(sem["route_psum"], count("route_psum", b - 1, 1))
                for r in range(2):
                    for tt in range(TT):
                        dve.tensor_scalar(route[:, tt, r, 0:EXPERTS], iota, ixf0[:, tt, r:r + 1], None,
                                          ALU.is_equal).then_inc(sem["pick0"], 1)
                dve.wait_ge(sem["pick0"], count("pick0", b, 11))
                chosen = route[:, :, :, 0:EXPERTS]
                dve.tensor_scalar(route[:, :, :, EXPERTS:2 * EXPERTS], chosen, -1.0, None, ALU.add).then_inc(sem["pick0"], 1)
                dve.tensor_copy(route[:, :, :, INFO - EXPERTS:INFO], chosen).then_inc(sem["pick0"], 1)

            def router0_values(b):
                dve.wait_ge(sem["gate0_exp"], count("gate0_exp", b, 1))
                dve.tensor_reduce(s0[:], e0[:], AX_X, ALU.add).then_inc(sem["value0"], 1)
                dve.wait_ge(sem["value0"], count("value0", b, 1))
                dve.reciprocal(r0[:], s0[:]).then_inc(sem["value0"], 1)
                dve.wait_ge(sem["value0"], count("value0", b, 2))
                dve.tensor_tensor(val0[:], e0[:, :, 0:2], r0[:][:, :, None].broadcast_to([P, TT, 2]),
                                  ALU.mult).then_inc(sem["value0"], 1)

            def relu_low(b, n):
                dve.wait_ge(sem["hid0_high"], count("hid0_high", b, n + 1))
                if n >= HRING:
                    dve.wait_ge(sem["out0_psum"], count("out0_psum", b, n - HRING + 1))
                else:
                    dve.wait_ge(sem["out1_psum"], count("out1_psum", b - 2, EXPERTS - HRING + n + 1))
                dve.scalar_tensor_tensor(out=hL[:, n % HRING], in0=Z[n % 2][:], scalar=0.0,
                                         in1=hH[:, n % HRING].bitcast(F32), op0=ALU.max,
                                         op1=ALU.subtract).then_inc(sem["hid0_low"], 1)

            def boost(b):
                dve.wait_ge(sem["out0_copied"], count("out0_copied", b, 1))
                dve.scalar_tensor_tensor(out=x2f[:], in0=eo[:, 0], scalar=0.5, in1=x1f[:], op0=ALU.mult,
                                         op1=ALU.add).then_inc(sem["boosted"], 1)
                dve.wait_ge(sem["boosted"], count("boosted", b, 1))
                dve.wait_ge(sem["hid0_psum"], count("hid0_psum", b - 1, 2 * EXPERTS))
                dve.tensor_copy(x2H[:], x2f[:]).then_inc(sem["boosted"], 1)
                dve.wait_ge(sem["boosted"], count("boosted", b, 2))
                dve.tensor_tensor(x2L[:], x2f[:], x2H[:].bitcast(F32), ALU.subtract).then_inc(sem["boosted"], 1)

            def moe0_stats(b):
                dve.wait_ge(sem["out0T_psum"], count("out0T_psum", b, 1))
                dve.wait_ge(sem["value0"], count("value0", b, 3))
                for tt in range(TT):
                    dve.scalar_tensor_tensor(out=f0[:, tt], in0=MI[:, tt * D:(tt + 1) * D],
                                             scalar=val0[:, tt, 0:1], in1=x1[:, tt], op0=ALU.mult,
                                             op1=ALU.add).then_inc(sem["moe0_norm"], 1)
                dve.wait_ge(sem["moe0_norm"], count("moe0_norm", b, 2))
                for tt in range(TT):
                    dve.scalar_tensor_tensor(out=f1[:, tt], in0=MI[:, (TT + tt) * D:(TT + tt + 1) * D],
                                             scalar=val0[:, tt, 1:2], in1=f0[:, tt], op0=ALU.mult,
                                             op1=ALU.add).then_inc(sem["moe0_norm"], 1)
                dve.wait_ge(sem["moe0_norm"], count("moe0_norm", b, 4))
                statistics(b, "moe0_norm", 4, f1, statB[:, 0], mvB[:, 0], LN_EPS)

            def moe0_norm(b):
                dve.wait_ge(sem["moe0_power"], count("moe0_power", b, 1))
                normalize(n0, f1, mvB[:, 0], rsB[:, 0], "moe0_norm")
                dve.wait_ge(sem["moe0_norm"], count("moe0_norm", b, 11))
                if has(b + 1):
                    dve.wait_ge(sem["oT_psum"], count("oT_psum", b + 1, 1))
                dve.tensor_tensor(ng[:], n0[:], Gam0[:, None, :].broadcast_to([P, TT, D]), ALU.mult).then_inc(sem["moe0_norm"], 1)
                dve.wait_ge(sem["moe0_norm"], count("moe0_norm", b, 12))
                dve.wait_ge(sem["xbet_done"], count("xbet_done", b, 1))
                dve.tensor_tensor(yB[:], ng[:], xbet[:], ALU.add).then_inc(sem["moe0_norm"], 1)

            def moe0_norm_stats(b):
                dve.wait_ge(sem["moe0_norm"], count("moe0_norm", b, 13))
                statistics(b, "moe0_norm", 13, yB, statB[:, 1], mvB[:, 1], LN_EPS)

            def moe0_end(b):
                dve.wait_ge(sem["moe0_power"], count("moe0_power", b, 2))
                dve.wait_ge(sem["xob_done"], count("xob_done", b - 1, 1))
                dve.wait_ge(sem["x2T_psum"], count("x2T_psum", b - 1, 1))
                normalize(x2, yB, mvB[:, 1], rsB[:, 1], "x2_done")

            def lin_features(b):
                dve.wait_ge(sem["q1_psum"], count("q1_psum", b, 1))
                dve.wait_ge(sem["q1_exp"], count("q1_exp", b - 1, 1))
                dve.tensor_scalar(uq, SB[0][:, T:2 * T], Bq1, 0.0, ALU.add, ALU.min).then_inc(sem["q1_min"], 1)
                for tt in range(TT):
                    dve.wait_ge(sem["kvg_psum"], count("kvg_psum", b, tt + 1))
                    if tt == 0:
                        dve.wait_ge(sem["kv_psum"], count("kv_psum", b - 1, 1))
                        dve.wait_ge(sem["kg_exp"], count("kg_exp", b - 1, 2))
                    dve.tensor_tensor(KVG[:, tt, 0:3 * D], (SB[1], PA)[tt][:, 0:3 * D], Bkvg, ALU.add).then_inc(sem["kvg_done"], 1)
                dve.wait_ge(sem["kvg_done"], count("kvg_done", b, TT))
                dve.tensor_scalar(uk[:], KVG[:, :, D:2 * D], 0.0, None, ALU.min).then_inc(sem["k1_min"], 1)

            def lin_keys(b):
                dve.wait_ge(sem["q1_exp"], count("q1_exp", b, 2))
                dve.wait_ge(sem["lin_psum"], count("lin_psum", b - 1, 1))
                dve.tensor_tensor(qf[:], pq[:], eq[:], ALU.add).then_inc(sem["q1_done"], 1)
                dve.wait_ge(sem["kg_exp"], count("kg_exp", b, 1))
                dve.scalar_tensor_tensor(out=kf[:], in0=KVG[:, :, D:2 * D], scalar=0.0, in1=ek[:],
                                         op0=ALU.max, op1=ALU.add).then_inc(sem["k1_done"], 1)

            def lin_blocks(b):
                dve.wait_ge(sem["kv_psum"], count("kv_psum", b, 1))
                dve.wait_ge(sem["lin_psum"], count("lin_psum", b - 1, 1))
                dve.tensor_tensor(BD[:, 0:D], PA[:, 0:D], bmask, ALU.mult).then_inc(sem["kv_blocks"], 1)
                dve.tensor_scalar(BD[:, D:D + HEADS], bmask[:, ::DH], PA[:, D:D + 1], None,
                                  ALU.mult).then_inc(sem["kv_blocks"], 1)

            def lin_gate_inverse(b):
                dve.wait_ge(sem["kg_exp"], count("kg_exp", b, 2))
                dve.tensor_scalar(both(sg[:]), both(eg[:]), 1.0, None, ALU.add).then_inc(sem["gate1_done"], 1)
                dve.wait_ge(sem["gate1_done"], count("gate1_done", b, 1))
                dve.reciprocal(both(sg[:]), both(sg[:])).then_inc(sem["gate1_done"], 1)

            def lin_gate(b):
                read = PA[:].rearrange("p (a c) -> p a c", a=TT)
                dve.wait_ge(sem["lin_psum"], count("lin_psum", b, 1))
                dve.tensor_scalar(den1[:], read[:, :, D:D + HEADS], 1e-6, None, ALU.add).then_inc(sem["lin_gated"], 1)
                dve.wait_ge(sem["gate1_done"], count("gate1_done", b, 2))
                dve.wait_ge(sem["linT_psum"], count("linT_psum", b - 1, 1))
                dve.tensor_tensor(gnum[:], read[:, :, 0:D], sg[:], ALU.mult).then_inc(sem["lin_gated"], 1)
                dve.wait_ge(sem["lin_gated"], count("lin_gated", b, 1))
                dve.reciprocal(den1[:], den1[:]).then_inc(sem["lin_gated"], 1)
                dve.wait_ge(sem["lin_gated"], count("lin_gated", b, 3))
                for tt in range(TT):
                    dve.tensor_tensor(go[:, tt].rearrange("p (h d) -> p h d", h=HEADS),
                                      gnum[:, tt].rearrange("p (h d) -> p h d", h=HEADS),
                                      den1[:, tt][:, :, None].broadcast_to([P, HEADS, DH]),
                                      ALU.mult).then_inc(sem["lin_gated"], 1)

            def lin_norm(b):
                dve.wait_ge(sem["linout_psum"], count("linout_psum", b, 1))
                dve.wait_ge(sem["xob_done"], count("xob_done", b, 1))
                dve.tensor_tensor(both(yC[:]), SA[0][:, T:2 * T], both(xob[:]), ALU.add).then_inc(sem["lin_norm"], 1)
                dve.wait_ge(sem["lin_norm"], count("lin_norm", b, 1))
                statistics(b, "lin_norm", 1, yC, statC, mvC, LN_EPS)

            def lin_norm_end(b):
                dve.wait_ge(sem["lin_power"], count("lin_power", b, 1))
                dve.wait_ge(sem["x3T_psum"], count("x3T_psum", b - 1, 1))
                normalize(x3, yC, mvC, rsC, "x3_done")

            def router1_low(b):
                dve.wait_ge(sem["x3T_high"], count("x3T_high", b, 2))
                dve.wait_ge(sem["hid1_psum"], count("hid1_psum", b - 1, EXPERTS))
                dve.tensor_tensor(x3L[:], SA[1][:, 0:T], x3H[:].bitcast(F32), ALU.subtract).then_inc(sem["x3T_low"], 1)

            def router1_pick(b):
                pick_two(b, "gate1_psum", SA[1], None, lg1, top1, ix1, ixf1, "pick1")
                dve.tensor_tensor(dl1[:], top1[:, :, 1:2], top1[:, :, 0:1], ALU.subtract).then_inc(sem["pick1"], 1)
                dve.wait_ge(sem["pick1"], count("pick1", b, 5))
                dve.tensor_copy(both(ixf1[:]), both(ix1[:])).then_inc(sem["pick1"], 1)

            def router1_weights(b):
                dve.wait_ge(sem["pick1_exp"], count("pick1_exp", b, 1))
                dve.tensor_scalar(s1[:], e1[:], 1.0, None, ALU.add).then_inc(sem["weight1"], 1)
                dve.wait_ge(sem["weight1"], count("weight1", b, 1))
                dve.reciprocal(w1[:, :, 0:1], s1[:]).then_inc(sem["weight1"], 1)
                dve.wait_ge(sem["weight1"], count("weight1", b, 2))
                dve.tensor_tensor(w1[:, :, 1:2], e1[:], w1[:, :, 0:1], ALU.mult).then_inc(sem["weight1"], 1)
                dve.wait_ge(sem["weight1"], count("weight1", b, 3))
                dve.wait_ge(sem["pick1"], count("pick1", b, 7))
                for r in range(2):
                    for tt in range(TT):
                        dve.tensor_scalar(ohw[:, r, tt], iota, ixf1[:, tt, r:r + 1], w1[:, tt, r:r + 1],
                                          ALU.is_equal, ALU.mult).then_inc(sem["weight1"], 1)
                dve.wait_ge(sem["weight1"], count("weight1", b, 7))
                dve.wait_ge(sem["weightsT_psum"], count("weightsT_psum", b - 1, 1))
                dve.tensor_tensor(wE[:], ohw[:, 0], ohw[:, 1], ALU.add).then_inc(sem["weights_done"], 1)

            def gelu_low(b, e):
                dve.wait_ge(sem["hid1_high"], count("hid1_high", b, e + 1))
                dve.tensor_tensor(hL[:, e % HRING], gf[:, e % GRING], hH[:, e % HRING].bitcast(F32),
                                  ALU.subtract).then_inc(sem["hid1_low_even"], 1)

            def expert_sums(b, k):
                dve.wait_ge(sem["out1T_psum"], count("out1T_psum", b, k + 1))
                if only(b, 0):
                    dve.wait_ge(sem["raw_split"], 4)
                for tt in range(TT):
                    dve.tensor_tensor(V[:, tt, 2 * k:2 * k + 2],
                                      SB[k % 2][:, tt * T:(tt + 1) * T].rearrange("p (e d) -> p e d", e=2),
                                      x3[:, tt][:, None, :].broadcast_to([P, 2, D]),
                                      ALU.add).then_inc(sem["expert_sum"], 1)

            def expert_stats(b, k):
                dve.wait_ge(sem["expert_sum"], count("expert_sum", b, 2 * (k // 2 + 1)))
                for tt in range(TT):
                    dve.bn_stats(statD[:, tt * EXPERTS + k], V[:, tt, k]).then_inc(sem["expert_norm"], 1)

            def expert_scales(b):
                dve.wait_ge(sem["expert_norm"], count("expert_norm", b, 16))
                me, mo, ve, vo = (statD[:, :, k] for k in (1, 4, 2, 5))
                dve.tensor_tensor(smD[:], me, mo, ALU.add).then_inc(sem["expert_norm"], 1)
                dve.tensor_tensor(dfD[:], me, mo, ALU.subtract).then_inc(sem["expert_norm"], 1)
                dve.scalar_tensor_tensor(out=qdD[:], in0=ve, scalar=D * LN_EPS_EXPERT, in1=vo, op0=ALU.add,
                                         op1=ALU.add).then_inc(sem["expert_norm"], 1)
                dve.wait_ge(sem["expert_norm"], count("expert_norm", b, 19))
                dve.scalar_tensor_tensor(out=ddD[:], in0=dfD[:], scalar=0.25, in1=dfD[:], op0=ALU.mult,
                                         op1=ALU.mult).then_inc(sem["expert_norm"], 1)
                dve.wait_ge(sem["expert_norm"], count("expert_norm", b, 20))
                dve.scalar_tensor_tensor(out=vrD[:], in0=qdD[:], scalar=1.0 / D, in1=ddD[:], op0=ALU.mult,
                                         op1=ALU.add).then_inc(sem["expert_norm"], 1)

            def expert_scales_end(b):
                dve.wait_ge(sem["expert_power"], count("expert_power", b, 1))
                dve.wait_ge(sem["weights_done"], count("weights_done", b, 1))
                dve.tensor_tensor(aD[:], rsD[:], both(wE[:]), ALU.mult).then_inc(sem["expert_norm"], 1)
                dve.wait_ge(sem["expert_norm"], count("expert_norm", b, 22))
                dve.scalar_tensor_tensor(out=cD[:], in0=smD[:], scalar=-0.5, in1=aD[:], op0=ALU.mult,
                                         op1=ALU.mult).then_inc(sem["expert_norm"], 1)

            def expert_totals(b):
                for tt in range(TT):
                    dve.wait_ge(sem["expert_gamma"], count("expert_gamma", b, tt + 1))
                    dve.tensor_reduce(rdD[:, tt], V[:, tt].rearrange("p e d -> p d e"), AX_X, ALU.add).then_inc(sem["expert_total"], 1)

            def last_stats(b):
                dve.wait_ge(sem["beta_psum"], count("beta_psum", b, 1))
                dve.tensor_tensor(both(zD[:]), MI[:, T:2 * T], both(x3[:]), ALU.add).then_inc(sem["last_norm"], 1)

            def last_stats_end(b):
                dve.wait_ge(sem["last_norm"], count("last_norm", b, 1))
                dve.wait_ge(sem["expert_total"], count("expert_total", b, TT))
                dve.tensor_tensor(both(yD[:]), both(zD[:]), both(rdD[:]), ALU.add).then_inc(sem["last_norm"], 1)
                dve.wait_ge(sem["last_norm"], count("last_norm", b, 2))
                statistics(b, "last_norm", 2, yD, statE, mvE, LN_EPS)

            def last_norm(b):
                dve.wait_ge(sem["last_power"], count("last_power", b, 1))
                normalize(res, yD, mvE, rsE, "res_done")

            def turn(t):
                z, l, m, a, n = t - 2, t - 1, t, t + 1, t + 2
                for e in range(EXPERTS):
                    if has(m) and not by_pool(e):
                        relu_low(m, e)
                    if has(a):
                        maximum(a, 2 * e)
                        maximum(a, 2 * e + 1)
                    if has(m) and e == 1:
                        router0_values(m)
                    if has(l):
                        if e == 2:
                            lin_features(l)
                        if e == 4:
                            lin_keys(l)
                        if e == 6:
                            lin_blocks(l)
                    if has(z):
                        if e < 2:
                            expert_stats(z, 4 + 2 * e)
                            expert_stats(z, 5 + 2 * e)
                        if e == 1:
                            expert_scales(z)
                        if e == 3:
                            expert_scales_end(z)
                if only(t, -1):
                    dve.wait_ge(sem["filled"], 6)
                if has(a):
                    negmax(a)
                if has(m):
                    boost(m)
                if has(a):
                    shift(a)
                for e in range(EXPERTS):
                    if has(m):
                        relu_low(m, EXPERTS + e)
                    if has(l):
                        if e == 0:
                            lin_gate_inverse(l)
                        if e == 1:
                            lin_gate(l)
                        if e == 3:
                            lin_norm(l)
                        if e == 4:
                            lin_norm_end(l)
                        if e == 7:
                            router1_low(l)
                    if has(z):
                        if e == 5:
                            expert_totals(z)
                            last_stats_end(z)
                        if e == 6:
                            last_norm(z)
                if has(l):
                    router1_pick(l)
                if has(a):
                    attn_divide(a)
                if has(m):
                    moe0_stats(m)
                if has(l):
                    gelu_low(l, 0)
                if has(a):
                    attn_stats(a)
                if has(m):
                    moe0_norm(m)
                if has(a):
                    attn_norm(a)
                if has(m):
                    moe0_norm_stats(m)
                if has(l):
                    gelu_low(l, 2)
                if has(a):
                    x1_low(a)
                if has(m):
                    moe0_end(m)
                if has(l):
                    router1_weights(l)
                if has(a):
                    router0_pick(a)
                if has(n):
                    qk_low(n)
                if has(l):
                    gelu_low(l, 4)
                    expert_sums(l, 0)
                    expert_stats(l, 0)
                    expert_stats(l, 1)
                if has(n):
                    values(n)
                if has(l):
                    gelu_low(l, 6)
                    expert_sums(l, 1)
                    expert_stats(l, 2)
                    expert_stats(l, 3)
                    expert_sums(l, 2)
                    expert_sums(l, 3)
                    last_stats(l)
                if has(z):
                    dve.wait_ge(sem["stored"], count("stored", z, 16))

            dve.wait_ge(sem["near_consts"], 32)
            dve.wait_ge(sem["filled"], 2)
            qk_low(0)
            values(0)
            dve.wait_ge(sem["consts"], 16 * 2)
            dve.wait_ge(sem["info_high"], 1)
            dve.scalar_tensor_tensor(out=infoW[:], in0=infoW[:].bitcast(F32), scalar=lowr, in1=infoRaw,
                                     op0=ALU.mult, op1=ALU.add).then_inc(sem["info_split"], 1)
            for t in range(-1, 2):
                turn(t)
            with dve.Fori(2, SEQS - 2) as t:
                turn(t)
            for t in range(SEQS - 2, SEQS + 2):
                turn(t)


def kernel(**inputs):
    import numpy as np
    import concourse.bacc as bacc
    from concourse.bass_utils import run_bass_kernel_spmd

    a = {k: np.asarray(v) for k, v in inputs.items()}
    x = a["L0_attn_x"]

    order = np.arange(D).reshape(G, QD, DH).transpose(1, 2, 0).reshape(-1)
    wqkv, bqkv = a["L0_attn_W_qkv"], a["L0_attn_b_qkv"]

    def side_by_side(names, blocks):
        packed = np.zeros((P, sum(n for _, n in names)), np.float32)
        at = 0
        for name, n in names:
            packed[:blocks[name].shape[0], at:at + n] = blocks[name]
            at += n
        return packed

    lowrows = np.zeros((INFO, 1), np.float32)
    lowrows[17] = -1.0
    lowrows[24:] = -1.0
    heads = np.arange(D) // DH
    blocks = {
        "wqk": np.concatenate([wqkv[0:D].T[:, order], wqkv[D:2 * D].T[:, order]], 1),
        "bqk": np.stack([bqkv[0:D][order], bqkv[D:2 * D][order]], 1),
        "wv": wqkv[2 * D:].T, "ident": np.eye(P, dtype=np.float32),
        "wo": a["L0_attn_W_out"].T, "g0w": a["L0_ffn_gate_W"],
        "iota": np.tile(np.arange(EXPERTS, dtype=np.float32), (P, 1)),
        "blockmask": (heads[:, None] == heads[None, :]).astype(np.float32),
        "wq1": a["L1_attn_wq_w"], "bq1": a["L1_attn_wq_b"][:, None],
        "wkvg": np.concatenate([a["L1_attn_wg_w"], a["L1_attn_wk_w"], a["L1_attn_wv_w"]], 1),
        "wout": a["L1_attn_out_w"], "g1w": a["L1_ffn_gate_w"],
        "b1b": a["L1_ffn_b1"].reshape(EXPERTS, HH, P).transpose(2, 0, 1).reshape(P, -1),
        "b2t": a["L1_ffn_b2"].T, "lowrows": lowrows,
    }
    rows = {
        "bv": bqkv[2 * D:], "bo": a["L0_attn_b_out"], "g0b": a["L0_ffn_gate_b"],
        "gam0": a["L0_ffn_ln_gamma"], "bet0": a["L0_ffn_ln_beta"],
        "bkvg": np.concatenate([a["L1_attn_wg_b"], a["L1_attn_wk_b"], a["L1_attn_wv_b"]]),
        "bout": a["L1_attn_out_b"], "lng": a["L1_ffn_ln_g"].reshape(-1),
    }
    info = np.zeros((INFO, NINF), np.float32)
    info[0:EXPERTS, EXPERTS * HID:] = a["L0_ffn_b2"]
    info[INFO - EXPERTS:, EXPERTS * HID:] = a["L0_ffn_b2"]
    for e in range(EXPERTS):
        info[EXPERTS + e, e * HID:(e + 1) * HID] = BIG
    info[16, 0:EXPERTS * HID] = a["L0_ffn_b1"].reshape(-1)
    info[17, 0:EXPERTS * HID] = a["L0_ffn_b1"].reshape(-1)

    def by_input(w):
        return w.transpose(1, 0, 2).reshape(D, -1)

    def by_hidden(w):
        return w.reshape(EXPERTS, HH, P, D).transpose(2, 0, 1, 3).reshape(P, -1)

    sent = {
        "xT": x.transpose(0, 2, 1), "xtok": x.reshape(SEQS, TT, P, D).transpose(0, 2, 1, 3),
        "pack_a": side_by_side(PACK_A, blocks), "pack_b": side_by_side(PACK_B, blocks),
        "row_a": np.concatenate([rows[n] for n, _ in ROW_A]),
        "row_b": np.concatenate([rows[n] for n, _ in ROW_B]),
        "lnb": a["L1_ffn_ln_b"], "info": info,
        "w1a": by_input(a["L0_ffn_W1"]), "w2a": by_hidden(a["L0_ffn_W2"]),
        "w1b": by_input(a["L1_ffn_w1"]), "w2b": by_hidden(a["L1_ffn_w2"]),
    }
    nc = bacc.Bacc("TRN2", target_bir_lowering=False, num_devices=1)
    arrays, args = {}, []
    for name, value in sent.items():
        value = np.ascontiguousarray(value)
        arrays[f"in_{name}"] = value
        args.append(nc.dram_tensor(f"in_{name}", value.shape, mybir.dt.from_np(value.dtype),
                                   kind="ExternalInput").ap())
    args.append(nc.dram_tensor("out_0", (SEQS, P, TT, D), F32, kind="ExternalOutput").ap())
    build(nc, *args)
    r = run_bass_kernel_spmd(nc, [arrays], core_ids=[0])
    got = r.results[0]["out_0"]
    return got.transpose(0, 2, 1, 3).reshape(SEQS, T, D)
```

```python
from contextlib import ExitStack

import concourse.bass as bass
from concourse import mybir

F32 = mybir.dt.float32
F32R = mybir.dt.float32r
U32 = mybir.dt.uint32
ALU = mybir.AluOpType
ACT = mybir.ActivationFunctionType
AX_X = mybir.AxisListType.X

P = 128
D = 128
HEADS = 16
DH = D // HEADS
EXPERTS = 8
HID = 256
PAIRS = EXPERTS // 2
POOL_LOW1 = (1, 3, 4, 5)
POOLED = 3
HH = HID // P
SEQS = 8
T = 256
TT = T // P
G = 4
QD = 4
PIECES = 4
SCALE = 1.0 / float(DH) ** 0.5
BIG = 1.0e30
INFO = 32
LN_EPS = 1e-5
LN_EPS_EXPERT = 1e-6


NINF = EXPERTS * HID + D
PACK_A = [("wqk", 2 * D), ("bqk", 2), ("wv", D), ("ident", P)]
PACK_B = [("wo", D), ("g0w", EXPERTS), ("iota", EXPERTS), ("blockmask", P), ("wq1", D), ("bq1", 1),
          ("wkvg", 3 * D), ("wout", D), ("g1w", EXPERTS), ("b1b", EXPERTS * HH), ("b2t", EXPERTS), ("lowrows", 1)]
ROW_A = [("bv", D)]
ROW_B = [("bo", D), ("g0b", EXPERTS), ("gam0", D), ("bet0", D), ("bkvg", 3 * D), ("bout", D),
         ("lng", EXPERTS * D)]


def build(nc, xT, xtok, pack_a, pack_b, row_a, row_b, lnb, info, w1a, w2a, w1b, w2b, out):
    with ExitStack() as ctx:
        def sb(name, shape, dt=F32):
            return ctx.enter_context(nc.sbuf_tensor(name, shape, dt))

        def bank(name):
            return ctx.enter_context(nc.psum_tensor(name, [P, 512], F32))

        packA = sb("packA", [P, sum(n for _, n in PACK_A)])
        packB = sb("packB", [P, sum(n for _, n in PACK_B)])
        rowA = sb("rowA", [P, sum(n for _, n in ROW_A)])
        rowB = sb("rowB", [P, sum(n for _, n in ROW_B)])
        part = {}
        for tile, names in ((packA, PACK_A), (packB, PACK_B), (rowA, ROW_A), (rowB, ROW_B)):
            at = 0
            for name, n in names:
                part[name] = tile[:, at:at + n]
                at += n
        idn, bmask, iota, lowr = part["ident"], part["blockmask"], part["iota"], part["lowrows"][0:INFO, :]
        Wqk = part["wqk"].rearrange("p (a d) -> p a d", a=2)
        Bqk, Wv, Wo, G0w, Wq1, Bq1 = (part[k] for k in ("bqk", "wv", "wo", "g0w", "wq1", "bq1"))
        Wkvg, Wout, G1w, B2t = part["wkvg"], part["wout"], part["g1w"], part["b2t"]
        B1b = part["b1b"].rearrange("p (e h) -> p e h", e=EXPERTS)
        Bv, Bo, G0b, Gam0, Bet0, Bkvg, Bout = (
            part[k] for k in ("bv", "bo", "g0b", "gam0", "bet0", "bkvg", "bout"))
        Lng = part["lng"].rearrange("p (e d) -> p e d", e=EXPERTS)
        Lnb = sb("Lnb", [EXPERTS, D])
        W1H = [sb(f"W1H{n}", [P, EXPERTS, HID], F32R) for n in range(2)]
        W1L = [sb(f"W1L{n}", [P, EXPERTS, HID], F32R) for n in range(2)]
        W2H = [sb(f"W2H{n}", [P, EXPERTS, HH, D], F32R) for n in range(2)]
        W2L = [sb(f"W2L{n}", [P, EXPERTS, HH, D], F32R) for n in range(2)]
        infoW = sb("infoW", [INFO, NINF], F32R)
        mhalf = sb("mhalf", [P, TT * EXPERTS])
        early = sb("early", [P, 1])

        den = sb("den", [P, TT, D])
        xTs = sb("xTs", [P, T])
        xto = sb("xto", [P, TT, D])
        xb = sb("xb", [P, TT, D])
        qkH = sb("qkH", [P, 2, T], F32R)
        qkL = sb("qkL", [P, 2, T], F32R)
        Qs = sb("Qs", [P, G, T], F32R)
        Km = sb("Km", [P, QD, G, T], F32R)
        Vst = sb("Vst", [P, TT, HEADS, 32])
        mx = sb("mx", [P, G, QD, TT])
        nmH = sb("nmH", [P, G, QD, TT], F32R)
        Mx = sb("Mx", [P, G, TT, P])
        PRING = 8
        Pt = sb("Pt", [P, PRING, TT * T])
        rec = sb("rec", [P, TT, HEADS])
        x1 = sb("x1", [P, TT, D])
        statA = sb("statA", [P, TT, 6])
        mvA = sb("mvA", [P, TT, 2])
        rsA = sb("rsA", [P, TT])
        x1f = sb("x1f", [P, T])
        x1H = sb("x1H", [P, T], F32R)
        x1L = sb("x1L", [P, T], F32R)
        lg0 = sb("lg0", [P, TT, EXPERTS])
        top0 = sb("top0", [P, TT, EXPERTS])
        ix0 = sb("ix0", [P, TT, EXPERTS], U32)
        ixf0 = sb("ixf0", [P, TT, EXPERTS])
        dl0 = sb("dl0", [P, TT, EXPERTS])
        e0 = sb("e0", [P, TT, EXPERTS])
        s0 = sb("s0", [P, TT])
        r0 = sb("r0", [P, TT])
        val0 = sb("val0", [P, TT, 2])
        route = sb("route", [P, TT, 2, INFO])
        rm = sb("rm", [INFO, 2, T], F32R)

        HRING = 4
        hH = sb("hH", [P, HRING, HH * T], F32R)
        hL = sb("hL", [P, HRING, HH * T], F32R)
        x2f = sb("x2f", [P, T])
        x2H = sb("x2H", [P, T], F32R)
        x2L = sb("x2L", [P, T], F32R)
        eo = sb("eo", [P, 2, T])
        f0 = sb("f0", [P, TT, D])
        f1 = sb("f1", [P, TT, D])
        n0 = sb("n0", [P, TT, D])
        ng = sb("ng", [P, TT, D])
        xbet = sb("xbet", [P, TT, D])
        x2 = sb("x2", [P, TT, D])
        statB = sb("statB", [P, 2, TT, 6])
        mvB = sb("mvB", [P, 2, TT, 2])
        rsB = sb("rsB", [P, 2, TT])

        xcf = sb("xcf", [P, T])
        eq = sb("eq", [P, T])
        pq = sb("pq", [P, T])
        qf = sb("qf", [P, T])
        KVG = sb("KVG", [P, TT, 3 * D + 2])
        kf = sb("kf", [P, TT, D])
        den1 = sb("den1", [P, TT, HEADS])
        BD = sb("BD", [P, D + HEADS])
        xob = sb("xob", [P, TT, D])
        x3 = sb("x3", [P, TT, D])
        statC = sb("statC", [P, TT, 6])
        mvC = sb("mvC", [P, TT, 2])
        rsC = sb("rsC", [P, TT])
        x3H = sb("x3H", [P, T], F32R)
        x3L = sb("x3L", [P, T], F32R)
        lg1 = sb("lg1", [P, TT, EXPERTS])
        top1 = sb("top1", [P, TT, EXPERTS])
        ix1 = sb("ix1", [P, TT, EXPERTS], U32)
        ixf1 = sb("ixf1", [P, TT, EXPERTS])
        dl1 = sb("dl1", [P, TT, 1])
        e1 = sb("e1", [P, TT, 1])
        s1 = sb("s1", [P, TT, 1])
        w1 = sb("w1", [P, TT, 2])
        ohw = sb("ohw", [P, 2, TT, EXPERTS])
        wE = sb("wE", [P, TT, EXPERTS])
        wET = sb("wET", [EXPERTS, T])

        GRING = 2
        gf = sb("gf", [P, GRING, HH * T])
        oT1 = sb("oT1", [P, 2, 2 * T])
        V = sb("V", [P, TT, EXPERTS, D])
        statD = sb("statD", [P, TT * EXPERTS, 6])
        smD = sb("smD", [P, TT * EXPERTS])
        dfD = sb("dfD", [P, TT * EXPERTS])
        qdD = sb("qdD", [P, TT * EXPERTS])
        ddD = sb("ddD", [P, TT * EXPERTS])
        vrD = sb("vrD", [P, TT * EXPERTS])
        rsD = sb("rsD", [P, TT * EXPERTS])
        aD = sb("aD", [P, TT * EXPERTS])
        cD = sb("cD", [P, TT * EXPERTS])
        zD = sb("zD", [P, TT, D])
        res = sb("res", [P, TT, D])
        statE = sb("statE", [P, TT, 6])
        mvE = sb("mvE", [P, TT, 2])
        rsE = sb("rsE", [P, TT])

        rawW = V[:].rearrange("p t e d -> p (t e d)")
        infoRaw = Pt[0:INFO].rearrange("p r n -> p (r n)")[:, 0:NINF]
        yA, yB, yC, yD = xb, xbet, xob, zD
        uk, ek, tg = f0, f1, n0
        go, gnum = f0, f1
        gT, x3f = xcf, eq
        Ot = oT1[:].rearrange("p a (b t) -> p (a b) t", b=2)
        AoT, rdD, Ao, uq = x2f, den, ng, eo[:, 1]

        HIGH = [W1H[0][:], W2H[0][:], W1H[1][:], W2H[1][:]]
        LOW = [W1L[0][:], W2L[0][:], W1L[1][:], W2L[1][:]]
        for weights in (HIGH, LOW):
            for k in range(4):
                weights[k] = weights[k].rearrange("p a b -> p (a b)" if k % 2 == 0 else "p a b c -> p (a b c)")

        SA = [bank(f"SA{n}") for n in range(2)]
        SB = [bank(f"SB{n}") for n in range(2)]
        PA = bank("PA")
        Z = [bank(f"Z{n}") for n in range(2)]
        MI = bank("MI")

        stacks = nc.dram_tensor("stacks", [2, QD, PIECES, 32, T], F32)
        q_stack, k_stack = stacks[0], stacks[1]

        sem, per_sequence = {}, {}
        for name, per in (
                ("near_consts", 0), ("consts", 0), ("info_in", 0), ("raw_in", 0), ("raw_high", 0), ("raw_split", 0),
                ("cleared", 0), ("held", 0), ("own_scaled", 0), ("own_gamma", 0), ("km_cleared", 0), ("filled", 0), ("stack_filled", 0), ("info_high", 0), ("info_split", 0),
                ("x_in", 32), ("qk_psum", 1), ("v_psum", 1), ("qk_high", 2), ("qk_low", 2), ("v_done", 2),
                ("stack_out", 16 * 6), ("stack_in", 16 * (1 + QD)), ("xb_done", 1),
                ("max_psum", HEADS), ("max_done", HEADS), ("negmax", 6), ("negmax_psum", 2),
                ("q_shifted", 2), ("exp_psum", HEADS), ("exp_done", HEADS), ("pv_psum", G),
                ("o_copied", 2), ("o_psum", TT), ("o_inverse", TT), ("o_done", TT), ("oT_psum", 1),
                ("oT_done", 1), ("attn_psum", 1), ("attn_norm", 6), ("attn_power", 1), ("x1_done", TT),
                ("x1T_psum", 1), ("x1T_high", 2), ("x1T_low", 1), ("gate0_psum", 1), ("pick0", 13),
                ("gate0_exp", 1), ("value0", 3), ("route_psum", 1), ("route_done", 1),
                ("hid0_psum", 2 * EXPERTS), ("hid0_high", 2 * EXPERTS), ("hid0_low", 2 * EXPERTS - POOLED), ("hid0_low_pool", POOLED), ("hid0_relu", POOLED),
                ("out0_psum", 2 * EXPERTS), ("out0_copied", 2), ("boosted", 3), ("out0T_psum", 1),
                ("moe0_norm", 18), ("moe0_power", 2), ("xbet_done", 1), ("x2_done", TT),
                ("x2T_psum", 1), ("x2T_done", 1), ("q1_psum", 1), ("kvg_psum", TT), ("q1_min", 1),
                ("q1_exp", 2), ("q1_done", 1), ("kvg_done", TT), ("k1_min", 1), ("kg_exp", 2),
                ("k1_done", 1), ("kv_psum", 1), ("kv_blocks", 2), ("lin_psum", 1),
                ("lin_gated", 5), ("linT_psum", 1), ("linT_done", 1), ("xob_done", 1),
                ("linout_psum", 1), ("lin_norm", 6), ("lin_power", 1), ("x3_done", TT),
                ("x3T_psum", 1), ("x3T_high", 2), ("x3T_low", 1), ("gate1_psum", 1), ("pick1", 7),
                ("pick1_exp", 1), ("weight1", 7), ("weights_done", 1), ("weightsT_psum", 1),
                ("weightsT_done", 1),
                ("gelu_table", 1), ("hid1_psum", EXPERTS), ("hid1_gelu", 2 * EXPERTS), ("hid1_high", EXPERTS),
                ("hid1_low", EXPERTS - len(POOL_LOW1)), ("hid1_low_pool", len(POOL_LOW1)), ("out1_psum", EXPERTS),
                ("out1_copied", EXPERTS), ("out1T_psum", PAIRS), ("expert_sum", 2 * PAIRS), ("expert_norm", 23), ("expert_power", 1),
                ("expert_scaled", TT * EXPERTS), ("expert_gamma", TT), ("beta_psum", 1),
                ("expert_total", TT), ("last_norm", 7), ("last_power", 1), ("res_done", TT),
                ("stored", 16)):
            sem[name] = ctx.enter_context(nc.semaphore(name))
            per_sequence[name] = per

        def count(name, b, step):
            value = b * per_sequence[name] + step
            return max(value, 0) if isinstance(value, int) else value

        def has(b):
            return not isinstance(b, int) or 0 <= b < SEQS

        def only(t, turn):
            return isinstance(t, int) and t == turn

        def low1(e):
            if e in POOL_LOW1:
                return "hid1_low_pool", POOL_LOW1.index(e) + 1
            return "hid1_low", e + 1 - sum(k < e for k in POOL_LOW1)

        def slot_heads(e):
            return range((3 * e + 1) // 2, (3 * e + 4) // 2)

        def max_bank(h):
            return SA[h % 2 if h < 12 else 1]

        def by_pool(n):
            return n < EXPERTS - 1 and n % 2 == 1

        def low0(n):
            if by_pool(n):
                return "hid0_low_pool", n // 2 + 1
            return "hid0_low", n // 2 + 1 if n < EXPERTS - 1 else n + 1 - POOLED

        def both(t):
            return t.rearrange("p a b -> p (a b)")

        block = ctx.enter_context(nc.Block())

        @block.sync
        def _(sp):
            def load_x(b):
                sp.wait_ge(sem["qk_psum"], count("qk_psum", b - 1, 1))
                sp.wait_ge(sem["v_psum"], count("v_psum", b - 1, 1))
                sp.wait_ge(sem["xb_done"], count("xb_done", b - 1, 1))
                sp.dma_start(xTs[:], xT[b]).then_inc(sem["x_in"], 16)
                sp.dma_start(xto[:], xtok[b]).then_inc(sem["x_in"], 16)

            def stack(b):
                sp.wait_ge(sem["stack_in"], count("stack_in", b - 1, 16 * (1 + QD)))
                sp.wait_ge(sem["qk_high"], count("qk_high", b, 2))
                for r in (0, 2):
                    sp.dma_start(q_stack[:, r], qkH[:, 0].bitcast(F32)).then_inc(sem["stack_out"], 16)
                for r in (0, 1):
                    sp.dma_start(k_stack[:, r], qkH[:, 1].bitcast(F32)).then_inc(sem["stack_out"], 16)
                sp.wait_ge(sem["qk_low"], count("qk_low", b, 2))
                sp.dma_start(q_stack[:, 1], qkL[:, 0].bitcast(F32)).then_inc(sem["stack_out"], 16)
                sp.dma_start(k_stack[:, 2], qkL[:, 1].bitcast(F32)).then_inc(sem["stack_out"], 16)
                sp.wait_ge(sem["stack_out"], count("stack_out", b, 16 * 6))
                sp.wait_ge(sem["exp_psum"], count("exp_psum", b - 1, HEADS))
                sp.dma_start(Qs[:].rearrange("p g t -> p (g t)").bitcast(F32),
                             q_stack.rearrange("i r (d g) t -> (i r d) (g t)", g=G)).then_inc(sem["stack_in"], 16)
                for i in range(QD):
                    sp.dma_start(Km[32 * i:32 * i + 32, i].rearrange("p g t -> p (g t)").bitcast(F32),
                                 k_stack[i].rearrange("r (d g) t -> (r d) (g t)", g=G)).then_inc(sem["stack_in"], 16)

            def store(b):
                sp.wait_ge(sem["res_done"], count("res_done", b, TT))
                sp.dma_start(out[b], res[:]).then_inc(sem["stored"], 16)

            sp.dma_start(packA[:], pack_a).then_inc(sem["near_consts"], 16)
            load_x(0)
            sp.dma_start(rowA[:], row_a[None, :].broadcast_to([P, row_a.shape[0]])).then_inc(sem["near_consts"], 16)
            sp.wait_ge(sem["filled"], 1)
            sp.dma_start(q_stack[:, PIECES - 1].rearrange("i (a b) t -> i a (b t)", a=8),
                         Km[0:32, QD - 1].rearrange("p g t -> p (g t)").bitcast(F32)).then_inc(sem["stack_filled"], 16)
            sp.dma_start(k_stack[:, PIECES - 1].rearrange("i (a b) t -> i a (b t)", a=8),
                         Mx[0:32].rearrange("p g a b -> p (g a b)")).then_inc(sem["stack_filled"], 16)
            sp.wait_ge(sem["stack_filled"], 16 * 2)
            sp.wait_ge(sem["km_cleared"], 1)
            stack(0)
            load_x(1)
            for n, source in enumerate((w2a, w1b)):
                sp.wait_ge(sem["raw_split"], n + 1)
                sp.dma_start(rawW, source).then_inc(sem["raw_in"], 16)
            stack(1)
            sp.wait_ge(sem["raw_split"], 3)
            sp.dma_start(rawW, w2b).then_inc(sem["raw_in"], 16)
            sp.dma_start(Lnb[:], lnb).then_inc(sem["raw_in"], 16)
            load_x(2)
            stack(2)
            load_x(3)
            stack(3)
            with sp.Fori(2, SEQS - 2) as t:
                load_x(t + 2)
                store(t - 2)
                stack(t + 2)
            for b in range(SEQS - 4, SEQS):
                store(b)
            sp.wait_ge(sem["stored"], 16 * SEQS)

        @block.gpsimd
        def _(pool):
            pool.memset(Mx[:].rearrange("p g a b -> p (g a b)"), 1.0).then_inc(sem["cleared"], 1)
            pool.wait_ge(sem["cleared"], 1)
            pool.memset(Km[:, QD - 1].rearrange("p g t -> p (g t)").bitcast(F32), 0.0).then_inc(sem["filled"], 1)
            pool.memset(Km[:, 0:QD - 1].rearrange("p i g t -> p (i g t)").bitcast(F32),
                        0.0).then_inc(sem["km_cleared"], 1)
            pool.memset(Vst[:].rearrange("p a b c -> p (a b c)"), 0.0).then_inc(sem["cleared"], 1)
            pool.memset(route[:].rearrange("p a b c -> p (a b c)"), 0.0).then_inc(sem["cleared"], 1)
            pool.wait_ge(sem["cleared"], 3)
            pool.memset(Vst[:, :, :, DH:DH + 1], 1.0).then_inc(sem["filled"], 1)
            pool.memset(route[:, :, :, 16:18], 1.0).then_inc(sem["filled"], 1)
            pool.memset(mhalf[:], -0.5).then_inc(sem["filled"], 1)
            pool.memset(KVG[:, :, 3 * D:3 * D + 2], 1.0).then_inc(sem["filled"], 1)
            pool.wait_ge(sem["stack_filled"], 16 * 2)
            pool.memset(Mx[:].rearrange("p g a b -> p (g a b)"), 0.0).then_inc(sem["filled"], 1)

            def split_low(k):
                pool.wait_ge(sem["raw_high"], k + 1)
                pool.tensor_tensor(LOW[k], rawW, HIGH[k].bitcast(F32), ALU.subtract).then_inc(sem["raw_split"], 1)

            def gelu_low(b, e):
                pool.wait_ge(sem["hid1_high"], count("hid1_high", b, e + 1))
                pool.tensor_tensor(hL[:, e % HRING], gf[:, e % GRING], hH[:, e % HRING].bitcast(F32),
                                   ALU.subtract).then_inc(sem["hid1_low_pool"], 1)

            def relu_low(b, n):
                k = n // 2
                pool.wait_ge(sem["hid0_high"], count("hid0_high", b, n + 1))
                pool.tensor_tensor(hL[:, n % HRING], gf[:, k % GRING], hH[:, n % HRING].bitcast(F32),
                                   ALU.subtract).then_inc(sem["hid0_low_pool"], 1)

            def power(target, variance, name):
                pool.tensor_tensor(target, variance, mhalf[:, 0:variance.shape[1]], ALU.pow).then_inc(sem[name], 1)

            def lin_power(b):
                pool.wait_ge(sem["lin_norm"], count("lin_norm", b, 6))
                pool.wait_ge(sem["x3_done"], count("x3_done", b - 1, TT))
                power(rsC[:], mvC[:, :, 1], "lin_power")

            def moe0_norm(b):
                pool.wait_ge(sem["moe0_power"], count("moe0_power", b, 1))
                pool.sem_inc(sem["held"], 1)
                for tt in range(TT):
                    pool.tensor_scalar(n0[:, tt], f1[:, tt], mvB[:, 0, tt, 0:1], rsB[:, 0, tt:tt + 1],
                                       ALU.subtract, ALU.mult).then_inc(sem["moe0_norm"], 1)
                pool.wait_ge(sem["moe0_norm"], count("moe0_norm", b, 11))
                if has(b + 1):
                    pool.wait_ge(sem["oT_psum"], count("oT_psum", b + 1, 1))
                pool.tensor_tensor(ng[:], n0[:], Gam0[:, None, :].broadcast_to([P, TT, D]),
                                   ALU.mult).then_inc(sem["moe0_norm"], 1)
                pool.wait_ge(sem["moe0_norm"], count("moe0_norm", b, 12))
                pool.wait_ge(sem["xbet_done"], count("xbet_done", b, 1))
                pool.tensor_tensor(yB[:], ng[:], xbet[:], ALU.add).then_inc(sem["moe0_norm"], 1)

            def turn(t):
                z, l, m, a = t - 2, t - 1, t, t + 1
                if only(t, -1):
                    split_low(0)
                    pool.wait_ge(sem["consts"], 16 * 2)
                if has(a):
                    pool.wait_ge(sem["x_in"], count("x_in", a, 32))
                    pool.wait_ge(sem["x1_done"], count("x1_done", a - 1, TT))
                    pool.tensor_tensor(xb[:], xto[:], Bo[:, None, :].broadcast_to([P, TT, D]),
                                       ALU.add).then_inc(sem["xb_done"], 1)
                if only(t, -1):
                    split_low(1)
                    split_low(2)
                if has(l):
                    pool.wait_ge(sem["x2_done"], count("x2_done", l, TT))
                    pool.wait_ge(sem["x3_done"], count("x3_done", l - 1, TT))
                    pool.tensor_tensor(xob[:], x2[:], Bout[:, None, :].broadcast_to([P, TT, D]),
                                       ALU.add).then_inc(sem["xob_done"], 1)
                if has(m):
                    relu_low(m, 1)
                    pool.wait_ge(sem["x1_done"], count("x1_done", m, TT))
                    pool.wait_ge(sem["x2_done"], count("x2_done", m - 1, TT))
                    pool.tensor_tensor(xbet[:], x1[:], Bet0[:, None, :].broadcast_to([P, TT, D]),
                                       ALU.add).then_inc(sem["xbet_done"], 1)
                if has(z):
                    pool.wait_ge(sem["expert_norm"], count("expert_norm", z, 21))
                    power(rsD[:], vrD[:], "expert_power")
                if has(m):
                    relu_low(m, 3)
                if has(z):
                    pool.wait_ge(sem["expert_norm"], count("expert_norm", z, 23))
                    pool.sem_inc(sem["held"], 1)
                    for n in range(EXPERTS * only(t, SEQS + 1), TT * EXPERTS):
                        tt, e = divmod(n, EXPERTS)
                        if n == 6 and has(m):
                            relu_low(m, 5)
                        pool.tensor_scalar(V[:, tt, e], V[:, tt, e], aD[:, n:n + 1], cD[:, n:n + 1],
                                           ALU.mult, ALU.add).then_inc(sem["expert_scaled"], 1)
                elif has(m):
                    relu_low(m, 5)
                if only(t, 0):
                    split_low(3)
                if has(z):
                    for tt in range(only(t, SEQS + 1), TT):
                        if tt == 1 and has(l) and not has(m):
                            lin_power(l)
                        scaled = (tt + 1 - only(t, SEQS + 1)) * EXPERTS
                        pool.wait_ge(sem["expert_scaled"], count("expert_scaled", z, scaled))
                        pool.tensor_tensor(V[:, tt], V[:, tt], Lng, ALU.mult).then_inc(sem["expert_gamma"], 1)
                if has(l) and has(m):
                    lin_power(l)
                if has(z):
                    pool.wait_ge(sem["last_norm"], count("last_norm", z, 7))
                    power(rsE[:], mvE[:, :, 1], "last_power")
                if has(m):
                    pool.wait_ge(sem["moe0_norm"], count("moe0_norm", m, 9))
                    pool.wait_ge(sem["moe0_norm"], count("moe0_norm", m - 1, 11))
                    power(rsB[:, 0], mvB[:, 0, :, 1], "moe0_power")
                if has(l):
                    gelu_low(l, 1)
                if has(a):
                    pool.wait_ge(sem["attn_norm"], count("attn_norm", a, 6))
                    pool.wait_ge(sem["x1_done"], count("x1_done", a - 1, TT))
                    power(rsA[:], mvA[:, :, 1], "attn_power")
                if has(m):
                    moe0_norm(m)
                if has(l):
                    gelu_low(l, POOL_LOW1[1])
                if has(m):
                    pool.wait_ge(sem["moe0_norm"], count("moe0_norm", m, 18))
                    pool.wait_ge(sem["x2_done"], count("x2_done", m - 1, TT))
                    power(rsB[:, 1], mvB[:, 1, :, 1], "moe0_power")
                if has(l):
                    for e in POOL_LOW1[2:]:
                        gelu_low(l, e)

            for t in range(-1, 2):
                turn(t)
            with pool.Fori(2, SEQS - 2) as t:
                turn(t)
            for t in range(SEQS - 2, SEQS + 2):
                turn(t)

        @block.scalar
        def _(act):
            def qk_high(b):
                act.wait_ge(sem["qk_psum"], count("qk_psum", b, 1))
                act.wait_ge(sem["stack_out"], count("stack_out", b - 1, 16 * 6))
                for a in range(2):
                    act.activation(qkH[:, a], MI[:, a * T:(a + 1) * T], ACT.Identity,
                                   bias=Bqk[:, a:a + 1]).then_inc(sem["qk_high"], 1)

            def attn_exp(b, h):
                act.wait_ge(sem["exp_psum"], count("exp_psum", b, h + 1))
                if h < PRING:
                    act.wait_ge(sem["pv_psum"], count("pv_psum", b - 1, (HEADS - PRING + h) // QD + 1))
                else:
                    act.wait_ge(sem["pv_psum"], count("pv_psum", b, (h - PRING) // QD + 1))
                act.activation(Pt[:, h % PRING], SB[h % 2][:], ACT.Exp, scale=SCALE).then_inc(sem["exp_done"], 1)

            def o_copy(b, j):
                act.wait_ge(sem["pv_psum"], count("pv_psum", b, 2 * j + 2))
                act.wait_ge(sem["o_psum"], count("o_psum", b - 1, TT))
                act.wait_ge(sem["out1T_psum"], count("out1T_psum", b - 3, PAIRS))
                act.activation(Ot[:, 2 * j:2 * j + 2].rearrange("p g t -> p (g t)"), PA[:],
                               ACT.Identity).then_inc(sem["o_copied"], 1)

            def relu_high(b, n):
                act.wait_ge(sem["hid0_psum"], count("hid0_psum", b, n + 1))
                if by_pool(n):
                    k = n // 2
                    if k >= GRING:
                        act.wait_ge(sem["hid0_low_pool"], count("hid0_low_pool", b, k - GRING + 1))
                    else:
                        low, step = low1(EXPERTS - GRING + k)
                        act.wait_ge(sem[low], count(low, b - 2, step))
                    act.activation(gf[:, k % GRING], Z[n % 2][:], ACT.Relu).then_inc(sem["hid0_relu"], 1)
                    act.wait_ge(sem["hid0_relu"], count("hid0_relu", b, k + 1))
                if n >= HRING:
                    act.wait_ge(sem["out0_psum"], count("out0_psum", b, n - HRING + 1))
                else:
                    act.wait_ge(sem["out1_psum"], count("out1_psum", b - 2, EXPERTS - HRING + n + 1))
                if by_pool(n):
                    act.activation(hH[:, n % HRING], gf[:, k % GRING], ACT.Identity).then_inc(sem["hid0_high"], 1)
                else:
                    act.activation(hH[:, n % HRING], Z[n % 2][:], ACT.Relu).then_inc(sem["hid0_high"], 1)

            def out_copy(b, r):
                act.wait_ge(sem["out0_psum"], count("out0_psum", b, (r + 1) * EXPERTS))
                if r == 0:
                    act.wait_ge(sem["boosted"], count("boosted", b, 2))
                act.wait_ge(sem["out0T_psum"], count("out0T_psum", b - 1, 1))
                act.activation(eo[:, r], MI[:, 0:T], ACT.Identity).then_inc(sem["out0_copied"], 1)

            def gelu(b, e):
                act.wait_ge(sem["hid1_psum"], count("hid1_psum", b, e + 1))
                if e >= GRING:
                    low, step = low1(e - GRING)
                    act.wait_ge(sem[low], count(low, b, step))
                elif has(b + 1):
                    act.wait_ge(sem["hid0_low_pool"], count("hid0_low_pool", b + 1, POOLED))
                else:
                    low, step = low1(EXPERTS - GRING + e)
                    act.wait_ge(sem[low], count(low, b - 1, step))
                for hh in range(HH):
                    act.activation(gf[:, e % GRING, hh * T:(hh + 1) * T], Z[e % 2][:, hh * T:(hh + 1) * T],
                                   ACT.Gelu, bias=B1b[:, e, hh:hh + 1]).then_inc(sem["hid1_gelu"], 1)

            def gelu_high(b, e):
                act.wait_ge(sem["hid1_gelu"], count("hid1_gelu", b, 2 * e + 2))
                if e >= HRING:
                    act.wait_ge(sem["out1_psum"], count("out1_psum", b, e - HRING + 1))
                elif has(b + 1):
                    act.wait_ge(sem["out0_psum"], count("out0_psum", b + 1, 2 * EXPERTS - HRING + e + 1))
                else:
                    act.wait_ge(sem["out1_psum"], count("out1_psum", b - 1, EXPERTS - HRING + e + 1))
                act.activation(hH[:, e % HRING], gf[:, e % GRING], ACT.Identity).then_inc(sem["hid1_high"], 1)

            def out1_copy(b, e):
                act.wait_ge(sem["out1_psum"], count("out1_psum", b, e + 1))
                if e >= 4:
                    act.wait_ge(sem["out1T_psum"], count("out1T_psum", b, e // 2 - 1))
                elif has(b + 2):
                    act.wait_ge(sem["o_psum"], count("o_psum", b + 2, TT))
                else:
                    act.wait_ge(sem["out1T_psum"], count("out1T_psum", b - 1, PAIRS - 1 + e // 2))
                act.activation(oT1[:, e // 2 % 2, (e % 2) * T:(e % 2 + 1) * T], SA[e % 2][:, 0:T], ACT.Identity,
                               bias=B2t[:, e:e + 1]).then_inc(sem["out1_copied"], 1)

            def attn_out(b):
                act.wait_ge(sem["oT_psum"], count("oT_psum", b, 1))
                act.wait_ge(sem["attn_psum"], count("attn_psum", b - 1, 1))
                act.activation(AoT[:], PA[:, 0:T], ACT.Identity).then_inc(sem["oT_done"], 1)

            def router0_in(b):
                act.wait_ge(sem["x1T_psum"], count("x1T_psum", b, 1))
                act.wait_ge(sem["boosted"], count("boosted", b - 1, 3))
                act.wait_ge(sem["hid0_psum"], count("hid0_psum", b - 1, EXPERTS))
                act.activation(x1f[:], PA[:, 0:T], ACT.Identity).then_inc(sem["x1T_high"], 1)
                act.activation(x1H[:], PA[:, 0:T], ACT.Identity).then_inc(sem["x1T_high"], 1)

            def router0_route(b):
                act.wait_ge(sem["route_psum"], count("route_psum", b, 1))
                act.wait_ge(sem["out0_psum"], count("out0_psum", b - 1, 2 * EXPERTS))
                act.activation(both(rm[:]), PA[0:INFO, :], ACT.Identity).then_inc(sem["route_done"], 1)

            def router0_exp(b):
                act.wait_ge(sem["pick0"], count("pick0", b, 6))
                act.wait_ge(sem["value0"], count("value0", b - 1, 3))
                act.activation(both(e0[:]), both(dl0[:]), ACT.Exp).then_inc(sem["gate0_exp"], 1)

            def lin_copy(b):
                act.wait_ge(sem["x2T_psum"], count("x2T_psum", b, 1))
                act.wait_ge(sem["linout_psum"], count("linout_psum", b - 1, 1))
                act.activation(xcf[:], SB[0][:, 0:T], ACT.Identity).then_inc(sem["x2T_done"], 1)

            def lin_queries(b):
                act.wait_ge(sem["q1_min"], count("q1_min", b, 1))
                act.wait_ge(sem["gate1_psum"], count("gate1_psum", b - 1, 1))
                act.activation(eq[:], uq, ACT.Exp).then_inc(sem["q1_exp"], 1)
                act.activation(pq[:], SB[0][:, T:2 * T], ACT.Relu, bias=Bq1).then_inc(sem["q1_exp"], 1)

            def lin_keys(b):
                act.wait_ge(sem["k1_min"], count("k1_min", b, 1))
                act.activation(both(ek[:]), both(uk[:]), ACT.Exp).then_inc(sem["kg_exp"], 1)
                act.activation(tg[:], KVG[:, :, 0:D], ACT.Tanh, scale=0.5).then_inc(sem["kg_exp"], 1)

            def lin_gated(b):
                act.wait_ge(sem["linT_psum"], count("linT_psum", b, 1))
                act.activation(gT[:], SA[0][:, 0:T], ACT.Identity).then_inc(sem["linT_done"], 1)

            def router1_in(b):
                act.wait_ge(sem["x3T_psum"], count("x3T_psum", b, 1))
                act.wait_ge(sem["hid1_psum"], count("hid1_psum", b - 1, EXPERTS))
                act.activation(x3f[:], SA[1][:, 0:T], ACT.Identity).then_inc(sem["x3T_high"], 1)
                act.activation(x3H[:], SA[1][:, 0:T], ACT.Identity).then_inc(sem["x3T_high"], 1)

            def router1_exp(b):
                act.wait_ge(sem["pick1"], count("pick1", b, 6))
                act.wait_ge(sem["weight1"], count("weight1", b - 1, 3))
                act.activation(e1[:], dl1[:], ACT.Exp).then_inc(sem["pick1_exp"], 1)

            def weights(b):
                act.wait_ge(sem["weightsT_psum"], count("weightsT_psum", b, 1))
                act.wait_ge(sem["beta_psum"], count("beta_psum", b - 1, 1))
                act.activation(wET[:], MI[0:EXPERTS, 0:T], ACT.Identity).then_inc(sem["weightsT_done"], 1)

            def split_high(k):
                act.wait_ge(sem["raw_in"], 16 * (k + 1) if k < 3 else 16 * 5)
                act.activation(HIGH[k], rawW, ACT.Identity).then_inc(sem["raw_high"], 1)

            def turn(t):
                l, m, a, n = t - 1, t, t + 1, t + 2
                if has(m):
                    router0_exp(m)
                for e in range(EXPERTS):
                    if has(m):
                        relu_high(m, e)
                    if has(l):
                        if e == 0:
                            lin_copy(l)
                        if e == 4:
                            lin_queries(l)
                        if e == 5:
                            lin_keys(l)
                    if only(t, -1) and e == 0:
                        split_high(1)
                        split_high(2)
                    if only(t, 0) and e == 4:
                        split_high(3)
                if has(m):
                    out_copy(m, 0)
                if only(t, -1):
                    qk_high(n)
                for e in range(EXPERTS):
                    if has(m):
                        relu_high(m, EXPERTS + e)
                    if has(a):
                        attn_exp(a, 2 * e)
                        attn_exp(a, 2 * e + 1)
                        if e == 6:
                            o_copy(a, 0)
                    if has(l):
                        if e == 2:
                            lin_gated(l)
                        if e == 6:
                            router1_in(l)
                if has(l):
                    router1_exp(l)
                if has(m):
                    out_copy(m, 1)
                if has(l):
                    act.wait_ge(sem["gelu_table"], count("gelu_table", l, 0))
                    act.activation(early[:], mhalf[:, 0:1], ACT.Gelu).then_inc(sem["gelu_table"], 1)
                if has(a):
                    o_copy(a, 1)
                for e in range(EXPERTS):
                    if has(l):
                        gelu(l, e)
                    if e == 3 and has(a):
                        router0_in(a)
                    if has(l):
                        gelu_high(l, e)
                        if e >= 2:
                            out1_copy(l, e - 2)
                    if e == 0 and has(a):
                        attn_out(a)
                    if e == 3 and has(n) and has(m):
                        qk_high(n)
                    if e == 5 and has(a):
                        router0_route(a)
                if has(l):
                    out1_copy(l, EXPERTS - 2)
                    out1_copy(l, EXPERTS - 1)
                if has(l):
                    weights(l)

            act.wait_ge(sem["near_consts"], 32)
            act.dma_start(packB[:], pack_b).then_inc(sem["consts"], 16)
            act.dma_start(rowB[:], row_b[None, :].broadcast_to([P, row_b.shape[0]])).then_inc(sem["consts"], 16)
            act.dma_start(infoRaw, info).then_inc(sem["info_in"], 16)
            act.dma_start(rawW, w1a).then_inc(sem["raw_in"], 16)
            qk_high(0)
            act.wait_ge(sem["info_in"], 16)
            act.activation(infoW[:], infoRaw, ACT.Identity).then_inc(sem["info_high"], 1)
            split_high(0)
            act.wait_ge(sem["info_split"], 1)
            for t in range(-1, 2):
                turn(t)
            with act.Fori(2, SEQS - 2) as t:
                turn(t)
            for t in range(SEQS - 2, SEQS + 2):
                turn(t)

        @block.tensor
        def _(pe):
            def project(b):
                pe.wait_ge(sem["x_in"], count("x_in", b, 32))
                if has(b - 2):
                    pe.wait_ge(sem["moe0_norm"], count("moe0_norm", b - 2, 4))
                else:
                    pe.wait_ge(sem["v_done"], count("v_done", b - 1, 2))
                for a in range(2):
                    last = pe.matmul(MI[:, a * T:(a + 1) * T], Wqk[:, a], xTs[:], start=True, stop=True)
                last.then_inc(sem["qk_psum"], 1)

            def project_values(b):
                pe.wait_ge(sem["qk_low"], count("qk_low", b, 2))
                for tt in range(TT):
                    last = pe.matmul(MI[:, tt * D:(tt + 1) * D], xTs[:, tt * P:(tt + 1) * P], Wv,
                                     start=True, stop=True)
                last.then_inc(sem["v_psum"], 1)

            def max_scores(b, h):
                g, i = divmod(h, QD)
                if h == 0:
                    pe.wait_ge(sem["stack_in"], count("stack_in", b, 16 * (1 + QD)))
                if h < 2:
                    pe.wait_ge(sem["out1_copied"], count("out1_copied", b - 3, EXPERTS))
                else:
                    pe.wait_ge(sem["max_done"], count("max_done", b, h - 1 if h < 12 else h))
                for tt in range(TT):
                    last = pe.matmul(max_bank(h)[:, tt * T:(tt + 1) * T], Qs[:, g, tt * P:(tt + 1) * P],
                                     Km[:, i, g], start=True, stop=True)
                last.then_inc(sem["max_psum"], 1)

            def negmax(b, j):
                pe.wait_ge(sem["negmax"], count("negmax", b, 3 * j + 3))
                pe.wait_ge(sem["max_done"], count("max_done", b, (11, HEADS)[j]))
                for g in (2 * j, 2 * j + 1):
                    for tt in range(TT):
                        at = (g % 2) * T + tt * P
                        last = pe.transpose(SA[j][:, at:at + P], Mx[:, g, tt], idn)
                last.then_inc(sem["negmax_psum"], 1)

            def exp_scores(b, h):
                g, i = divmod(h, QD)
                pe.wait_ge(sem["q_shifted"], count("q_shifted", b, g // 2 + 1))
                if h == 0:
                    pe.wait_ge(sem["q1_exp"], count("q1_exp", b - 2, 2))
                    pe.wait_ge(sem["kvg_done"], count("kvg_done", b - 2, TT))
                if h >= 2:
                    pe.wait_ge(sem["exp_done"], count("exp_done", b, h - 1))
                for kt in range(TT):
                    last = pe.matmul(SB[h % 2][:, kt * T:(kt + 1) * T], Km[:, i, g, kt * P:(kt + 1) * P],
                                     Qs[:, g], start=True, stop=True)
                last.then_inc(sem["exp_psum"], 1)

            def weighted_values(b, g):
                if g == 0:
                    pe.wait_ge(sem["v_done"], count("v_done", b, 2))
                    pe.wait_ge(sem["lin_gated"], count("lin_gated", b - 2, 5))
                if g == 2:
                    pe.wait_ge(sem["o_copied"], count("o_copied", b, 1))
                pe.wait_ge(sem["exp_done"], count("exp_done", b, QD * g + QD))
                for kt in range(TT):
                    for i in range(QD):
                        h = QD * g + i
                        last = pe.matmul(PA[32 * i:32 * i + 32, (g % 2) * T:(g % 2 + 1) * T], Vst[:, kt, h],
                                         Pt[:, h % PRING, kt * T:(kt + 1) * T], start=(kt == 0),
                                         stop=(kt == TT - 1), skip_group_check=True)
                last.then_inc(sem["pv_psum"], 1)

            def attn_turns(b):
                pe.wait_ge(sem["o_copied"], count("o_copied", b, 2))
                pe.wait_ge(sem["exp_done"], count("exp_done", b, HEADS))
                for tt in range(TT):
                    for g in range(G):
                        last = pe.transpose(SB[tt][:, g * P:(g + 1) * P], Ot[:, g, tt * P:(tt + 1) * P], idn)
                    last.then_inc(sem["o_psum"], 1)

            def attn_heads(b):
                pe.wait_ge(sem["o_done"], count("o_done", b, TT))
                for tt in range(TT):
                    last = pe.transpose(PA[:, tt * P:(tt + 1) * P], Ao[:, tt], idn)
                last.then_inc(sem["oT_psum"], 1)

            def attn_out(b):
                pe.wait_ge(sem["oT_done"], count("oT_done", b, 1))
                for tt in range(TT):
                    last = pe.matmul(PA[:, T + tt * D:T + (tt + 1) * D], AoT[:, tt * P:(tt + 1) * P], Wo,
                                     start=True, stop=True)
                last.then_inc(sem["attn_psum"], 1)

            def router0_in(b):
                pe.wait_ge(sem["x1_done"], count("x1_done", b, TT))
                for tt in range(TT):
                    last = pe.transpose(PA[:, tt * P:(tt + 1) * P], x1[:, tt], idn)
                last.then_inc(sem["x1T_psum"], 1)

            def router0_gate(b):
                pe.wait_ge(sem["x1T_high"], count("x1T_high", b, 2))
                pe.wait_ge(sem["x1T_low"], count("x1T_low", b, 1))
                for tt in range(TT):
                    last = pe.matmul(PA[:, tt * EXPERTS:(tt + 1) * EXPERTS], x1f[:, tt * P:(tt + 1) * P], G0w,
                                     start=True, stop=True)
                last.then_inc(sem["gate0_psum"], 1)

            def router0_route(b):
                pe.wait_ge(sem["pick0"], count("pick0", b, 13))
                for r in range(2):
                    for tt in range(TT):
                        at = r * T + tt * P
                        last = pe.transpose(PA[0:INFO, at:at + P], route[:, tt, r], idn)
                last.then_inc(sem["route_psum"], 1)

            def hidden0(b, n):
                r, e = divmod(n, EXPERTS)
                if n == 0:
                    pe.wait_ge(sem["x1T_high"], count("x1T_high", b, 2))
                    pe.wait_ge(sem["x1T_low"], count("x1T_low", b, 1))
                    pe.wait_ge(sem["route_done"], count("route_done", b, 1))
                if n == EXPERTS:
                    pe.wait_ge(sem["boosted"], count("boosted", b, 1))
                if n >= 2:
                    low, step = low0(n - 2)
                    pe.wait_ge(sem[low], count(low, b, step))
                else:
                    pe.wait_ge(sem["hid1_gelu"], count("hid1_gelu", b - 2, 2 * (EXPERTS - 2 + n) + 2))
                high, rest = ((x1H, x1L), (x2H, x2L))[r]
                for hh in range(HH):
                    z = Z[n % 2][:, hh * T:(hh + 1) * T]
                    w = slice(hh * P, (hh + 1) * P)
                    pe.matmul(z, W1H[0][:, e, w], high[:], start=True, stop=False)
                    pe.matmul(z, W1L[0][:, e, w], high[:], start=False, stop=False)
                    at = e * HID + hh * P
                    pe.matmul(z, infoW[:, at:at + P], rm[:, r], start=False, stop=False)
                    if n == EXPERTS and hh == 0:
                        pe.wait_ge(sem["boosted"], count("boosted", b, 3))
                    last = pe.matmul(z, W1H[0][:, e, w], rest[:], start=False, stop=True)
                last.then_inc(sem["hid0_psum"], 1)

            def outs0(b, n):
                r, e = divmod(n, EXPERTS)
                o = MI[:, 0:T]
                if n == 0:
                    pe.wait_ge(sem["last_norm"], count("last_norm", b - 2, 1))
                    if has(b + 1):
                        pe.wait_ge(sem["v_done"], count("v_done", b + 1, 2))
                if e == 0:
                    if r == 1:
                        pe.wait_ge(sem["out0_copied"], count("out0_copied", b, 1))
                    pe.matmul(o, infoW[:, EXPERTS * HID:NINF], rm[:, r], start=True, stop=False)
                pe.wait_ge(sem["hid0_high"], count("hid0_high", b, n + 1))
                for hh in range(HH):
                    h_high = hH[:, n % HRING, hh * T:(hh + 1) * T]
                    pe.matmul(o, W2H[0][:, e, hh], h_high, start=False, stop=False)
                    pe.matmul(o, W2L[0][:, e, hh], h_high, start=False, stop=False)
                if not by_pool(n):
                    outs0_low(b, n)

            def outs0_low(b, n):
                e = n % EXPERTS
                low, step = low0(n)
                pe.wait_ge(sem[low], count(low, b, step))
                for hh in range(HH):
                    last = pe.matmul(MI[:, 0:T], W2H[0][:, e, hh], hL[:, n % HRING, hh * T:(hh + 1) * T],
                                     start=False, stop=(e == EXPERTS - 1 and hh == HH - 1))
                last.then_inc(sem["out0_psum"], 1)

            def moe0_turns(b):
                pe.wait_ge(sem["out0_copied"], count("out0_copied", b, 2))
                for r in range(2):
                    for tt in range(TT):
                        at = (r * TT + tt) * D
                        last = pe.transpose(MI[:, at:at + D], eo[:, r, tt * P:(tt + 1) * P], idn)
                last.then_inc(sem["out0T_psum"], 1)

            def lin_turn(b):
                pe.wait_ge(sem["x2_done"], count("x2_done", b, TT))
                if has(b + 1):
                    pe.wait_ge(sem["o_done"], count("o_done", b + 1, TT))
                pe.wait_ge(sem["expert_sum"], count("expert_sum", b - 1, 2 * PAIRS))
                for tt in range(TT):
                    last = pe.transpose(SB[0][:, tt * P:(tt + 1) * P], x2[:, tt], idn)
                last.then_inc(sem["x2T_psum"], 1)

            def lin_project(b):
                pe.wait_ge(sem["x2T_done"], count("x2T_done", b, 1))
                pe.matmul(SB[0][:, T:2 * T], Wq1, xcf[:], start=True, stop=True).then_inc(sem["q1_psum"], 1)
                for tt in range(TT):
                    pe.matmul((SB[1], PA)[tt][:, 0:3 * D], xcf[:, tt * P:(tt + 1) * P], Wkvg,
                              start=True, stop=True).then_inc(sem["kvg_psum"], 1)

            def lin_kv(b):
                pe.wait_ge(sem["k1_done"], count("k1_done", b, 1))
                pe.wait_ge(sem["kvg_done"], count("kvg_done", b, TT))
                for tt in range(TT):
                    last = pe.matmul(PA[:, 0:D + 1], kf[:, tt], KVG[:, tt, 2 * D:3 * D + 1], start=(tt == 0),
                                     stop=(tt == TT - 1))
                last.then_inc(sem["kv_psum"], 1)

            def lin_read(b):
                pe.wait_ge(sem["kv_blocks"], count("kv_blocks", b, 2))
                pe.wait_ge(sem["q1_done"], count("q1_done", b, 1))
                for tt in range(TT):
                    last = pe.matmul(PA[:, tt * 2 * D:tt * 2 * D + D + HEADS], qf[:, tt * P:(tt + 1) * P], BD[:],
                                     start=True, stop=True)
                last.then_inc(sem["lin_psum"], 1)

            def lin_gated(b):
                pe.wait_ge(sem["lin_gated"], count("lin_gated", b, 5))
                if has(b + 2):
                    pe.wait_ge(sem["q_shifted"], count("q_shifted", b + 2, 1))
                else:
                    pe.wait_ge(sem["out1_copied"], count("out1_copied", b - 1, EXPERTS))
                for tt in range(TT):
                    last = pe.transpose(SA[0][:, tt * P:(tt + 1) * P], go[:, tt], idn)
                last.then_inc(sem["linT_psum"], 1)

            def lin_out(b):
                pe.wait_ge(sem["linT_done"], count("linT_done", b, 1))
                for tt in range(TT):
                    last = pe.matmul(SA[0][:, T + tt * D:T + (tt + 1) * D], gT[:, tt * P:(tt + 1) * P], Wout,
                                     start=True, stop=True)
                last.then_inc(sem["linout_psum"], 1)

            def router1_in(b):
                pe.wait_ge(sem["x3_done"], count("x3_done", b, TT))
                if has(b + 2):
                    pe.wait_ge(sem["q_shifted"], count("q_shifted", b + 2, 2))
                for tt in range(TT):
                    last = pe.transpose(SA[1][:, tt * P:(tt + 1) * P], x3[:, tt], idn)
                last.then_inc(sem["x3T_psum"], 1)

            def router1_gate(b):
                pe.wait_ge(sem["x3T_high"], count("x3T_high", b, 2))
                pe.wait_ge(sem["x3T_low"], count("x3T_low", b, 1))
                for tt in range(TT):
                    last = pe.matmul(SA[1][:, tt * EXPERTS:(tt + 1) * EXPERTS], x3f[:, tt * P:(tt + 1) * P], G1w,
                                     start=True, stop=True)
                last.then_inc(sem["gate1_psum"], 1)

            def weights(b):
                pe.wait_ge(sem["weights_done"], count("weights_done", b, 1))
                if has(b + 3):
                    pe.wait_ge(sem["v_done"], count("v_done", b + 3, 2))
                elif has(b + 1):
                    pe.wait_ge(sem["moe0_norm"], count("moe0_norm", b + 1, 4))
                else:
                    pe.wait_ge(sem["last_norm"], count("last_norm", b - 1, 1))
                for tt in range(TT):
                    last = pe.transpose(MI[0:EXPERTS, tt * P:(tt + 1) * P], wE[:, tt], idn)
                last.then_inc(sem["weightsT_psum"], 1)

            def hidden1(b, e):
                if only(b, 0) and e == 0:
                    pe.wait_ge(sem["raw_split"], 4)
                if e == 0:
                    pe.wait_ge(sem["x3T_high"], count("x3T_high", b, 2))
                    pe.wait_ge(sem["x3T_low"], count("x3T_low", b, 1))
                if e >= 2:
                    pe.wait_ge(sem["hid1_gelu"], count("hid1_gelu", b, 2 * e - 2))
                elif has(b + 1):
                    low, step = low0(2 * EXPERTS - 2 + e)
                    pe.wait_ge(sem[low], count(low, b + 1, step))
                else:
                    pe.wait_ge(sem["hid1_gelu"], count("hid1_gelu", b - 1, 2 * (EXPERTS - 2 + e) + 2))
                for hh in range(HH):
                    z = Z[e % 2][:, hh * T:(hh + 1) * T]
                    w = slice(hh * P, (hh + 1) * P)
                    pe.matmul(z, W1H[1][:, e, w], x3H[:], start=True, stop=False)
                    pe.matmul(z, W1H[1][:, e, w], x3L[:], start=False, stop=False)
                    last = pe.matmul(z, W1L[1][:, e, w], x3H[:], start=False, stop=True)
                last.then_inc(sem["hid1_psum"], 1)

            def outs1(b, e):
                if e == 0:
                    pe.wait_ge(sem["pick1"], count("pick1", b, 1))
                if e >= 2:
                    pe.wait_ge(sem["out1_copied"], count("out1_copied", b, e - 1))
                pe.wait_ge(sem["hid1_high"], count("hid1_high", b, e + 1))
                o = SA[e % 2][:, 0:T]
                for hh in range(HH):
                    h_high = hH[:, e % HRING, hh * T:(hh + 1) * T]
                    pe.matmul(o, W2H[1][:, e, hh], h_high, start=(hh == 0), stop=False)
                    pe.matmul(o, W2L[1][:, e, hh], h_high, start=False, stop=False)
                low, step = low1(e)
                pe.wait_ge(sem[low], count(low, b, step))
                for hh in range(HH):
                    last = pe.matmul(o, W2H[1][:, e, hh], hL[:, e % HRING, hh * T:(hh + 1) * T], start=False,
                                     stop=(hh == HH - 1))
                last.then_inc(sem["out1_psum"], 1)

            def turns1(b, k):
                pe.wait_ge(sem["out1_copied"], count("out1_copied", b, 2 * k + 2))
                if k >= 2:
                    pe.wait_ge(sem["expert_sum"], count("expert_sum", b, 2 * (k - 1)))
                elif has(b + 2):
                    pe.wait_ge(sem["o_done"], count("o_done", b + 2, TT))
                else:
                    pe.wait_ge(sem["expert_sum"], count("expert_sum", b - 1, 2 * PAIRS))
                for tt in range(TT):
                    for e in range(2):
                        c = (2 * tt + e) * D
                        last = pe.transpose(SB[k % 2][:, c:c + D], oT1[:, k % 2, e * T + tt * P:e * T + (tt + 1) * P],
                                            idn)
                last.then_inc(sem["out1T_psum"], 1)

            def beta_sums(b):
                pe.wait_ge(sem["weightsT_done"], count("weightsT_done", b, 1))
                for tt in range(TT):
                    last = pe.matmul(MI[:, T + tt * D:T + (tt + 1) * D], wET[:, tt * P:(tt + 1) * P], Lnb[:],
                                     start=True, stop=True)
                last.then_inc(sem["beta_psum"], 1)

            def turn(t):
                l, m, a, n = t - 1, t, t + 1, t + 2
                for e in range(EXPERTS):
                    if has(m):
                        hidden0(m, e)
                    heads = slot_heads(e)
                    if has(a):
                        max_scores(a, heads[0])
                    if has(m) and e >= 1:
                        if e >= 2 and by_pool(e - 2):
                            outs0_low(m, e - 2)
                        outs0(m, e - 1)
                    if has(a) and len(heads) == 2:
                        max_scores(a, heads[1])
                    if has(l):
                        if e == 0:
                            lin_turn(l)
                        if e == 1:
                            lin_project(l)
                        if e == 6:
                            lin_kv(l)
                if has(m):
                    outs0(m, EXPERTS - 1)
                if only(t, -1):
                    pe.wait_ge(sem["filled"], 6)
                    pe.wait_ge(sem["consts"], 16 * 2)
                if has(a):
                    negmax(a, 0)
                if has(l):
                    lin_read(l)
                if only(t, -1):
                    project(n)
                for e in range(EXPERTS):
                    if has(a) and e < 4:
                        max_scores(a, 12 + e)
                    if has(m):
                        hidden0(m, EXPERTS + e)
                    if has(a):
                        exp_scores(a, 2 * e)
                    if has(m) and e >= 1:
                        outs0(m, EXPERTS + e - 1)
                    if has(a):
                        exp_scores(a, 2 * e + 1)
                        if e == 3:
                            negmax(a, 1)
                        if e in (3, 5, 7):
                            weighted_values(a, (e - 3) // 2)
                    if has(l):
                        if e == 2:
                            lin_gated(l)
                        if e == 3:
                            lin_out(l)
                        if e == 6:
                            router1_in(l)
                        if e == 7:
                            router1_gate(l)
                if has(m):
                    outs0(m, 2 * EXPERTS - 1)
                if has(l):
                    hidden1(l, 0)
                if has(a):
                    weighted_values(a, G - 1)
                if has(l):
                    hidden1(l, 1)
                if has(a):
                    attn_turns(a)
                if has(m):
                    moe0_turns(m)
                if has(l):
                    hidden1(l, 2)
                if has(a):
                    attn_heads(a)
                    attn_out(a)
                for e in range(EXPERTS):
                    if has(l) and 0 < e < EXPERTS - 2:
                        hidden1(l, e + 2)
                    if e == 4 and has(a):
                        router0_route(a)
                    if has(l):
                        if e == EXPERTS - 1:
                            weights(l)
                        outs1(l, e)
                        if e >= 3 and e % 2 == 1:
                            turns1(l, (e - 3) // 2)
                    if e == 1 and has(n) and has(m):
                        project(n)
                    if e == 1 and has(a):
                        router0_in(a)
                    if e == 2 and has(a):
                        router0_gate(a)
                    if e == 4 and has(n):
                        project_values(n)
                if has(l):
                    turns1(l, PAIRS - 1)
                    beta_sums(l)

            pe.wait_ge(sem["near_consts"], 32)
            project(0)
            project_values(0)
            turn(-1)
            pe.wait_ge(sem["info_split"], 1)
            pe.wait_ge(sem["raw_split"], 2)
            turn(0)
            turn(1)
            with pe.Fori(2, SEQS - 2) as t:
                turn(t)
            for t in range(SEQS - 2, SEQS + 2):
                turn(t)

        @block.vector
        def _(dve):
            def qk_low(b):
                dve.wait_ge(sem["qk_high"], count("qk_high", b, 2))
                dve.wait_ge(sem["stack_out"], count("stack_out", b - 1, 16 * 6))
                for a in range(2):
                    dve.scalar_tensor_tensor(out=qkL[:, a], in0=MI[:, a * T:(a + 1) * T],
                                             scalar=Bqk[:, a:a + 1], in1=qkH[:, a].bitcast(F32),
                                             op0=ALU.add, op1=ALU.subtract).then_inc(sem["qk_low"], 1)

            def values(b):
                dve.wait_ge(sem["v_psum"], count("v_psum", b, 1))
                dve.wait_ge(sem["pv_psum"], count("pv_psum", b - 1, G))
                for kt in range(TT):
                    dve.tensor_tensor(Vst[:, kt, :, 0:DH],
                                      MI[:, kt * D:(kt + 1) * D].rearrange("p (h d) -> p h d", h=HEADS),
                                      Bv.rearrange("p (h d) -> p h d", h=HEADS), ALU.add).then_inc(sem["v_done"], 1)

            def maximum(b, h):
                g, i = divmod(h, QD)
                dve.wait_ge(sem["max_psum"], count("max_psum", b, h + 1))
                dve.tensor_reduce(mx[:, g, i], max_bank(h)[:].rearrange("p (q k) -> p q k", q=TT), AX_X, ALU.max).then_inc(sem["max_done"], 1)

            def negmax(b, j):
                g = slice(2 * j, 2 * j + 2)
                at = Mx[:, g].rearrange("p g q (i c) -> p g i q c", c=32)
                dve.wait_ge(sem["max_done"], count("max_done", b, 8 * j + 8))
                dve.wait_ge(sem["negmax_psum"], count("negmax_psum", b - 1, 2))
                dve.tensor_scalar(nmH[:, g].rearrange("p g i q -> p (g i q)"),
                                  mx[:, g].rearrange("p g i q -> p (g i q)"), -1.0, None,
                                  ALU.mult).then_inc(sem["negmax"], 1)
                dve.tensor_scalar(at[:, :, :, :, 24], mx[:, g], -1.0, None, ALU.mult).then_inc(sem["negmax"], 1)
                dve.wait_ge(sem["negmax"], count("negmax", b, 3 * j + 2))
                dve.tensor_tensor(at[:, :, :, :, 25], at[:, :, :, :, 24], nmH[:, g].bitcast(F32),
                                  ALU.subtract).then_inc(sem["negmax"], 1)

            def shift(b, j):
                dve.wait_ge(sem["negmax_psum"], count("negmax_psum", b, j + 1))
                q = Qs[:, 2 * j:2 * j + 2].rearrange("p g t -> p (g t)")
                dve.tensor_tensor(q, SA[j][:], q.bitcast(F32), ALU.add).then_inc(sem["q_shifted"], 1)

            def attn_divide(b):
                for tt in range(TT):
                    o = SB[tt][:].rearrange("p (h c) -> p h c", c=32)
                    dve.wait_ge(sem["o_psum"], count("o_psum", b, tt + 1))
                    dve.reciprocal(rec[:, tt], o[:, :, DH]).then_inc(sem["o_inverse"], 1)
                    dve.wait_ge(sem["o_inverse"], count("o_inverse", b, tt + 1))
                    dve.wait_ge(sem["oT_psum"], count("oT_psum", b - 1, 1))
                    dve.tensor_tensor(Ao[:, tt].rearrange("p (h d) -> p h d", h=HEADS), o[:, :, 0:DH],
                                      rec[:, tt][:, :, None].broadcast_to([P, HEADS, DH]), ALU.mult).then_inc(sem["o_done"], 1)

            def statistics(b, name, step, y, stat, mv, eps):
                for tt in range(TT):
                    dve.bn_stats(stat[:, tt], y[:, tt]).then_inc(sem[name], 1)
                dve.wait_ge(sem[name], count(name, b, step + 2))
                dve.sem_inc(sem["held"], 1)
                for tt in range(TT):
                    dve.bn_aggr(mv[:, tt], stat[:, tt]).then_inc(sem[name], 1)
                dve.wait_ge(sem[name], count(name, b, step + 4))
                dve.tensor_scalar(mv[:, :, 1], mv[:, :, 1], eps, None, ALU.add).then_inc(sem[name], 1)

            def normalize(target, y, mv, rs, name):
                for tt in range(TT):
                    dve.tensor_scalar(target[:, tt], y[:, tt], mv[:, tt, 0:1], rs[:, tt:tt + 1],
                                      ALU.subtract, ALU.mult).then_inc(sem[name], 1)

            def attn_stats(b):
                dve.wait_ge(sem["attn_psum"], count("attn_psum", b, 1))
                dve.wait_ge(sem["xb_done"], count("xb_done", b, 1))
                dve.tensor_tensor(both(yA[:]), PA[:, T:2 * T], both(xb[:]), ALU.add).then_inc(sem["attn_norm"], 1)
                dve.wait_ge(sem["attn_norm"], count("attn_norm", b, 1))
                statistics(b, "attn_norm", 1, yA, statA, mvA, LN_EPS)

            def attn_norm(b):
                dve.wait_ge(sem["attn_power"], count("attn_power", b, 1))
                dve.wait_ge(sem["xbet_done"], count("xbet_done", b - 1, 1))
                dve.wait_ge(sem["x1T_psum"], count("x1T_psum", b - 1, 1))
                normalize(x1, yA, mvA, rsA, "x1_done")

            def x1_low(b):
                dve.wait_ge(sem["x1T_high"], count("x1T_high", b, 2))
                dve.wait_ge(sem["hid0_psum"], count("hid0_psum", b - 1, EXPERTS))
                dve.tensor_tensor(x1L[:], PA[:, 0:T], x1H[:].bitcast(F32), ALU.subtract).then_inc(sem["x1T_low"], 1)

            def pick_two(b, psum_name, bankt, bias, lg, top, ix, ixf, name):
                dve.wait_ge(sem[psum_name], count(psum_name, b, 1))
                if bias is None:
                    dve.tensor_copy(both(lg[:]), bankt[:, 0:TT * EXPERTS]).then_inc(sem[name], 1)
                else:
                    dve.tensor_tensor(lg[:], bankt[:, 0:TT * EXPERTS].rearrange("p (a e) -> p a e", a=TT),
                                      bias[:, None, :].broadcast_to([P, TT, EXPERTS]), ALU.add).then_inc(sem[name], 1)
                dve.wait_ge(sem[name], count(name, b, 1))
                dve.sem_inc(sem["held"], 1)
                for tt in range(TT):
                    dve.max(top[:, tt], lg[:, tt]).then_inc(sem[name], 1)
                dve.wait_ge(sem[name], count(name, b, 3))
                dve.sem_inc(sem["held"], 1)
                for tt in range(TT):
                    dve.max_index(ix[:, tt], top[:, tt], lg[:, tt]).then_inc(sem[name], 1)

            def router0_pick(b):
                pick_two(b, "gate0_psum", PA, G0b, lg0, top0, ix0, ixf0, "pick0")
                dve.wait_ge(sem["gate0_exp"], count("gate0_exp", b - 1, 1))
                dve.tensor_tensor(dl0[:], top0[:], top0[:, :, 0:1].broadcast_to([P, TT, EXPERTS]),
                                  ALU.subtract).then_inc(sem["pick0"], 1)
                dve.wait_ge(sem["pick0"], count("pick0", b, 5))
                dve.tensor_copy(both(ixf0[:]), both(ix0[:])).then_inc(sem["pick0"], 1)
                dve.wait_ge(sem["pick0"], count("pick0", b, 7))
                dve.wait_ge(sem["route_psum"], count("route_psum", b - 1, 1))
                for r in range(2):
                    for tt in range(TT):
                        dve.tensor_scalar(route[:, tt, r, 0:EXPERTS], iota, ixf0[:, tt, r:r + 1], None,
                                          ALU.is_equal).then_inc(sem["pick0"], 1)
                dve.wait_ge(sem["pick0"], count("pick0", b, 11))
                chosen = route[:, :, :, 0:EXPERTS]
                dve.tensor_scalar(route[:, :, :, EXPERTS:2 * EXPERTS], chosen, -1.0, None, ALU.add).then_inc(sem["pick0"], 1)
                dve.tensor_copy(route[:, :, :, INFO - EXPERTS:INFO], chosen).then_inc(sem["pick0"], 1)

            def router0_values(b):
                dve.wait_ge(sem["gate0_exp"], count("gate0_exp", b, 1))
                dve.tensor_reduce(s0[:], e0[:], AX_X, ALU.add).then_inc(sem["value0"], 1)
                dve.wait_ge(sem["value0"], count("value0", b, 1))
                dve.reciprocal(r0[:], s0[:]).then_inc(sem["value0"], 1)
                dve.wait_ge(sem["value0"], count("value0", b, 2))
                dve.tensor_tensor(val0[:], e0[:, :, 0:2], r0[:][:, :, None].broadcast_to([P, TT, 2]),
                                  ALU.mult).then_inc(sem["value0"], 1)

            def relu_low(b, n):
                dve.wait_ge(sem["hid0_high"], count("hid0_high", b, n + 1))
                if n >= HRING:
                    dve.wait_ge(sem["out0_psum"], count("out0_psum", b, n - HRING + 1))
                else:
                    dve.wait_ge(sem["out1_psum"], count("out1_psum", b - 2, EXPERTS - HRING + n + 1))
                dve.scalar_tensor_tensor(out=hL[:, n % HRING], in0=Z[n % 2][:], scalar=0.0,
                                         in1=hH[:, n % HRING].bitcast(F32), op0=ALU.max,
                                         op1=ALU.subtract).then_inc(sem["hid0_low"], 1)

            def boost(b):
                dve.wait_ge(sem["out0_psum"], count("out0_psum", b, EXPERTS))
                dve.wait_ge(sem["hid0_psum"], count("hid0_psum", b - 1, 2 * EXPERTS))
                for target in (x2H, x2f):
                    dve.scalar_tensor_tensor(out=target[:], in0=MI[:, 0:T], scalar=0.5, in1=x1f[:], op0=ALU.mult,
                                             op1=ALU.add).then_inc(sem["boosted"], 1)
                dve.wait_ge(sem["boosted"], count("boosted", b, 2))
                dve.tensor_tensor(x2L[:], x2f[:], x2H[:].bitcast(F32), ALU.subtract).then_inc(sem["boosted"], 1)

            def moe0_stats(b):
                dve.wait_ge(sem["out0T_psum"], count("out0T_psum", b, 1))
                dve.wait_ge(sem["value0"], count("value0", b, 3))
                for tt in range(TT):
                    dve.scalar_tensor_tensor(out=f0[:, tt], in0=MI[:, tt * D:(tt + 1) * D],
                                             scalar=val0[:, tt, 0:1], in1=x1[:, tt], op0=ALU.mult,
                                             op1=ALU.add).then_inc(sem["moe0_norm"], 1)
                dve.wait_ge(sem["moe0_norm"], count("moe0_norm", b, 2))
                for tt in range(TT):
                    dve.scalar_tensor_tensor(out=f1[:, tt], in0=MI[:, (TT + tt) * D:(TT + tt + 1) * D],
                                             scalar=val0[:, tt, 1:2], in1=f0[:, tt], op0=ALU.mult,
                                             op1=ALU.add).then_inc(sem["moe0_norm"], 1)
                dve.wait_ge(sem["moe0_norm"], count("moe0_norm", b, 4))
                statistics(b, "moe0_norm", 4, f1, statB[:, 0], mvB[:, 0], LN_EPS)

            def moe0_norm_stats(b):
                dve.wait_ge(sem["moe0_norm"], count("moe0_norm", b, 13))
                statistics(b, "moe0_norm", 13, yB, statB[:, 1], mvB[:, 1], LN_EPS)

            def moe0_end(b):
                dve.wait_ge(sem["moe0_power"], count("moe0_power", b, 2))
                dve.wait_ge(sem["xob_done"], count("xob_done", b - 1, 1))
                dve.wait_ge(sem["x2T_psum"], count("x2T_psum", b - 1, 1))
                normalize(x2, yB, mvB[:, 1], rsB[:, 1], "x2_done")

            def lin_features(b):
                dve.wait_ge(sem["q1_psum"], count("q1_psum", b, 1))
                dve.wait_ge(sem["q1_exp"], count("q1_exp", b - 1, 1))
                dve.tensor_scalar(uq, SB[0][:, T:2 * T], Bq1, 0.0, ALU.add, ALU.min).then_inc(sem["q1_min"], 1)
                for tt in range(TT):
                    dve.wait_ge(sem["kvg_psum"], count("kvg_psum", b, tt + 1))
                    if tt == 0:
                        dve.wait_ge(sem["kv_psum"], count("kv_psum", b - 1, 1))
                        dve.wait_ge(sem["kg_exp"], count("kg_exp", b - 1, 2))
                    dve.tensor_tensor(KVG[:, tt, 0:3 * D], (SB[1], PA)[tt][:, 0:3 * D], Bkvg, ALU.add).then_inc(sem["kvg_done"], 1)
                dve.wait_ge(sem["kvg_done"], count("kvg_done", b, TT))
                dve.tensor_scalar(uk[:], KVG[:, :, D:2 * D], 0.0, None, ALU.min).then_inc(sem["k1_min"], 1)

            def lin_keys(b):
                dve.wait_ge(sem["q1_exp"], count("q1_exp", b, 2))
                dve.wait_ge(sem["lin_psum"], count("lin_psum", b - 1, 1))
                dve.tensor_tensor(qf[:], pq[:], eq[:], ALU.add).then_inc(sem["q1_done"], 1)
                dve.wait_ge(sem["kg_exp"], count("kg_exp", b, 1))
                dve.scalar_tensor_tensor(out=kf[:], in0=KVG[:, :, D:2 * D], scalar=0.0, in1=ek[:],
                                         op0=ALU.max, op1=ALU.add).then_inc(sem["k1_done"], 1)

            def lin_blocks(b):
                dve.wait_ge(sem["kv_psum"], count("kv_psum", b, 1))
                dve.wait_ge(sem["lin_psum"], count("lin_psum", b - 1, 1))
                dve.tensor_tensor(BD[:, 0:D], PA[:, 0:D], bmask, ALU.mult).then_inc(sem["kv_blocks"], 1)
                dve.tensor_scalar(BD[:, D:D + HEADS], bmask[:, ::DH], PA[:, D:D + 1], None,
                                  ALU.mult).then_inc(sem["kv_blocks"], 1)

            def lin_gate(b):
                read = PA[:].rearrange("p (a c) -> p a c", a=TT)
                dve.wait_ge(sem["lin_psum"], count("lin_psum", b, 1))
                dve.tensor_scalar(den1[:], read[:, :, D:D + HEADS], 1e-6, 2.0, ALU.add, ALU.mult).then_inc(sem["lin_gated"], 1)
                dve.wait_ge(sem["kg_exp"], count("kg_exp", b, 2))
                dve.wait_ge(sem["linT_psum"], count("linT_psum", b - 1, 1))
                dve.scalar_tensor_tensor(out=gnum[:], in0=tg[:], scalar=1.0, in1=read[:, :, 0:D],
                                         op0=ALU.add, op1=ALU.mult).then_inc(sem["lin_gated"], 1)
                dve.wait_ge(sem["lin_gated"], count("lin_gated", b, 1))
                dve.reciprocal(den1[:], den1[:]).then_inc(sem["lin_gated"], 1)
                dve.wait_ge(sem["lin_gated"], count("lin_gated", b, 3))
                for tt in range(TT):
                    dve.tensor_tensor(go[:, tt].rearrange("p (h d) -> p h d", h=HEADS),
                                      gnum[:, tt].rearrange("p (h d) -> p h d", h=HEADS),
                                      den1[:, tt][:, :, None].broadcast_to([P, HEADS, DH]),
                                      ALU.mult).then_inc(sem["lin_gated"], 1)

            def lin_norm(b):
                dve.wait_ge(sem["linout_psum"], count("linout_psum", b, 1))
                dve.wait_ge(sem["xob_done"], count("xob_done", b, 1))
                dve.tensor_tensor(both(yC[:]), SA[0][:, T:2 * T], both(xob[:]), ALU.add).then_inc(sem["lin_norm"], 1)
                dve.wait_ge(sem["lin_norm"], count("lin_norm", b, 1))
                statistics(b, "lin_norm", 1, yC, statC, mvC, LN_EPS)

            def lin_norm_end(b):
                dve.wait_ge(sem["lin_power"], count("lin_power", b, 1))
                dve.wait_ge(sem["x3T_psum"], count("x3T_psum", b - 1, 1))
                normalize(x3, yC, mvC, rsC, "x3_done")

            def router1_low(b):
                dve.wait_ge(sem["x3T_high"], count("x3T_high", b, 2))
                dve.wait_ge(sem["hid1_psum"], count("hid1_psum", b - 1, EXPERTS))
                dve.tensor_tensor(x3L[:], SA[1][:, 0:T], x3H[:].bitcast(F32), ALU.subtract).then_inc(sem["x3T_low"], 1)

            def router1_pick(b):
                pick_two(b, "gate1_psum", SA[1], None, lg1, top1, ix1, ixf1, "pick1")
                dve.tensor_tensor(dl1[:], top1[:, :, 1:2], top1[:, :, 0:1], ALU.subtract).then_inc(sem["pick1"], 1)
                dve.wait_ge(sem["pick1"], count("pick1", b, 5))
                dve.tensor_copy(both(ixf1[:]), both(ix1[:])).then_inc(sem["pick1"], 1)

            def router1_weights(b):
                dve.wait_ge(sem["pick1_exp"], count("pick1_exp", b, 1))
                dve.tensor_scalar(s1[:], e1[:], 1.0, None, ALU.add).then_inc(sem["weight1"], 1)
                dve.wait_ge(sem["weight1"], count("weight1", b, 1))
                dve.reciprocal(w1[:, :, 0:1], s1[:]).then_inc(sem["weight1"], 1)
                dve.wait_ge(sem["weight1"], count("weight1", b, 2))
                dve.tensor_tensor(w1[:, :, 1:2], e1[:], w1[:, :, 0:1], ALU.mult).then_inc(sem["weight1"], 1)
                dve.wait_ge(sem["weight1"], count("weight1", b, 3))
                dve.wait_ge(sem["pick1"], count("pick1", b, 7))
                for r in range(2):
                    for tt in range(TT):
                        dve.tensor_scalar(ohw[:, r, tt], iota, ixf1[:, tt, r:r + 1], w1[:, tt, r:r + 1],
                                          ALU.is_equal, ALU.mult).then_inc(sem["weight1"], 1)
                dve.wait_ge(sem["weight1"], count("weight1", b, 7))
                dve.wait_ge(sem["weightsT_psum"], count("weightsT_psum", b - 1, 1))
                dve.tensor_tensor(wE[:], ohw[:, 0], ohw[:, 1], ALU.add).then_inc(sem["weights_done"], 1)

            def gelu_low(b, e):
                dve.wait_ge(sem["hid1_high"], count("hid1_high", b, e + 1))
                dve.tensor_tensor(hL[:, e % HRING], gf[:, e % GRING], hH[:, e % HRING].bitcast(F32),
                                  ALU.subtract).then_inc(sem["hid1_low"], 1)

            def expert_sums(b, k):
                dve.wait_ge(sem["out1T_psum"], count("out1T_psum", b, k + 1))
                if only(b, 0):
                    dve.wait_ge(sem["raw_split"], 4)
                for tt in range(TT):
                    dve.tensor_tensor(V[:, tt, 2 * k:2 * k + 2],
                                      SB[k % 2][:, tt * T:(tt + 1) * T].rearrange("p (e d) -> p e d", e=2),
                                      x3[:, tt][:, None, :].broadcast_to([P, 2, D]),
                                      ALU.add).then_inc(sem["expert_sum"], 1)

            def expert_stats(b, k):
                dve.wait_ge(sem["expert_sum"], count("expert_sum", b, 2 * (k // 2 + 1)))
                for tt in range(TT):
                    dve.bn_stats(statD[:, tt * EXPERTS + k], V[:, tt, k]).then_inc(sem["expert_norm"], 1)

            def expert_scales(b):
                dve.wait_ge(sem["expert_norm"], count("expert_norm", b, 16))
                me, mo, ve, vo = (statD[:, :, k] for k in (1, 4, 2, 5))
                dve.tensor_tensor(smD[:], me, mo, ALU.add).then_inc(sem["expert_norm"], 1)
                dve.tensor_tensor(dfD[:], me, mo, ALU.subtract).then_inc(sem["expert_norm"], 1)
                dve.scalar_tensor_tensor(out=qdD[:], in0=ve, scalar=D * LN_EPS_EXPERT, in1=vo, op0=ALU.add,
                                         op1=ALU.add).then_inc(sem["expert_norm"], 1)
                dve.wait_ge(sem["expert_norm"], count("expert_norm", b, 19))
                dve.scalar_tensor_tensor(out=ddD[:], in0=dfD[:], scalar=0.25, in1=dfD[:], op0=ALU.mult,
                                         op1=ALU.mult).then_inc(sem["expert_norm"], 1)
                dve.wait_ge(sem["expert_norm"], count("expert_norm", b, 20))
                dve.scalar_tensor_tensor(out=vrD[:], in0=qdD[:], scalar=1.0 / D, in1=ddD[:], op0=ALU.mult,
                                         op1=ALU.add).then_inc(sem["expert_norm"], 1)

            def expert_scales_end(b):
                dve.wait_ge(sem["expert_power"], count("expert_power", b, 1))
                dve.wait_ge(sem["weights_done"], count("weights_done", b, 1))
                dve.tensor_tensor(aD[:], rsD[:], both(wE[:]), ALU.mult).then_inc(sem["expert_norm"], 1)
                dve.wait_ge(sem["expert_norm"], count("expert_norm", b, 22))
                dve.scalar_tensor_tensor(out=cD[:], in0=smD[:], scalar=-0.5, in1=aD[:], op0=ALU.mult,
                                         op1=ALU.mult).then_inc(sem["expert_norm"], 1)

            def own_tile(b):
                for e in range(EXPERTS):
                    dve.tensor_scalar(V[:, 0, e], V[:, 0, e], aD[:, e:e + 1], cD[:, e:e + 1], ALU.mult,
                                      ALU.add).then_inc(sem["own_scaled"], 1)
                dve.wait_ge(sem["own_scaled"], EXPERTS)
                dve.tensor_tensor(V[:, 0], V[:, 0], Lng, ALU.mult).then_inc(sem["own_gamma"], 1)

            def expert_totals(b):
                for tt in range(TT):
                    if only(b, SEQS - 1) and tt == 0:
                        dve.wait_ge(sem["own_gamma"], 1)
                    else:
                        dve.wait_ge(sem["expert_gamma"], count("expert_gamma", b, tt + 1 - only(b, SEQS - 1)))
                    dve.tensor_reduce(rdD[:, tt], V[:, tt].rearrange("p e d -> p d e"), AX_X, ALU.add).then_inc(sem["expert_total"], 1)

            def last_stats(b):
                dve.wait_ge(sem["beta_psum"], count("beta_psum", b, 1))
                dve.tensor_tensor(both(zD[:]), MI[:, T:2 * T], both(x3[:]), ALU.add).then_inc(sem["last_norm"], 1)

            def last_stats_end(b):
                dve.wait_ge(sem["last_norm"], count("last_norm", b, 1))
                dve.wait_ge(sem["expert_total"], count("expert_total", b, TT))
                dve.tensor_tensor(both(yD[:]), both(zD[:]), both(rdD[:]), ALU.add).then_inc(sem["last_norm"], 1)
                dve.wait_ge(sem["last_norm"], count("last_norm", b, 2))
                statistics(b, "last_norm", 2, yD, statE, mvE, LN_EPS)

            def last_norm(b):
                dve.wait_ge(sem["last_power"], count("last_power", b, 1))
                normalize(res, yD, mvE, rsE, "res_done")

            def turn(t):
                z, l, m, a, n = t - 2, t - 1, t, t + 1, t + 2
                for e in range(EXPERTS):
                    heads = slot_heads(e)
                    if has(a):
                        maximum(a, heads[0])
                    if has(m) and not by_pool(e):
                        relu_low(m, e)
                    if has(a) and len(heads) == 2:
                        maximum(a, heads[1])
                    if has(m) and e == 1:
                        router0_values(m)
                    if has(l):
                        if e == 3:
                            lin_features(l)
                        if e == 5:
                            lin_keys(l)
                        if e == 7:
                            lin_blocks(l)
                    if has(z):
                        if e == 0:
                            expert_stats(z, 6)
                            expert_stats(z, 7)
                        if e == 1:
                            expert_scales(z)
                        if e == 3:
                            expert_scales_end(z)
                            if only(t, SEQS + 1):
                                dve.wait_ge(sem["expert_norm"], count("expert_norm", z, 23))
                                own_tile(z)
                    if has(a) and e == 6:
                        if only(t, -1):
                            dve.wait_ge(sem["filled"], 6)
                        negmax(a, 0)
                if has(m):
                    boost(m)
                if has(a):
                    shift(a, 0)
                if only(t, -1):
                    qk_low(n)
                for e in range(EXPERTS):
                    if has(a) and e < 4:
                        maximum(a, 12 + e)
                        if e == 3:
                            negmax(a, 1)
                    if has(m):
                        relu_low(m, EXPERTS + e)
                    if has(a) and e == 3:
                        shift(a, 1)
                    if has(l):
                        if e == 1:
                            lin_gate(l)
                        if e == 3:
                            lin_norm(l)
                        if e == 4:
                            lin_norm_end(l)
                        if e == 7:
                            router1_low(l)
                    if has(z) and not only(t, SEQS):
                        if e == 5:
                            expert_totals(z)
                            last_stats_end(z)
                        if e == 6:
                            last_norm(z)
                if has(l):
                    router1_pick(l)
                if has(a):
                    attn_divide(a)
                if has(m):
                    moe0_stats(m)
                if has(l):
                    gelu_low(l, 0)
                if only(t, SEQS):
                    expert_totals(z)
                    last_stats_end(z)
                    last_norm(z)
                if has(a):
                    attn_stats(a)
                if has(l):
                    gelu_low(l, 2)
                if has(a):
                    attn_norm(a)
                if has(l):
                    router1_weights(l)
                if has(a):
                    x1_low(a)
                if has(n) and has(m):
                    qk_low(n)
                if has(m):
                    moe0_norm_stats(m)
                if has(a):
                    router0_pick(a)
                if has(m):
                    moe0_end(m)
                if has(l):
                    expert_sums(l, 0)
                    expert_stats(l, 0)
                    expert_stats(l, 1)
                if has(n):
                    values(n)
                if has(l):
                    gelu_low(l, 6)
                    expert_sums(l, 1)
                    gelu_low(l, 7)
                    expert_stats(l, 2)
                    expert_stats(l, 3)
                    expert_sums(l, 2)
                    expert_sums(l, 3)
                    last_stats(l)
                    expert_stats(l, 4)
                    expert_stats(l, 5)
                if has(z):
                    dve.wait_ge(sem["stored"], count("stored", z, 16))

            dve.wait_ge(sem["near_consts"], 32)
            dve.wait_ge(sem["filled"], 2)
            qk_low(0)
            values(0)
            dve.wait_ge(sem["consts"], 16 * 2)
            dve.wait_ge(sem["info_high"], 1)
            dve.scalar_tensor_tensor(out=infoW[:], in0=infoW[:].bitcast(F32), scalar=lowr, in1=infoRaw,
                                     op0=ALU.mult, op1=ALU.add).then_inc(sem["info_split"], 1)
            for t in range(-1, 2):
                turn(t)
            with dve.Fori(2, SEQS - 2) as t:
                turn(t)
            for t in range(SEQS - 2, SEQS + 2):
                turn(t)


def kernel(**inputs):
    import numpy as np
    import concourse.bacc as bacc
    from concourse.bass_utils import run_bass_kernel_spmd

    a = {k: np.asarray(v) for k, v in inputs.items()}
    x = a["L0_attn_x"]

    order = np.arange(D).reshape(G, QD, DH).transpose(1, 2, 0).reshape(-1)
    wqkv, bqkv = a["L0_attn_W_qkv"], a["L0_attn_b_qkv"]

    def side_by_side(names, blocks):
        packed = np.zeros((P, sum(n for _, n in names)), np.float32)
        at = 0
        for name, n in names:
            packed[:blocks[name].shape[0], at:at + n] = blocks[name]
            at += n
        return packed

    lowrows = np.zeros((INFO, 1), np.float32)
    lowrows[17] = -1.0
    lowrows[24:] = -1.0
    heads = np.arange(D) // DH
    blocks = {
        "wqk": np.concatenate([wqkv[0:D].T[:, order], wqkv[D:2 * D].T[:, order]], 1),
        "bqk": np.stack([bqkv[0:D][order], bqkv[D:2 * D][order]], 1),
        "wv": wqkv[2 * D:].T, "ident": np.eye(P, dtype=np.float32),
        "wo": a["L0_attn_W_out"].T, "g0w": a["L0_ffn_gate_W"],
        "iota": np.tile(np.arange(EXPERTS, dtype=np.float32), (P, 1)),
        "blockmask": (heads[:, None] == heads[None, :]).astype(np.float32),
        "wq1": a["L1_attn_wq_w"], "bq1": a["L1_attn_wq_b"][:, None],
        "wkvg": np.concatenate([a["L1_attn_wg_w"], a["L1_attn_wk_w"], a["L1_attn_wv_w"]], 1),
        "wout": a["L1_attn_out_w"], "g1w": a["L1_ffn_gate_w"],
        "b1b": a["L1_ffn_b1"].reshape(EXPERTS, HH, P).transpose(2, 0, 1).reshape(P, -1),
        "b2t": a["L1_ffn_b2"].T, "lowrows": lowrows,
    }
    rows = {
        "bv": bqkv[2 * D:], "bo": a["L0_attn_b_out"], "g0b": a["L0_ffn_gate_b"],
        "gam0": a["L0_ffn_ln_gamma"], "bet0": a["L0_ffn_ln_beta"],
        "bkvg": np.concatenate([a["L1_attn_wg_b"], a["L1_attn_wk_b"], a["L1_attn_wv_b"]]),
        "bout": a["L1_attn_out_b"], "lng": a["L1_ffn_ln_g"].reshape(-1),
    }
    info = np.zeros((INFO, NINF), np.float32)
    info[0:EXPERTS, EXPERTS * HID:] = a["L0_ffn_b2"]
    info[INFO - EXPERTS:, EXPERTS * HID:] = a["L0_ffn_b2"]
    for e in range(EXPERTS):
        info[EXPERTS + e, e * HID:(e + 1) * HID] = BIG
    info[16, 0:EXPERTS * HID] = a["L0_ffn_b1"].reshape(-1)
    info[17, 0:EXPERTS * HID] = a["L0_ffn_b1"].reshape(-1)

    def by_input(w):
        return w.transpose(1, 0, 2).reshape(D, -1)

    def by_hidden(w):
        return w.reshape(EXPERTS, HH, P, D).transpose(2, 0, 1, 3).reshape(P, -1)

    sent = {
        "xT": x.transpose(0, 2, 1), "xtok": x.reshape(SEQS, TT, P, D).transpose(0, 2, 1, 3),
        "pack_a": side_by_side(PACK_A, blocks), "pack_b": side_by_side(PACK_B, blocks),
        "row_a": np.concatenate([rows[n] for n, _ in ROW_A]),
        "row_b": np.concatenate([rows[n] for n, _ in ROW_B]),
        "lnb": a["L1_ffn_ln_b"], "info": info,
        "w1a": by_input(a["L0_ffn_W1"]), "w2a": by_hidden(a["L0_ffn_W2"]),
        "w1b": by_input(a["L1_ffn_w1"]), "w2b": by_hidden(a["L1_ffn_w2"]),
    }
    nc = bacc.Bacc("TRN2", target_bir_lowering=False, num_devices=1)
    arrays, args = {}, []
    for name, value in sent.items():
        value = np.ascontiguousarray(value)
        arrays[f"in_{name}"] = value
        args.append(nc.dram_tensor(f"in_{name}", value.shape, mybir.dt.from_np(value.dtype),
                                   kind="ExternalInput").ap())
    args.append(nc.dram_tensor("out_0", (SEQS, P, TT, D), F32, kind="ExternalOutput").ap())
    build(nc, *args)
    r = run_bass_kernel_spmd(nc, [arrays], core_ids=[0])
    got = r.results[0]["out_0"]
    return got.transpose(0, 2, 1, 3).reshape(SEQS, T, D)
```
